# Optimizing a Trainium2 kernel written in Bass

```python
import numpy as np
import jax
import jax.numpy as jnp

def _softmax(x, axis=-1):
    return jax.nn.softmax(x, axis=axis)

def _gelu(x):
    return jax.nn.gelu(x, approximate=True)

def _silu(x):
    return jax.nn.silu(x)

def _sigmoid(x):
    return jax.nn.sigmoid(x)

def _layernorm(x, axis=-1, eps=1e-05):
    m = jnp.mean(x, axis=axis, keepdims=True)
    v = jnp.var(x, axis=axis, keepdims=True)
    return (x - m) / jnp.sqrt(v + eps)

def _scatter_add(tgt, idx, src, axis=0):
    return tgt.at[idx].add(src)

def _segment_sum(src, seg, n):
    return jax.ops.segment_sum(src, seg, n)
kernel_name = 'mk_lm_tower_d2_tok_ids256_r4_d4ac97'

def setup_inputs(seed: int=0):
    np.random.seed(seed)
    _w = jnp.asarray

    def _rec_inputs():
        import jax
        import jax.numpy as jnp
        _rk = jax.random.key(seed)
        x = jax.random.randint(jax.random.fold_in(_rk, 1), (8, 512), 0, 128, jnp.int32)
        return x
    x = _rec_inputs()

    def _L0_tok_setup():
        import jax, jax.numpy as jnp
        import numpy as np
        VOCAB = 128
        D = 64
        S = 128
        B = 128
        MAX_LEN = 128
        SEP_ID = 13
        PAD_ID = 1

        def _make_pe():
            pos = np.arange(MAX_LEN, dtype=np.float32)[:, None]
            div = np.exp(np.arange(0, D, 2, dtype=np.float32) * (-np.log(10000.0) / D))
            pe = np.zeros((MAX_LEN, D), dtype=np.float32)
            pe[:, 0::2] = np.sin(pos * div)
            pe[:, 1::2] = np.cos(pos * div)
            return jnp.asarray(pe)
        key = jax.random.key(seed)
        k1, k2 = jax.random.split(key)
        sequence = jax.random.randint(k1, (S, B), 0, VOCAB)
        token_W = jax.random.normal(k2, (VOCAB, D), dtype=jnp.float32) * 0.02
        token_W = token_W.at[0].set(0.0)
        pe = _make_pe()
        return {'sequence': sequence, 'token_W': token_W, 'pe': pe}
    _L0_tok_all = _L0_tok_setup()
    _L0_tok_in = {k: v for k, v in _L0_tok_all.items() if k in ('token_W', 'pe')}
    del _L0_tok_all

    def _L0_attn_setup():
        import jax, jax.numpy as jnp
        import numpy as np
        key = jax.random.key(seed)
        k1, k2, k3 = jax.random.split(key, 3)
        d = 64
        x = jax.random.normal(k1, (8, 512, d), dtype=jnp.float32)
        Wq = jax.random.normal(k2, (d, d), dtype=jnp.float32) * d ** (-0.5)
        Wk = jax.random.normal(k3, (d, d), dtype=jnp.float32) * d ** (-0.5)
        return {'x': x, 'Wq': Wq, 'Wk': Wk}
    _L0_attn_all = _L0_attn_setup()
    _L0_attn_in = {k: v for k, v in _L0_attn_all.items() if k in ('Wq', 'Wk')}
    del _L0_attn_all

    def _L0_ffn_setup():
        import jax, jax.numpy as jnp
        import numpy as np
        B, N, D = (16, 1024, 64)
        NUM_EXPERTS, TOP_K, HEADS = (4, 2, 4)
        N_EDGES = 262144
        LN_EPS = 1e-05

        def _layernorm(x, g, b):
            mu = x.mean(-1, keepdims=True)
            var = ((x - mu) ** 2).mean(-1, keepdims=True)
            return (x - mu) * jax.lax.rsqrt(var + LN_EPS) * g + b

        def _forward(x, edge_index, W_gat, att_src, att_dst, b_gat, ln_gamma, ln_beta, W1, b1, W2, b2):
            Bc, Nc, Dc = x.shape
            M = Bc * Nc
            x_flat = x.reshape(M, Dc)
            h = (x_flat @ W_gat).reshape(M, HEADS, NUM_EXPERTS)
            loops = jnp.arange(M, dtype=edge_index.dtype)
            src = jnp.concatenate([edge_index[0], loops])
            dst = jnp.concatenate([edge_index[1], loops])
            a_src = (h * att_src).sum(-1)
            a_dst = (h * att_dst).sum(-1)
            e = jax.nn.leaky_relu(a_src[src] + a_dst[dst], negative_slope=0.2)
            e_max = jax.ops.segment_max(e, dst, num_segments=M)
            ee = jnp.exp(e - e_max[dst])
            denom = jax.ops.segment_sum(ee, dst, num_segments=M)
            alpha = ee / (denom[dst] + 1e-16)
            msg = h[src] * alpha[:, :, None]
            agg = jax.ops.segment_sum(msg, dst, num_segments=M).reshape(M, HEADS * NUM_EXPERTS) + b_gat
            scores = _layernorm(agg, ln_gamma, ln_beta).reshape(M, HEADS, NUM_EXPERTS).mean(1)
            scores = scores.reshape(Bc, Nc, NUM_EXPERTS)
            topk_s, topk_i = jax.lax.top_k(scores, TOP_K)
            w = jax.nn.softmax(topk_s, axis=-1)
            out = jnp.zeros_like(x)
            for ei in range(NUM_EXPERTS):
                g = jnp.where(topk_i == ei, w, 0.0).sum(-1)
                hh = jax.nn.gelu(x @ W1[ei] + b1[ei], approximate=False)
                out = out + g[..., None] * (hh @ W2[ei] + b2[ei])
            return out
        key = jax.random.key(seed)
        ks = jax.random.split(key, 8)
        s = 0.05
        return {'x': jax.random.normal(ks[0], (B, N, D), jnp.float32), 'W_gat': jax.random.normal(ks[1], (D, HEADS * NUM_EXPERTS), jnp.float32) * s, 'att_src': jax.random.normal(ks[2], (HEADS, NUM_EXPERTS), jnp.float32) * s, 'att_dst': jax.random.normal(ks[3], (HEADS, NUM_EXPERTS), jnp.float32) * s, 'b_gat': jnp.zeros((HEADS * NUM_EXPERTS,), jnp.float32), 'ln_gamma': jnp.ones((HEADS * NUM_EXPERTS,), jnp.float32), 'ln_beta': jnp.zeros((HEADS * NUM_EXPERTS,), jnp.float32), 'W1': jax.random.normal(ks[4], (NUM_EXPERTS, D, 2 * D), jnp.float32) * s, 'b1': jnp.zeros((NUM_EXPERTS, 2 * D), jnp.float32), 'W2': jax.random.normal(ks[5], (NUM_EXPERTS, 2 * D, D), jnp.float32) * s, 'b2': jnp.zeros((NUM_EXPERTS, D), jnp.float32), 'edge_index': jax.random.randint(ks[6], (2, N_EDGES), 0, B * N, jnp.int32)}
    _L0_ffn_all = _L0_ffn_setup()
    _L0_ffn_in = {k: v for k, v in _L0_ffn_all.items() if k in ('W_gat', 'att_src', 'att_dst', 'b_gat', 'ln_gamma', 'ln_beta', 'W1', 'b1', 'W2', 'b2', 'edge_index')}
    del _L0_ffn_all

    def _L1_attn_setup():
        import jax, jax.numpy as jnp
        import numpy as np
        N_HASHES = 4
        N_BUCKETS = 8
        NUM_HEADS = 8
        LN_EPS = 1e-05

        def layer_norm(x, g, b):
            m = jnp.mean(x, axis=-1, keepdims=True)
            v = jnp.mean(jnp.square(x - m), axis=-1, keepdims=True)
            return (x - m) * jax.lax.rsqrt(v + LN_EPS) * g + b
        key = jax.random.key(seed)
        ks = jax.random.split(key, 8)
        B, N, C = (16, 2048, 64)
        dff = 4 * C
        w = 0.05
        return {'x': jax.random.normal(ks[0], (B, N, C), jnp.float32), 'rotations': jax.random.normal(ks[1], (1, C, N_HASHES, N_BUCKETS // 2), jnp.float32), 'norm1_g': jnp.ones((C,), jnp.float32), 'norm1_b': jnp.zeros((C,), jnp.float32), 'q_w': jax.random.normal(ks[2], (C, C), jnp.float32) * w, 'kv_w': jax.random.normal(ks[3], (C, 2 * C), jnp.float32) * w, 'norm2_g': jnp.ones((C,), jnp.float32), 'norm2_b': jnp.zeros((C,), jnp.float32), 'fc1_w': jax.random.normal(ks[4], (C, dff), jnp.float32) * w, 'fc1_b': jnp.zeros((dff,), jnp.float32), 'fc2_w': jax.random.normal(ks[5], (dff, C), jnp.float32) * w, 'fc2_b': jnp.zeros((C,), jnp.float32)}
    _L1_attn_all = _L1_attn_setup()
    _L1_attn_in = {k: v for k, v in _L1_attn_all.items() if k in ('rotations', 'norm1_g', 'norm1_b', 'q_w', 'kv_w', 'norm2_g', 'norm2_b', 'fc1_w', 'fc1_b', 'fc2_w', 'fc2_b')}
    del _L1_attn_all

    def _L1_ffn_setup():
        import jax, jax.numpy as jnp
        import numpy as np
        TOP_K = 2
        key = jax.random.key(seed)
        ks = jax.random.split(key, 4)
        B, L, D, H, E = (8, 1024, 64, 256, 8)
        s = 0.02
        return {'x': jax.random.normal(ks[0], (B, L, D), jnp.float32), 'Wg': jax.random.normal(ks[1], (D, E), jnp.float32) * s, 'bg': jnp.zeros((E,), jnp.float32), 'W1': jax.random.normal(ks[2], (E, D, H), jnp.float32) * s, 'b1': jnp.zeros((E, H), jnp.float32), 'W2': jax.random.normal(ks[3], (E, H, D), jnp.float32) * s, 'b2': jnp.zeros((E, D), jnp.float32)}
    _L1_ffn_all = _L1_ffn_setup()
    _L1_ffn_in = {k: v for k, v in _L1_ffn_all.items() if k in ('Wg', 'bg', 'W1', 'b1', 'W2', 'b2')}
    del _L1_ffn_all
    return {'x': x, 'L0_tok_token_W': _L0_tok_in['token_W'], 'L0_tok_pe': _L0_tok_in['pe'], 'L0_attn_Wq': _L0_attn_in['Wq'], 'L0_attn_Wk': _L0_attn_in['Wk'], 'L0_ffn_W_gat': _L0_ffn_in['W_gat'], 'L0_ffn_att_src': _L0_ffn_in['att_src'], 'L0_ffn_att_dst': _L0_ffn_in['att_dst'], 'L0_ffn_b_gat': _L0_ffn_in['b_gat'], 'L0_ffn_ln_gamma': _L0_ffn_in['ln_gamma'], 'L0_ffn_ln_beta': _L0_ffn_in['ln_beta'], 'L0_ffn_W1': _L0_ffn_in['W1'], 'L0_ffn_b1': _L0_ffn_in['b1'], 'L0_ffn_W2': _L0_ffn_in['W2'], 'L0_ffn_b2': _L0_ffn_in['b2'], 'L0_ffn_edge_index': _L0_ffn_in['edge_index'], 'L1_attn_rotations': _L1_attn_in['rotations'], 'L1_attn_norm1_g': _L1_attn_in['norm1_g'], 'L1_attn_norm1_b': _L1_attn_in['norm1_b'], 'L1_attn_q_w': _L1_attn_in['q_w'], 'L1_attn_kv_w': _L1_attn_in['kv_w'], 'L1_attn_norm2_g': _L1_attn_in['norm2_g'], 'L1_attn_norm2_b': _L1_attn_in['norm2_b'], 'L1_attn_fc1_w': _L1_attn_in['fc1_w'], 'L1_attn_fc1_b': _L1_attn_in['fc1_b'], 'L1_attn_fc2_w': _L1_attn_in['fc2_w'], 'L1_attn_fc2_b': _L1_attn_in['fc2_b'], 'L1_ffn_Wg': _L1_ffn_in['Wg'], 'L1_ffn_bg': _L1_ffn_in['bg'], 'L1_ffn_W1': _L1_ffn_in['W1'], 'L1_ffn_b1': _L1_ffn_in['b1'], 'L1_ffn_W2': _L1_ffn_in['W2'], 'L1_ffn_b2': _L1_ffn_in['b2']}

def reference(x, L0_tok_token_W, L0_tok_pe, L0_attn_Wq, L0_attn_Wk, L0_ffn_W_gat, L0_ffn_att_src, L0_ffn_att_dst, L0_ffn_b_gat, L0_ffn_ln_gamma, L0_ffn_ln_beta, L0_ffn_W1, L0_ffn_b1, L0_ffn_W2, L0_ffn_b2, L0_ffn_edge_index, L1_attn_rotations, L1_attn_norm1_g, L1_attn_norm1_b, L1_attn_q_w, L1_attn_kv_w, L1_attn_norm2_g, L1_attn_norm2_b, L1_attn_fc1_w, L1_attn_fc1_b, L1_attn_fc2_w, L1_attn_fc2_b, L1_ffn_Wg, L1_ffn_bg, L1_ffn_W1, L1_ffn_b1, L1_ffn_W2, L1_ffn_b2):
    import jax
    import jax.numpy as jnp

    def _L0_tok_ref(sequence, token_W, pe):
        import jax, jax.numpy as jnp
        import numpy as np
        VOCAB = 128
        D = 64
        S = 128
        B = 128
        MAX_LEN = 128
        SEP_ID = 13
        PAD_ID = 1

        def _make_pe():
            pos = np.arange(MAX_LEN, dtype=np.float32)[:, None]
            div = np.exp(np.arange(0, D, 2, dtype=np.float32) * (-np.log(10000.0) / D))
            pe = np.zeros((MAX_LEN, D), dtype=np.float32)
            pe[:, 0::2] = np.sin(pos * div)
            pe[:, 1::2] = np.cos(pos * div)
            return jnp.asarray(pe)
        tok_emb = token_W[sequence] * (sequence != 0)[..., None].astype(token_W.dtype)
        S_, B_ = sequence.shape

        def step(carry, xs):
            prev_sep, pad_num = carry
            tok, j = xs
            is_sep = tok == SEP_ID
            skip = prev_sep & (tok == PAD_ID) & ~is_sep
            pos_emb = pe[j - pad_num]
            emb = jnp.where(skip[:, None], jnp.zeros((), pe.dtype), pos_emb)
            new_carry = (is_sep | skip, pad_num + skip.astype(pad_num.dtype))
            return (new_carry, emb)
        init = (jnp.zeros((B_,), dtype=bool), jnp.zeros((B_,), dtype=jnp.int32))
        _, pos_emb = jax.lax.scan(step, init, (sequence, jnp.arange(S_, dtype=jnp.int32)))
        return tok_emb + pos_emb

    def _L0_attn_ref(x, Wq, Wk):
        import jax, jax.numpy as jnp
        import numpy as np
        d = x.shape[-1]
        scale = d ** (-0.5)
        q = jnp.einsum('bnd,ed->bne', x, Wq)
        k = jnp.einsum('bnd,ed->bne', x, Wk)
        sim = jnp.einsum('bid,bjd->bij', q, k) * scale
        attn = jax.nn.softmax(sim, axis=-1)
        out = jnp.einsum('bij,bjd->bid', attn, x)
        return out

    def _L0_ffn_ref(x, W_gat, att_src, att_dst, b_gat, ln_gamma, ln_beta, W1, b1, W2, b2, edge_index):
        import jax, jax.numpy as jnp
        import numpy as np
        B, N, D = (16, 1024, 64)
        NUM_EXPERTS, TOP_K, HEADS = (4, 2, 4)
        N_EDGES = 262144
        LN_EPS = 1e-05

        def _layernorm(x, g, b):
            mu = x.mean(-1, keepdims=True)
            var = ((x - mu) ** 2).mean(-1, keepdims=True)
            return (x - mu) * jax.lax.rsqrt(var + LN_EPS) * g + b

        def _forward(x, edge_index, W_gat, att_src, att_dst, b_gat, ln_gamma, ln_beta, W1, b1, W2, b2):
            Bc, Nc, Dc = x.shape
            M = Bc * Nc
            x_flat = x.reshape(M, Dc)
            h = (x_flat @ W_gat).reshape(M, HEADS, NUM_EXPERTS)
            loops = jnp.arange(M, dtype=edge_index.dtype)
            src = jnp.concatenate([edge_index[0], loops])
            dst = jnp.concatenate([edge_index[1], loops])
            a_src = (h * att_src).sum(-1)
            a_dst = (h * att_dst).sum(-1)
            e = jax.nn.leaky_relu(a_src[src] + a_dst[dst], negative_slope=0.2)
            e_max = jax.ops.segment_max(e, dst, num_segments=M)
            ee = jnp.exp(e - e_max[dst])
            denom = jax.ops.segment_sum(ee, dst, num_segments=M)
            alpha = ee / (denom[dst] + 1e-16)
            msg = h[src] * alpha[:, :, None]
            agg = jax.ops.segment_sum(msg, dst, num_segments=M).reshape(M, HEADS * NUM_EXPERTS) + b_gat
            scores = _layernorm(agg, ln_gamma, ln_beta).reshape(M, HEADS, NUM_EXPERTS).mean(1)
            scores = scores.reshape(Bc, Nc, NUM_EXPERTS)
            topk_s, topk_i = jax.lax.top_k(scores, TOP_K)
            w = jax.nn.softmax(topk_s, axis=-1)
            out = jnp.zeros_like(x)
            for ei in range(NUM_EXPERTS):
                g = jnp.where(topk_i == ei, w, 0.0).sum(-1)
                hh = jax.nn.gelu(x @ W1[ei] + b1[ei], approximate=False)
                out = out + g[..., None] * (hh @ W2[ei] + b2[ei])
            return out
        return _forward(x, edge_index, W_gat, att_src, att_dst, b_gat, ln_gamma, ln_beta, W1, b1, W2, b2)

    def _L1_attn_ref(x, rotations, norm1_g, norm1_b, q_w, kv_w, norm2_g, norm2_b, fc1_w, fc1_b, fc2_w, fc2_b):
        import jax, jax.numpy as jnp
        import numpy as np
        N_HASHES = 4
        N_BUCKETS = 8
        NUM_HEADS = 8
        LN_EPS = 1e-05

        def layer_norm(x, g, b):
            m = jnp.mean(x, axis=-1, keepdims=True)
            v = jnp.mean(jnp.square(x - m), axis=-1, keepdims=True)
            return (x - m) * jax.lax.rsqrt(v + LN_EPS) * g + b
        B, N, C = x.shape
        H = NUM_HEADS
        Dh = C // H
        scale = Dh ** (-0.5)
        x_ = layer_norm(x, norm1_g, norm1_b)
        q = (x_ @ q_w).reshape(B, N, H, Dh).transpose(0, 2, 1, 3)
        rotated = jnp.einsum('btf,fhi->bhti', x_, rotations[0])
        rotated = jnp.concatenate([rotated, -rotated], axis=-1)
        buckets = jnp.argmax(rotated, axis=-1)
        one_hot = jax.nn.one_hot(buckets, N_BUCKETS, dtype=x.dtype)
        sum_buckets = jnp.sum(one_hot, axis=2)
        pooled = jnp.einsum('bnf,bhni->bhif', x_, one_hot)
        pooled = pooled / (jax.lax.stop_gradient(sum_buckets)[..., None] + 1e-20)
        rp_x = pooled.reshape(B, N_HASHES * N_BUCKETS, C)
        sumb = jax.lax.stop_gradient(sum_buckets.reshape(B, N_HASHES * N_BUCKETS))
        M = N_HASHES * N_BUCKETS
        kv = (rp_x @ kv_w).reshape(B, M, 2, H, Dh).transpose(2, 0, 3, 1, 4)
        k, v = (kv[0], kv[1])
        attn = jnp.einsum('bhnd,bhmd->bhnm', q, k) * scale
        mask = (sumb >= 1)[:, None, None, :]
        attn = jnp.where(mask, attn, -jnp.finfo(attn.dtype).max)
        attn = jax.nn.softmax(attn, axis=-1)
        out = jnp.einsum('bhnm,bhmd->bnhd', attn, v).reshape(B, N, C)
        x = x + out
        y = layer_norm(x, norm2_g, norm2_b)
        h = jax.nn.gelu(y @ fc1_w + fc1_b, approximate=False)
        y = h @ fc2_w + fc2_b
        return x + y

    def _L1_ffn_ref(x, Wg, bg, W1, b1, W2, b2):
        import jax, jax.numpy as jnp
        import numpy as np
        TOP_K = 2
        B, L, D = x.shape
        E = W1.shape[0]
        xf = x.reshape(-1, D)
        gate_logits = xf @ Wg + bg
        top_w, top_i = jax.lax.top_k(gate_logits, TOP_K)
        top_w = jax.nn.softmax(top_w, axis=-1)
        w_dense = jnp.sum(jax.nn.one_hot(top_i, E, dtype=xf.dtype) * top_w[..., None], axis=1)
        out = jnp.zeros_like(xf)
        for e in range(E):
            h = jax.nn.gelu(xf @ W1[e] + b1[e], approximate=False)
            out = out + w_dense[:, e:e + 1] * (h @ W2[e] + b2[e])
        return out.reshape(B, L, D)
    h = _L0_tok_ref(x, L0_tok_token_W, L0_tok_pe)
    h = h + _L0_attn_ref(_layernorm(h, axis=-1), L0_attn_Wq, L0_attn_Wk)
    h = h + _L0_ffn_ref(_layernorm(h, axis=-1), L0_ffn_W_gat, L0_ffn_att_src, L0_ffn_att_dst, L0_ffn_b_gat, L0_ffn_ln_gamma, L0_ffn_ln_beta, L0_ffn_W1, L0_ffn_b1, L0_ffn_W2, L0_ffn_b2, L0_ffn_edge_index)
    h = h + _L1_attn_ref(_layernorm(h, axis=-1), L1_attn_rotations, L1_attn_norm1_g, L1_attn_norm1_b, L1_attn_q_w, L1_attn_kv_w, L1_attn_norm2_g, L1_attn_norm2_b, L1_attn_fc1_w, L1_attn_fc1_b, L1_attn_fc2_w, L1_attn_fc2_b)
    h = h + _L1_ffn_ref(_layernorm(h, axis=-1), L1_ffn_Wg, L1_ffn_bg, L1_ffn_W1, L1_ffn_b1, L1_ffn_W2, L1_ffn_b2)
    return h

_drawn_inputs = setup_inputs


def setup_inputs(seed=0):
    import zlib

    import numpy as np

    out = dict(_drawn_inputs(seed))
    spreads = {'L0_ffn_b_gat': (0.0, 0.443),
     'L0_ffn_ln_gamma': (1.0, 0.2),
     'L0_ffn_ln_beta': (0.0, 0.524),
     'L0_ffn_b1': (0.0, 0.632),
     'L0_ffn_b2': (0.0, 0.1),
     'L1_attn_norm1_g': (1.0, 0.2),
     'L1_attn_norm1_b': (0.0, 0.492),
     'L1_attn_norm2_g': (1.0, 0.6),
     'L1_attn_norm2_b': (0.0, 0.8),
     'L1_attn_fc1_b': (0.0, 0.417),
     'L1_attn_fc2_b': (0.0, 0.1),
     'L1_ffn_bg': (0.0, 0.1),
     'L1_ffn_b1': (0.0, 0.8),
     'L1_ffn_b2': (0.0, 0.284)}
    factors = {'L0_tok_token_W': 2.687,
     'L0_attn_Wq': 8.0,
     'L0_attn_Wk': 8.0,
     'L0_ffn_att_src': 8.0,
     'L0_ffn_att_dst': 8.0,
     'L1_attn_rotations': 8.0,
     'L1_attn_q_w': 8.0,
     'L1_ffn_W1': 7.332,
     'L1_ffn_W2': 6.35}
    for name, (base, spread) in spreads.items():
        noise = np.random.default_rng([zlib.crc32(name.encode()), seed]).standard_normal(out[name].shape)
        drawn = base * np.exp(spread * noise) if base else spread * noise
        out[name] = jnp.asarray(drawn.astype(out[name].dtype))
    for name, factor in factors.items():
        out[name] = (out[name] * factor).astype(out[name].dtype)
    return out
```

```python
from contextlib import ExitStack

import numpy as np

import concourse.bass as bass
from concourse import mybir

F32 = mybir.dt.float32
I32 = mybir.dt.int32
ALU = mybir.AluOpType
ACT = mybir.ActivationFunctionType
AX = mybir.AxisListType.X
RMAX = bass.bass_isa.ReduceOp.max

P = 128
LN_EPS = 1e-05
SEP_ID, PAD_ID = 13, 1
NEG = -1.0e30
MARGIN = 60.0


def tower_program(nc, seq, tok_w, pe_w, wq, wk, w_gat, att_src, att_dst, b_gat, ln_g, ln_b,
                  m0_w1, m0_b1, m0_w2, m0_b2, edges, rot, n1_g, n1_b, q_w, kv_w, n2_g, n2_b,
                  fc1_w, fc1_b, fc2_w, fc2_b, wg, bg, m1_w1, m1_b1, m1_w2, m1_b2, out):
    S, B = seq.shape
    V, D = tok_w.shape
    N = S * B
    T = N // P
    TB = B // P
    E0, H0 = m0_w1.shape[0], m0_w1.shape[2]
    E1, H1 = m1_w1.shape[0], m1_w1.shape[2]
    HF = fc1_w.shape[1]
    GH, GE = att_src.shape
    GC = GH * GE
    SC = GH + GC
    NEDGE = edges.shape[1]
    EC = NEDGE // P
    NH, NBK = rot.shape[2], 2 * rot.shape[3]
    M = NH * NBK
    AH = 8
    DH = D // AH
    G = 8
    CH = B
    assert V == P and N % P == 0 and NEDGE % (2 * G * P) == 0 and D == 64 and N == 4096

    with ExitStack() as ctx:
        def sb(name, shape, dt=F32):
            return ctx.enter_context(nc.sbuf_tensor(name, shape, dt))

        sems = {}

        def sem(name):
            if name not in sems:
                sems[name] = ctx.enter_context(nc.semaphore(name))
            return sems[name]

        ident = sb("ident", [P, P])
        iota_free = sb("iota_free", [P, P])
        iota_part = sb("iota_part", [P, 1])
        ones = sb("ones", [P, P])
        zeros = sb("zeros", [P, 512])
        later = sb("later", [P, E1, E1])
        bucket_rank = sb("bucket_rank", [P, NBK])
        head_mask = sb("head_mask", [D, AH])
        row_mask = sb("row_mask", [P, 2, AH, DH])
        w_tok = sb("w_tok", [V, D])
        w_pe = sb("w_pe", [S, D])
        w_q, w_k = sb("w_q", [D, D]), sb("w_k", [D, D])
        w_g = sb("w_g", [D, 2 * D])
        w_gat_s = sb("w_gat_s", [D, GC])
        att_s, att_d = sb("att_s", [P, GC]), sb("att_d", [P, GC])
        bgat_s, lng_s, lnb_s = sb("bgat_s", [P, GC]), sb("lng_s", [P, GC]), sb("lnb_s", [P, GC])
        w_rot = sb("w_rot", [D, NH * NBK // 2])
        norm_s = sb("norm_s", [P, 4, D])
        w_qq, w_kv = sb("w_qq", [D, 2 * D]), sb("w_kv", [D, 2 * D])
        w_gate, b_gate = sb("w_gate", [D, E1]), sb("b_gate", [1, E1])
        w1_0, b1_0 = sb("w1_0", [D, E0, H0]), sb("b1_0", [P, E0])
        w2_0, b2_0 = sb("w2_0", [P, E0, D]), sb("b2_0", [1, E0, D])
        w1_f, b1_f = sb("w1_f", [D, HF]), sb("b1_f", [P, HF // P])
        w2_f, b2_f = sb("w2_f", [P, HF // P, D]), sb("b2_f", [1, D])
        w1_1, b1_1 = sb("w1_1", [D, E1, H1]), sb("b1_1", [P, E1 * H1 // P])
        w2_1, b2_1 = sb("w2_1", [P, E1 * H1 // P, D]), sb("b2_1", [1, E1, D])
        h = sb("h", [P, T, D])
        xn = sb("xn", [P, T, D])
        x5 = sb("x5", [P, T, D])
        xT = sb("xT", [D, N])
        tmp = sb("tmp", [P, T, D])
        stat = sb("stat", [P, 8, T])
        gate = sb("gate", [P, T, E1])
        pairs = sb("pairs", [P, T, E1, E1])
        pairs2 = sb("pairs2", [P, T, E1, E1])
        small = sb("small", [P, 8, T * GH])
        hg = sb("hg", [P, T, GC])
        src_rows = sb("src_rows", [P, T, SC])
        dst_rows = sb("dst_rows", [P, T, 2 * GH])
        pad_row = sb("pad_row", [1, 2 * GH])
        arena = sb("arena", [P, 3 * EC])
        key_a, key_b = arena[:, 0:EC], arena[:, EC:2 * EC]
        src_f = arena[:, 2 * EC:3 * EC]
        e_idx = sb("e_idx", [P, 2, EC], I32)
        seq_bc = e_idx[:, :, :].rearrange("p a b -> p (a b)")
        onehot_tok = arena[:, 0:N]
        tokc = sb("tokc", [P, T], I32)
        n_valid = sb("n_valid", [P, 2])
        pool_pad = sb("pool_pad", [P, 2])
        n_cols = sb("n_cols", [P, 1], I32)
        idx_st = sb("idx_st", [P, 2, 2, G], I32)
        src_g = sb("src_g", [P, 2, G, SC])
        dst_g = sb("dst_g", [P, 2, G, 2 * GH])
        z_e = sb("z_e", [P, 2, 2, G, GH])
        msg = sb("msg", [P, 2, G, SC])
        dst_part = sb("dst_part", [P, 2, 2, G], I32)
        dst_partf = sb("dst_partf", [P, 2, 2, G])
        hot_hi = sb("hot_hi", [P, 2, G, T])
        hot_lo = sb("hot_lo", [P, 2, G, P])
        spread = sb("spread", [P, 2, G, T, SC])
        big = spread[:, :, :, :, :].rearrange("p a g t c -> p (a g t c)")
        yst = sb("yst", [D, 2, P])
        prob = big[:, 0:1024].rearrange("p (a n) -> p a n", a=2)
        probT = big[:, 1024:2048].rearrange("p (a n) -> p a n", a=2)
        hid = big[:, 2048:3072].rearrange("p (a n) -> p a n", a=2)
        mx = sb("mx", [P, 2, 4])
        mout = sb("mout", [P, 2, TB * D])
        hot_b = big[:, 4096:4096 + T * M].rearrange("p (t h i) -> p t h i", t=T, h=NH)
        rotv = big[:, 5120:5120 + T * M].rearrange("p (t h i) -> p t h i", t=T, h=NH)
        hmax = big[:, 6144:6144 + T * NH].rearrange("p (t h) -> p t h", t=T)
        pooled = big[0:D, 6272:6272 + S * P].rearrange("p (s r m) -> p s r m", s=S, m=M)
        counts = big[:, 7296:7296 + S * M]
        kT = big[0:D, 7552:7552 + S * M]
        k_bd = big[0:D, 7808:7808 + S * AH * M].rearrange("p (s h m) -> p s h m", s=S, h=AH)
        v_bd = arena[:, 0:S * 2 * D].rearrange("p (s g c) -> p s g c", s=S, g=2)
        score = arena[:, 1024:1536].rearrange("p (a n) -> p a n", a=2)
        scoreT = arena[:, 1536:2048].rearrange("p (a n) -> p a n", a=2)
        head_st = sb("head_st", [P, 2, 3, AH])

        tab_src = nc.dram_tensor("tab_src", [N, SC], F32, kind="Internal").ap()
        tab_dst = nc.dram_tensor("tab_dst", [N + 1, 2 * GH], F32, kind="Internal").ap()

        bank = [ctx.enter_context(nc.psum_tensor(f"bank{i}", [P, 512], F32)) for i in range(8)]

        block = ctx.enter_context(nc.Block())

        def tiles(ap):
            return ap.rearrange("p (t c) -> p t c", c=D)

        @block.sync
        def _(sp):
            def load(dst, src, name, columns=False):
                sp.dma_start(dst, src, allow_slow_non_contiguous=columns).then_inc(sem(name), 16)

            load(seq_bc, seq.rearrange("s b -> (s b)").rearrange("(a n) -> a n", a=1).broadcast_to([P, N]), "tokens_in")
            load(tokc[:, :], seq.rearrange("s (q p) -> p (s q)", p=P), "tokens_in", True)
            load(w_tok[:, :], tok_w, "tokens_in")
            load(w_pe[:, :], pe_w[0:S, :], "tokens_in")
            load(w_q[:, :], wq, "attn_w_in")
            load(w_k[:, :], wk, "attn_w_in")
            load(w_gat_s[:, :], w_gat, "gat_w_in")
            for dst, src in ((att_s, att_src.rearrange("h e -> (h e)")), (att_d, att_dst.rearrange("h e -> (h e)")),
                             (bgat_s, b_gat), (lng_s, ln_g), (lnb_s, ln_b)):
                load(dst[:, :], src.rearrange("(a n) -> a n", a=1).broadcast_to([P, GC]), "gat_w_in")
            load(w1_0[:, :, :], m0_w1.rearrange("e d h -> d e h"), "moe0_w_in")
            load(b1_0[:, :], m0_b1.rearrange("e h -> h e"), "moe0_w_in", True)
            load(w2_0[:, :, :], m0_w2.rearrange("e h d -> h e d"), "moe0_w_in")
            load(b2_0[:, :, :], m0_b2.rearrange("(a e) d -> a e d", a=1), "moe0_w_in")
            load(w_rot[:, :], rot.rearrange("a d h i -> (a d) (h i)"), "lsh_w_in")
            for i, src in enumerate((n1_g, n1_b, n2_g, n2_b)):
                load(norm_s[:, i, :], src.rearrange("(a n) -> a n", a=1).broadcast_to([P, D]), "lsh_w_in")
            load(w_qq[:, 0:D], q_w, "lsh_w_in")
            load(w_qq[:, D:2 * D], q_w, "lsh_w_in")
            load(w_kv[:, :], kv_w, "lsh_w_in")
            load(w1_f[:, :], fc1_w, "fc_w_in")
            load(b1_f[:, :], fc1_b.rearrange("(k p) -> p k", p=P), "fc_w_in", True)
            load(w2_f[:, :, :], fc2_w.rearrange("(k p) d -> p k d", p=P), "fc_w_in")
            load(b2_f[:, :], fc2_b.rearrange("(a n) -> a n", a=1), "fc_w_in")
            load(w_gate[:, :], wg, "moe1_w_in")
            load(b_gate[:, :], bg.rearrange("(a n) -> a n", a=1), "moe1_w_in")
            load(w1_1[:, :, :], m1_w1.rearrange("e d h -> d e h"), "moe1_w_in")
            load(b1_1[:, :], m1_b1.rearrange("e (k p) -> p (e k)", p=P), "moe1_w_in", True)
            load(w2_1[:, :, :], m1_w2.rearrange("e (k p) d -> p (e k) d", p=P), "moe1_w_in")
            load(b2_1[:, :, :], m1_b2.rearrange("(a e) d -> a e d", a=1), "moe1_w_in")
            sp.wait_ge(sem("onehot_tok_made"), 1)
            load(e_idx[:, :, :], edges.rearrange("a (p c) -> p a c", p=P), "edges_in")
            sp.wait_ge(sem("node_rows_made"), 1)
            sp.dma_start(tab_src.rearrange("(t p) c -> p t c", p=P), src_rows[:, :, :]).then_inc(sem("tables_out"), 16)
            sp.dma_start(tab_dst[0:N, :].rearrange("(t p) c -> p t c", p=P), dst_rows[:, :, :])\
              .then_inc(sem("tables_out"), 16)
            sp.dma_start(tab_dst[N:N + 1, :], pad_row[:, :]).then_inc(sem("tables_out"), 16)
            sp.wait_ge(sem("h_final"), 1)
            sp.dma_start(out.rearrange("s (q p) d -> p (s q) d", p=P), h[:, :, :]).then_inc(sem("out_written"), 16)
            sp.wait_ge(sem("out_written"), 16)

        LOADS = {"tokens_in": 4, "attn_w_in": 2, "gat_w_in": 6, "moe0_w_in": 4, "lsh_w_in": 8,
                 "fc_w_in": 4, "moe1_w_in": 6, "edges_in": 1}

        def loaded(eng, name):
            eng.wait_ge(sem(name), 16 * LOADS[name])

        @block.gpsimd
        def _(pool):
            made = sem("pool_consts")
            pool.memset(ident[:, :], 0.0).then_inc(made, 1)
            pool.memset(ones[:, :], 1.0).then_inc(made, 1)
            pool.memset(zeros[:, :], 0.0).then_inc(made, 1)
            pool.memset(later[:, :, :], 1.0).then_inc(made, 1)
            pool.memset(head_mask[:, :], 1.0).then_inc(made, 1)
            pool.memset(row_mask[:, :, :, :], 1.0).then_inc(made, 1)
            pool.memset(pad_row[:, :], 0.0).then_inc(made, 1)
            pool.iota(iota_free[:, :], [[1, P]], base=0, channel_multiplier=0,
                      allow_small_or_imprecise_dtypes=True).then_inc(made, 1)
            pool.iota(iota_part[:, :], [[0, 1]], base=0, channel_multiplier=1,
                      allow_small_or_imprecise_dtypes=True).then_inc(made, 1)
            pool.iota(bucket_rank[:, :], [[-1, NBK]], base=NBK, channel_multiplier=0,
                      allow_small_or_imprecise_dtypes=True).then_inc(made, 1)
            pool.wait_ge(made, 10)
            pool.affine_select(out=ident[:, :], in_=ident[:, :], compare_op=ALU.not_equal, fill=1.0,
                               base=0, pattern=[[-1, P]], channel_multiplier=1).then_inc(made, 1)
            pool.affine_select(out=later[:, :, :], in_=later[:, :, :], compare_op=ALU.is_gt, fill=0.0,
                               base=0, pattern=[[1, E1], [-1, E1]], channel_multiplier=0).then_inc(made, 1)
            pool.affine_select(out=head_mask[:, :], in_=head_mask[:, :], compare_op=ALU.is_ge, fill=0.0,
                               base=0, pattern=[[-DH, AH]], channel_multiplier=1).then_inc(made, 1)
            pool.affine_select(out=row_mask[:, :, :, :], in_=row_mask[:, :, :, :], compare_op=ALU.is_ge,
                               fill=0.0, base=0, pattern=[[P, 2], [-M, AH], [0, DH]],
                               channel_multiplier=1).then_inc(made, 1)
            pool.wait_ge(made, 14)
            pool.affine_select(out=head_mask[:, :], in_=head_mask[:, :], compare_op=ALU.is_gt, fill=0.0,
                               base=DH, pattern=[[DH, AH]], channel_multiplier=-1).then_inc(made, 1)
            pool.affine_select(out=row_mask[:, :, :, :], in_=row_mask[:, :, :, :], compare_op=ALU.is_gt,
                               fill=0.0, base=M, pattern=[[-P, 2], [M, AH], [0, DH]],
                               channel_multiplier=-1).then_inc(made, 1)
            pool.wait_ge(made, 16)
            pool.memset(pool_pad[:, :], 0.0).then_inc(made, 1)
            pool.wait_ge(made, 17)
            pool.memset(n_valid[:, 1:2], 0.0).then_inc(sem("consts_made"), 1)

            pool.wait_ge(sem("rows_counted"), 1)
            pool.partition_all_reduce(n_valid[:, 1:2], n_valid[:, 0:1], P, RMAX).then_inc(sem("count_reduced"), 1)
            pool.wait_ge(sem("a_src_max_part"), 1)
            pool.partition_all_reduce(small[:, 4, 0:GH], small[:, 3, 0:GH], P, RMAX)\
                .then_inc(sem("a_src_max_all"), 1)

            pool.wait_ge(sem("tables_out"), 48)
            pool.wait_ge(sem("cols_known"), 1)
            n = pool.value_load(n_cols[0:1, 0:1], min_val=0, max_val=EC)
            with pool.Fori(0, EC // (2 * G)) as i:
                with pool.If(i * (2 * G) < n):
                    for a in range(2):
                        pool.wait_ge(sem("gathered_used"), 2 * i + a + 1)
                        pool.tensor_copy(idx_st[:, a, :, :], e_idx[:, :, bass.ds(i * (2 * G) + a * G, G)])\
                            .then_inc(sem("indices_staged"), 1)
                        pool.wait_ge(sem("indices_staged"), 2 * i + a + 1)
                        pool.tensor_tensor(pool_pad[:, 0:1], pool_pad[:, 1:2], pool_pad[:, 1:2], ALU.add)
                        for j in range(G):
                            pool.indirect_dma_start(
                                out=src_g[:, a, j, :], out_offset=None, in_=tab_src,
                                in_offset=bass.IndirectOffsetOnAxis(ap=idx_st[:, a, 0, j:j + 1], axis=0))\
                                .then_inc(sem(f"gathered{a}"), 16)
                            pool.indirect_dma_start(
                                out=dst_g[:, a, j, :], out_offset=None, in_=tab_dst,
                                in_offset=bass.IndirectOffsetOnAxis(ap=idx_st[:, a, 1, j:j + 1], axis=0))\
                                .then_inc(sem(f"gathered{a}"), 16)
                with pool.Else():
                    pool.nop()

        @block.vector
        def _(dve):
            step = sem("dve_steps")
            count = [0]

            def seq_(ins):
                count[0] += 1
                ins.then_inc(step, 1)
                dve.wait_ge(step, count[0])

            def bc(ap, n):
                return ap.unsqueeze(2).broadcast_to([ap.shape[0], ap.shape[1], n])

            def rep(ap, n):
                return ap.unsqueeze(1).broadcast_to([ap.shape[0], n, ap.shape[1]])

            lns = [0]

            def layer_norm(dst, src, gb=None, width=D):
                lns[0] += 1
                t = src.shape[1]
                cen = tmp[:, 0:t, 0:width]
                seq_(dve.tensor_reduce(stat[:, 0, :], src, AX, ALU.add))
                seq_(dve.tensor_scalar(stat[:, 1, :], stat[:, 0, :], -1.0 / width, None, ALU.mult))
                dve.tensor_tensor(cen, src, bc(stat[:, 1, :], width), ALU.add).then_inc(sem("ln_centred"), 1)
                dve.wait_ge(sem("ln_squared"), lns[0])
                seq_(dve.tensor_reduce(stat[:, 2, :], dst, AX, ALU.add))
                dve.tensor_scalar(stat[:, 3, :], stat[:, 2, :], 1.0 / width, LN_EPS, ALU.mult, ALU.add)\
                   .then_inc(sem("ln_var"), 1)
                dve.wait_ge(sem("ln_std"), lns[0])
                seq_(dve.reciprocal(stat[:, 5, :], stat[:, 4, :]))
                seq_(dve.tensor_tensor(dst, cen, bc(stat[:, 5, :], width), ALU.mult))
                if gb:
                    seq_(dve.tensor_tensor(dst, dst, rep(gb[0], t), ALU.mult))
                    seq_(dve.tensor_tensor(dst, dst, rep(gb[1], t), ALU.add))

            def top2(sc, E):
                a = sc.unsqueeze(3).broadcast_to([P, T, E, E])
                b = sc.unsqueeze(2).broadcast_to([P, T, E, E])
                gt, eq = pairs[:, :, 0:E, 0:E], pairs2[:, :, 0:E, 0:E]
                dve.tensor_tensor(gt, b, a, ALU.is_gt)
                seq_(dve.tensor_tensor(eq, b, a, ALU.is_equal))
                seq_(dve.tensor_tensor(eq, eq, later[:, 0:E, 0:E].unsqueeze(1).broadcast_to([P, T, E, E]), ALU.mult))
                seq_(dve.tensor_tensor(gt, gt, eq, ALU.add))
                rank, top = pairs2[:, :, 0, 0:E], stat[:, 0, :]
                seq_(dve.tensor_reduce(rank, gt, AX, ALU.add))
                seq_(dve.tensor_reduce(top, sc, AX, ALU.max))
                shifted = pairs2[:, :, 1, 0:E]
                dve.tensor_tensor(shifted, sc, bc(top, E), ALU.subtract).then_inc(sem("gate_shifted"), 1)
                gates[0] += 1
                dve.wait_ge(sem("gate_exp"), gates[0])
                ex = pairs[:, :, 0, 0:E]
                seq_(dve.tensor_scalar(rank, rank, 1.5, None, ALU.is_lt))
                seq_(dve.tensor_tensor(ex, ex, rank, ALU.mult))
                seq_(dve.tensor_reduce(stat[:, 1, :], ex, AX, ALU.add))
                seq_(dve.reciprocal(stat[:, 2, :], stat[:, 1, :]))
                seq_(dve.tensor_tensor(gate[:, :, 0:E], ex, bc(stat[:, 2, :], E), ALU.mult))

            gates = [0]

            dve.wait_ge(sem("consts_made"), 1)
            loaded(dve, "tokens_in")
            seq_(dve.tensor_copy(onehot_tok, seq_bc))
            dve.tensor_scalar(onehot_tok, onehot_tok, iota_part[:, 0:1], None, ALU.is_equal)\
               .then_inc(sem("onehot_tok_made"), 1)
            dve.tensor_scalar(w_tok[0:1, :], w_tok[0:1, :], 0.0, None, ALU.mult).then_inc(sem("w_tok_masked"), 1)
            tok, sep = small[:, 0, 0:T], small[:, 1, 0:T]
            pad, code = small[:, 2, 0:T], small[:, 3, 0:T]
            prev, npad = small[:, 4, 0:TB], small[:, 5, 0:TB]
            skip = small[:, 6, 0:TB]
            seq_(dve.tensor_copy(tok, tokc[:, :]))
            dve.tensor_scalar(sep, tok, float(SEP_ID), None, ALU.is_equal)
            dve.tensor_scalar(pad, tok, float(PAD_ID), None, ALU.is_equal)
            dve.memset(prev, 0.0)
            seq_(dve.memset(npad, 0.0))
            for s in range(S):
                q = slice(s * TB, (s + 1) * TB)
                seq_(dve.tensor_tensor(skip, prev, pad[:, q], ALU.mult))
                dve.scalar_tensor_tensor(out=code[:, q], in0=skip, scalar=100.0, in1=npad,
                                         op0=ALU.mult, op1=ALU.subtract)
                seq_(dve.tensor_tensor(prev, sep[:, q], skip, ALU.max))
                seq_(dve.tensor_tensor(npad, npad, skip, ALU.add))
                seq_(dve.tensor_scalar(code[:, q], code[:, q], float(s), None, ALU.add))
            onehot_pos = hg[:, :, 0:S]
            dve.tensor_tensor(onehot_pos, bc(code, S), rep(iota_free[:, 0:S], T), ALU.is_equal)\
               .then_inc(sem("onehot_pos_made"), 1)

            for b in range(4):
                dve.wait_ge(sem("embedded"), b + 1)
                ins = dve.tensor_copy(h[:, 8 * b:8 * b + 8, :], tiles(bank[b][:, :]))
                seq_(ins)
            layer_norm(xn[:, :, :], h[:, :, :])
            dve.memset(stat[:, 7, 2:3], 0.0).then_inc(sem("xn_ready"), 1)
            with dve.Fori(0, S) as b:
                for q in range(TB):
                    a = q % 2
                    it = TB * b + q
                    dve.wait_ge(sem("scores_ready"), it + 1)
                    dve.tensor_reduce(mx[:, a, 0:1], bank[a][:, :], AX, ALU.max).then_inc(sem("att_step"), 1)
                    dve.wait_ge(sem("att_step"), 2 * it + 1)
                    dve.tensor_scalar(mx[:, a, 1:2], mx[:, a, 0:1], -float(D) ** -0.5, None, ALU.mult)\
                       .then_inc(sem("max_ready"), 1)
                    dve.wait_ge(sem("prob_ready"), it + 1)
                    dve.reciprocal(mx[:, a, 3:4], mx[:, a, 2:3]).then_inc(sem("att_step"), 1)
                    dve.wait_ge(sem("probT_psum"), it + 1)
                    dve.tensor_copy(probT[:, a, :], bank[2 + a][:, :]).then_inc(sem("probT_ready"), 1)
                    dve.wait_ge(sem("att_step"), 2 * it + 2)
                    dve.wait_ge(sem("att_out"), it + 1)
                    dst = h[:, bass.ds(it, 1), :].rearrange("p t c -> p (t c)")
                    dve.scalar_tensor_tensor(out=dst, in0=bank[4 + a][:, 0:D], scalar=mx[:, a, 3:4], in1=dst,
                                             op0=ALU.mult, op1=ALU.add).then_inc(sem("att_added"), 1)
            dve.wait_ge(sem("att_added"), T)

            layer_norm(xn[:, :, :], h[:, :, :])
            dve.memset(stat[:, 7, 2:3], 0.0).then_inc(sem("xn_ready"), 1)

            loaded(dve, "edges_in")
            dve.tensor_scalar(src_f, e_idx[:, 0, :], float(N - 1), None, ALU.min)
            seq_(dve.tensor_scalar(key_b, e_idx[:, 1, :], float(N), float(N), ALU.min, ALU.mult))
            seq_(dve.tensor_tensor(key_a, key_b, src_f, ALU.add))
            seq_(dve.tensor_scalar(key_a, key_a, float(N * N), None, ALU.min))
            cur, nxt = key_a, key_b
            size = 2
            while size <= EC:
                m = size // 2
                while m >= 1:
                    if size < EC:
                        x = cur.rearrange("p (n r k u m) -> p n r k u m", r=2, u=2, m=m, k=size // (2 * m))
                        y = nxt.rearrange("p (n r k u m) -> p n r k u m", r=2, u=2, m=m, k=size // (2 * m))
                        dirs = [(x[:, :, r], y[:, :, r], r) for r in (0, 1)]
                    else:
                        dirs = [(cur.rearrange("p (n k u m) -> p n k u m", n=1, u=2, m=m),
                                 nxt.rearrange("p (n k u m) -> p n k u m", n=1, u=2, m=m), 0)]
                    for xx, yy, r in dirs:
                        lo, hi = xx[:, :, :, 0, :], xx[:, :, :, 1, :]
                        ops = (ALU.min, ALU.max) if r == 0 else (ALU.max, ALU.min)
                        dve.tensor_tensor(yy[:, :, :, 0, :], lo, hi, ops[0])
                        ins = dve.tensor_tensor(yy[:, :, :, 1, :], lo, hi, ops[1])
                    seq_(ins)
                    cur, nxt = nxt, cur
                    m //= 2
                size *= 2
            seq_(dve.tensor_scalar(nxt, cur, float(N * N), None, ALU.is_lt))
            dve.tensor_reduce(n_valid[:, 0:1], nxt, AX, ALU.add).then_inc(sem("rows_counted"), 1)
            dve.wait_ge(sem("rows_counted"), 1)
            seq_(dve.tensor_copy(e_idx[:, 0, :], cur))
            dve.tensor_scalar(e_idx[:, 1, :], e_idx[:, 0, :], 12, None, ALU.logical_shift_right)
            seq_(dve.tensor_scalar(e_idx[:, 0, :], e_idx[:, 0, :], N - 1, None, ALU.bitwise_and))
            dve.wait_ge(sem("count_reduced"), 1)
            dve.tensor_copy(n_cols[:, :], n_valid[:, 1:2]).then_inc(sem("cols_known"), 1)

            loaded(dve, "gat_w_in")
            dve.wait_ge(sem("gat_h"), 1)
            seq_(dve.tensor_copy(hg[:, :, :].rearrange("p t c -> p (t c)"), bank[2][:, :]))
            a_src, a_dst, upper, self_e = (small[:, i, :] for i in range(4))
            shift, ee_self = small[:, 5, :], small[:, 6, :]
            prod = pairs[:, :, 0:GH, 0:GE]
            hg4 = hg[:, :, :].rearrange("p t (h e) -> p t h e", h=GH)
            for att, dst in ((att_s, a_src), (att_d, a_dst)):
                w = att[:, :].rearrange("p (h e) -> p h e", h=GH).unsqueeze(1).broadcast_to([P, T, GH, GE])
                seq_(dve.tensor_tensor(prod, hg4, w, ALU.mult))
                seq_(dve.tensor_reduce(dst.rearrange("p (t h) -> p t h", t=T), prod, AX, ALU.add))
            dve.tensor_reduce(small[:, 3, 0:GH], a_src.rearrange("p (t h) -> p h t", t=T), AX, ALU.max)\
               .then_inc(sem("a_src_max_part"), 1)
            dve.wait_ge(sem("a_src_max_all"), 1)
            seq_(dve.tensor_tensor(upper.rearrange("p (t h) -> p t h", t=T), a_dst.rearrange("p (t h) -> p t h", t=T),
                                   rep(small[:, 4, 0:GH], T), ALU.add))
            seq_(dve.tensor_tensor(self_e, a_src, a_dst, ALU.add))
            for x in (upper, self_e):
                seq_(dve.scalar_tensor_tensor(out=x, in0=x, scalar=0.2, in1=x, op0=ALU.mult, op1=ALU.max))
            seq_(dve.scalar_tensor_tensor(out=shift, in0=self_e, scalar=MARGIN, in1=upper,
                                          op0=ALU.add, op1=ALU.min))
            dve.tensor_tensor(upper, self_e, shift, ALU.subtract).then_inc(sem("self_shifted"), 1)
            dve.tensor_copy(src_rows[:, :, 0:GH], a_src.rearrange("p (t h) -> p t h", t=T))
            dve.tensor_copy(src_rows[:, :, GH:SC], hg[:, :, :])
            dve.tensor_copy(dst_rows[:, :, 0:GH], a_dst.rearrange("p (t h) -> p t h", t=T))
            dve.tensor_copy(dst_rows[:, :, GH:2 * GH], shift.rearrange("p (t h) -> p t h", t=T))\
               .then_inc(sem("dst_rows_made"), 1)
            dve.wait_ge(sem("dst_rows_made"), 1)
            dve.memset(stat[:, 7, 0:1], 0.0).then_inc(sem("node_rows_made"), 1)
            dve.memset(stat[:, 7, 1:2], 0.0).then_inc(sem("gathered_used"), 2)

            dve.wait_ge(sem("cols_known"), 1)
            n = dve.value_load(n_cols[0:1, 0:1], min_val=0, max_val=EC)
            with dve.Fori(0, EC // (2 * G)) as i:
                with dve.If(i * (2 * G) < n):
                    for a in range(2):
                        g = 2 * i + a
                        cols = e_idx[:, 1, bass.ds(i * (2 * G) + a * G, G)]
                        dve.tensor_scalar(dst_part[:, a, 0, :], cols, P - 1, None, ALU.bitwise_and)\
                           .then_inc(sem("edge_step"), 1)
                        dve.tensor_scalar(dst_part[:, a, 1, :], cols, 7, None, ALU.logical_shift_right)\
                           .then_inc(sem("edge_step"), 1)
                        dve.wait_ge(sem("edge_step"), 7 * g + 2)
                        dve.tensor_copy(dst_partf[:, a, :, :], dst_part[:, a, :, :]).then_inc(sem("edge_step"), 1)
                        dve.wait_ge(sem("edge_step"), 7 * g + 3)
                        dve.wait_ge(sem("edge_bufs_free"), g + 1)
                        dve.tensor_tensor(hot_lo[:, a, :, :], bc(dst_partf[:, a, 0, :], P),
                                          rep(iota_free[:, :], G), ALU.is_equal)
                        dve.tensor_tensor(hot_hi[:, a, :, :], bc(dst_partf[:, a, 1, :], T),
                                          rep(iota_free[:, 0:T], G), ALU.is_equal).then_inc(sem("edge_step"), 1)
                        dve.wait_ge(sem(f"gathered{a}"), 32 * G * (i + 1))
                        dve.tensor_tensor(z_e[:, a, 0, :, :], src_g[:, a, :, 0:GH], dst_g[:, a, :, 0:GH],
                                          ALU.add).then_inc(sem("edge_step"), 1)
                        dve.wait_ge(sem("edge_step"), 7 * g + 5)
                        dve.scalar_tensor_tensor(out=z_e[:, a, 1, :, :], in0=z_e[:, a, 0, :, :], scalar=0.2,
                                                 in1=z_e[:, a, 0, :, :], op0=ALU.mult, op1=ALU.max)\
                           .then_inc(sem("edge_step"), 1)
                        dve.wait_ge(sem("edge_step"), 7 * g + 6)
                        dve.tensor_tensor(z_e[:, a, 0, :, :], z_e[:, a, 1, :, :], dst_g[:, a, :, GH:2 * GH],
                                          ALU.subtract).then_inc(sem("edge_scores"), 1)
                        dve.wait_ge(sem("edge_exp"), g + 1)
                        dve.tensor_tensor(
                            msg[:, a, :, GH:SC].rearrange("p g (h e) -> p g h e", h=GH),
                            src_g[:, a, :, GH:SC].rearrange("p g (h e) -> p g h e", h=GH),
                            msg[:, a, :, 0:GH].unsqueeze(3).broadcast_to([P, G, GH, GE]), ALU.mult)\
                           .then_inc(sem("edge_step"), 1)
                        dve.wait_ge(sem("edge_step"), 7 * g + 7)
                        dve.tensor_tensor(
                            spread[:, a, :, :, :],
                            hot_hi[:, a, :, :].unsqueeze(3).broadcast_to([P, G, T, SC]),
                            msg[:, a, :, :].unsqueeze(2).broadcast_to([P, G, T, SC]), ALU.mult)\
                           .then_inc(sem("edges_spread"), 1)
                        dve.wait_ge(sem("edges_spread"), g + 1)
                        dve.memset(stat[:, 7, 2:3], 0.0).then_inc(sem("gathered_used"), 1)
                with dve.Else():
                    dve.nop()

            den, agg = small[:, 0, :], hg
            dve.wait_ge(sem("edges_summed"), 1)
            dve.wait_ge(sem("self_exp"), 1)
            sums = [bank[4 + i][:, 0:T // 2 * SC].rearrange("p (t c) -> p t c", c=SC) for i in range(2)]
            ee3 = ee_self.rearrange("p (t h) -> p t h", t=T)
            seq_(dve.tensor_tensor(hg4, hg4, ee3.unsqueeze(3).broadcast_to([P, T, GH, GE]), ALU.mult))
            for i in range(2):
                q = slice(i * T // 2, (i + 1) * T // 2)
                dve.tensor_tensor(agg[:, q, :], agg[:, q, :], sums[i][:, :, GH:SC], ALU.add)
                seq_(dve.tensor_tensor(den.rearrange("p (t h) -> p t h", t=T)[:, q, :], ee3[:, q, :],
                                       sums[i][:, :, 0:GH], ALU.add))
            seq_(dve.scalar_tensor_tensor(out=den, in0=ee_self, scalar=1e-16, in1=den, op0=ALU.mult, op1=ALU.add))
            seq_(dve.reciprocal(small[:, 1, :], den))
            seq_(dve.tensor_tensor(hg4, hg4, small[:, 1, :].rearrange("p (t h) -> p t h", t=T).unsqueeze(3)
                                   .broadcast_to([P, T, GH, GE]), ALU.mult))
            seq_(dve.tensor_tensor(src_rows[:, :, 0:GC], agg[:, :, :], rep(bgat_s[:, :], T), ALU.add))
            layer_norm(hg[:, :, :], src_rows[:, :, 0:GC], (lng_s[:, :], lnb_s[:, :]), GC)
            score4 = small[:, 2, :].rearrange("p (t e) -> p t e", t=T)
            seq_(dve.tensor_reduce(score4, hg[:, :, :].rearrange("p t (h e) -> p t e h", h=GH), AX, ALU.add))
            seq_(dve.tensor_scalar(small[:, 2, :], small[:, 2, :], 1.0 / GH, None, ALU.mult))
            top2(score4, GE)

            steps = [0]

            def mlp_sum(acc, n_steps, gated, name):
                with dve.Fori(0, N // CH) as c:
                    for e in range(n_steps):
                        a = e % 2
                        k = c * n_steps + e
                        dve.wait_ge(sem(f"{name}_out"), k + 1)
                        dst = acc[:, bass.ds(c * TB, TB), :]
                        part = bank[2 + a][:, 0:TB * D].rearrange("p (t c) -> p t c", c=D)
                        if gated:
                            mo = mout[:, a, :].rearrange("p (t c) -> p t c", c=D)
                            g_ = gate[:, bass.ds(c * TB, TB), e:e + 1].broadcast_to([P, TB, D])
                            dve.tensor_tensor(mo, part, g_, ALU.mult).then_inc(sem(f"{name}_taken"), 1)
                            dve.wait_ge(sem(f"{name}_taken"), k + 1 + 2)
                            dve.tensor_tensor(dst, dst, mo, ALU.add).then_inc(sem(f"{name}_added"), 1)
                        else:
                            dve.tensor_tensor(dst, dst, part, ALU.add).then_inc(sem(f"{name}_added"), 1)
                            dve.wait_ge(sem(f"{name}_added"), k + 1)
                            dve.memset(stat[:, 7, 2:3], 0.0).then_inc(sem(f"{name}_taken"), 1)
                        dve.wait_ge(sem(f"{name}_added"), k + 1)

            mlp_sum(h, E0, True, "moe0")

            layer_norm(xn[:, :, :], h[:, :, :])
            loaded(dve, "lsh_w_in")
            layer_norm(x5[:, :, :], xn[:, :, :], (norm_s[:, 0, :], norm_s[:, 1, :]))
            dve.memset(stat[:, 7, 2:3], 0.0).then_inc(sem("x_ready"), 1)
            dve.wait_ge(sem("rotated"), 1)
            rp = bank[2][:, :].rearrange("p (t h i) -> p t h i", t=T, h=NH)
            for t in range(0, T, T // 2):
                q = slice(t, t + T // 2)
                dve.tensor_copy(rotv[:, q, :, 0:NBK // 2], rp[:, q])
                dve.tensor_scalar(rotv[:, q, :, NBK // 2:NBK], rp[:, q], -1.0, None, ALU.mult)\
                   .then_inc(sem("rot_copied"), 1)
            dve.wait_ge(sem("rot_copied"), 2)
            hm = hmax.rearrange("p t h -> p (t h)")
            rot2, hot2 = (x.rearrange("p t h i -> p (t h) i") for x in (rotv, hot_b))
            seq_(dve.tensor_reduce(hm, rot2, AX, ALU.max))
            seq_(dve.tensor_tensor(hot2, rot2, bc(hm, NBK), ALU.is_equal))
            seq_(dve.tensor_tensor(hot2, hot2, rep(bucket_rank[:, :], T * NH), ALU.mult))
            seq_(dve.tensor_reduce(hm, hot2, AX, ALU.max))
            seq_(dve.tensor_tensor(hot2, rep(bucket_rank[:, :], T * NH), bc(hm, NBK), ALU.is_equal))
            dve.memset(stat[:, 7, 2:3], 0.0).then_inc(sem("buckets_made"), 1)
            dve.wait_ge(sem("pooled_psum"), 1)
            seq_(dve.tensor_scalar(counts, bank[3][:, 0:S * M], 1e-20, None, ALU.add))
            seq_(dve.reciprocal(kT, counts[0:D, :]))
            dve.tensor_tensor(pooled, *(x.rearrange("p (s m) -> p s m", s=S).unsqueeze(2)
                                        .broadcast_to([D, S, P // M, M]) for x in (bank[2][0:D, 0:S * M], kT)),
                              ALU.mult).then_inc(sem("pooled_made"), 1)
            seq_(dve.tensor_scalar(counts, counts, 0.5, NEG, ALU.is_lt, ALU.mult))
            dve.wait_ge(sem("kv_psum"), 1)
            seq_(dve.tensor_copy(kT, bank[3][0:D, 0:S * M]))
            for s in range(S):
                dve.tensor_tensor(k_bd[:, s], kT[:, s * M:(s + 1) * M].unsqueeze(1).broadcast_to([D, AH, M]),
                                  bc(head_mask[:, :], M), ALU.mult)
                dve.tensor_tensor(v_bd[:, s], bank[2][:, s * D:(s + 1) * D].unsqueeze(1).broadcast_to([P, 2, D]),
                                  row_mask[:, :, :, :].rearrange("p g h d -> p g (h d)"), ALU.mult)\
                   .then_inc(sem("kv_made"), 1)
            dve.wait_ge(sem("kv_made"), S)
            dve.memset(stat[:, 7, 2:3], 0.0).then_inc(sem("kv_ready"), 1)
            with dve.Fori(0, S) as b:
                for q in range(TB):
                    a = q % 2
                    it = TB * b + q
                    s4 = score[:, a, :]
                    s3 = s4.rearrange("p (h m) -> p h m", h=AH)
                    dve.wait_ge(sem("lsh_scores"), it + 1)
                    dve.tensor_tensor(s3, bank[a][:, 0:AH * M].rearrange("p (h m) -> p h m", h=AH),
                                      counts[:, bass.ds(b * M, M)].unsqueeze(1).broadcast_to([P, AH, M]), ALU.add)\
                       .then_inc(sem("lsh_step"), 1)
                    dve.wait_ge(sem("lsh_step"), 5 * it + 1)
                    dve.tensor_reduce(head_st[:, a, 0, :], s3, AX, ALU.max).then_inc(sem("lsh_step"), 1)
                    dve.wait_ge(sem("lsh_step"), 5 * it + 2)
                    dve.tensor_tensor(s3, s3, bc(head_st[:, a, 0, :], M), ALU.subtract).then_inc(sem("lsh_shifted"), 1)
                    dve.wait_ge(sem("lsh_exp"), it + 1)
                    dve.tensor_reduce(head_st[:, a, 1, :], s3, AX, ALU.add).then_inc(sem("lsh_step"), 1)
                    dve.wait_ge(sem("lsh_step"), 5 * it + 3)
                    dve.reciprocal(head_st[:, a, 2, :], head_st[:, a, 1, :]).then_inc(sem("lsh_step"), 1)
                    dve.wait_ge(sem("lsh_step"), 5 * it + 4)
                    dve.wait_ge(sem("lsh_att"), it + 1)
                    o3 = mout[:, a, 0:D].rearrange("p (h d) -> p h d", h=AH)
                    dve.tensor_tensor(o3, bank[4 + a][:, 0:D].rearrange("p (h d) -> p h d", h=AH),
                                      bc(head_st[:, a, 2, :], DH), ALU.mult).then_inc(sem("lsh_step"), 1)
                    dve.wait_ge(sem("lsh_step"), 5 * it + 5)
                    row = xn[:, bass.ds(it, 1), :].rearrange("p t c -> p (t c)")
                    dve.tensor_tensor(row, row, mout[:, a, 0:D], ALU.add).then_inc(sem("lsh_added"), 1)
            dve.wait_ge(sem("lsh_added"), T)
            layer_norm(x5[:, :, :], xn[:, :, :], (norm_s[:, 2, :], norm_s[:, 3, :]))
            dve.memset(stat[:, 7, 2:3], 0.0).then_inc(sem("x_ready"), 1)
            mlp_sum(xn, 1, False, "fc")
            seq_(dve.tensor_tensor(h[:, :, :], h[:, :, :], xn[:, :, :], ALU.add))
            layer_norm(xn[:, :, :], h[:, :, :])
            dve.memset(stat[:, 7, 2:3], 0.0).then_inc(sem("xn_ready"), 1)
            dve.wait_ge(sem("gate_logits"), 1)
            lg = tmp[:, :, 0:E1]
            seq_(dve.tensor_copy(lg, bank[2][:, 0:T * E1].rearrange("p (t e) -> p t e", t=T)))
            top2(lg, E1)
            mlp_sum(h, E1, True, "moe1")
            dve.memset(stat[:, 7, 2:3], 0.0).then_inc(sem("h_final"), 1)

        @block.scalar
        def _(act):
            lns = [0]

            def layer_norm(dst, width=D):
                lns[0] += 1
                act.wait_ge(sem("ln_centred"), lns[0])
                act.activation(dst, tmp[:, 0:T, 0:width], ACT.Square).then_inc(sem("ln_squared"), 1)
                act.wait_ge(sem("ln_var"), lns[0])
                act.activation(stat[:, 4, :], stat[:, 3, :], ACT.Sqrt).then_inc(sem("ln_std"), 1)

            turned = [0]

            def turn(dst):
                for k in range(N // 512):
                    turned[0] += 1
                    act.wait_ge(sem("turned_psum"), turned[0])
                    act.activation(dst[:, k * 512:(k + 1) * 512], bank[k % 2][0:D, :], ACT.Copy)\
                       .then_inc(sem("turned"), 1)

            gates = [0]

            def top2(E):
                gates[0] += 1
                act.wait_ge(sem("gate_shifted"), gates[0])
                act.activation(pairs[:, :, 0, 0:E], pairs2[:, :, 1, 0:E], ACT.Exp).then_inc(sem("gate_exp"), 1)

            for k in range(N // 512):
                act.wait_ge(sem("pos_psum"), k + 1)
                act.activation(xT[0:S, k * 512:(k + 1) * 512], bank[4 + k % 2][0:S, :], ACT.Copy)\
                   .then_inc(sem("pos_turned"), 1)
            act.wait_ge(sem("g_psum"), 1)
            act.activation(w_g[:, :], bank[6][0:D, 0:2 * D], ACT.Copy).then_inc(sem("g_ready"), 1)
            layer_norm(xn[:, :, :])
            turn(xT)
            with act.Fori(0, S) as b:
                for q in range(TB):
                    a = q % 2
                    it = TB * b + q
                    act.wait_ge(sem("y_psum"), it + 1)
                    act.activation(yst[:, a, :], bank[6 + a][0:D, 0:P], ACT.Copy).then_inc(sem("y_ready"), 1)
                    act.wait_ge(sem("max_ready"), it + 1)
                    act.activation(prob[:, a, :], bank[a][:, :], ACT.Exp, bias=mx[:, a, 1:2],
                                   scale=float(D) ** -0.5, accum_out=mx[:, a, 2:3]).then_inc(sem("prob_ready"), 1)
            layer_norm(xn[:, :, :])
            turn(xT)
            act.wait_ge(sem("self_shifted"), 1)
            act.activation(small[:, 6, :], small[:, 2, :], ACT.Exp).then_inc(sem("self_exp"), 1)
            act.wait_ge(sem("cols_known"), 1)
            n = act.value_load(n_cols[0:1, 0:1], min_val=0, max_val=EC)
            with act.Fori(0, EC // (2 * G)) as i:
                with act.If(i * (2 * G) < n):
                    for a in range(2):
                        g = 2 * i + a
                        act.wait_ge(sem("edge_scores"), g + 1)
                        act.activation(msg[:, a, :, 0:GH], z_e[:, a, 0, :, :], ACT.Exp).then_inc(sem("edge_exp"), 1)
                with act.Else():
                    act.nop()
            layer_norm(hg[:, :, :], GC)
            top2(GE)

            def mlp(b1, n_steps, HB, name):
                with act.Fori(0, N // CH) as c:
                    for e in range(n_steps * HB):
                        k = c * (n_steps * HB) + e
                        act.wait_ge(sem(f"{name}_hid_psum"), k + 1)
                        act.wait_ge(sem(f"{name}_hid_free"), k + 1)
                        act.activation(hid[:, e % 2, :], bank[e % 2][:, :], ACT.Gelu, bias=b1[:, e:e + 1])\
                           .then_inc(sem(f"{name}_hid"), 1)

            loaded(act, "moe0_w_in")
            mlp(b1_0, E0, H0 // P, "moe0")
            layer_norm(xn[:, :, :])
            layer_norm(x5[:, :, :])
            turn(xT)
            act.wait_ge(sem("kv_ready"), 1)
            with act.Fori(0, S) as b:
                for q in range(TB):
                    a = q % 2
                    it = TB * b + q
                    act.wait_ge(sem("lq_psum"), it + 1)
                    act.activation(yst[:, a, :], bank[6 + a][0:D, 0:P], ACT.Copy).then_inc(sem("lq_ready"), 1)
                    act.wait_ge(sem("lsh_shifted"), it + 1)
                    act.activation(score[:, a, :], score[:, a, :], ACT.Exp, scale=float(DH) ** -0.5)\
                       .then_inc(sem("lsh_exp"), 1)
                    act.wait_ge(sem("lshT_psum"), it + 1)
                    act.activation(scoreT[:, a, :], bank[2 + a][:, 0:2 * P], ACT.Copy).then_inc(sem("lshT"), 1)
            layer_norm(x5[:, :, :])
            turn(xT)
            loaded(act, "fc_w_in")
            mlp(b1_f, 1, HF // P, "fc")
            layer_norm(xn[:, :, :])
            turn(xT)
            top2(E1)
            loaded(act, "moe1_w_in")
            mlp(b1_1, E1, H1 // P, "moe1")

        @block.tensor
        def _(pe):
            def mm(o, l, r, start=True, stop=True):
                return pe.matmul(o, l, r, start=start, stop=stop)

            turned = [0]

            def turn(src):
                for k in range(N // 512):
                    if k >= 2:
                        pe.wait_ge(sem("turned"), turned[0] - 1)
                    for j in range(4):
                        ins = pe.transpose(bank[k % 2][0:D, j * P:(j + 1) * P], src[:, 4 * k + j, :], ident[:, :])
                    ins.then_inc(sem("turned_psum"), 1)
                    turned[0] += 1
                pe.wait_ge(sem("turned"), turned[0])

            pe.wait_ge(sem("consts_made"), 1)
            pe.wait_ge(sem("onehot_pos_made"), 1)
            for k in range(N // 512):
                if k >= 2:
                    pe.wait_ge(sem("pos_turned"), k - 1)
                for j in range(4):
                    ins = pe.transpose(bank[4 + k % 2][0:S, j * P:(j + 1) * P], hg[:, 4 * k + j, 0:S], ident[:, :])
                ins.then_inc(sem("pos_psum"), 1)
            loaded(pe, "attn_w_in")
            mm(bank[6][0:D, 0:D], w_q[:, :], w_k[:, :])
            mm(bank[6][0:D, D:2 * D], w_q[:, :], w_k[:, :]).then_inc(sem("g_psum"), 1)
            pe.wait_ge(sem("onehot_tok_made"), 1)
            pe.wait_ge(sem("w_tok_masked"), 1)
            loaded(pe, "tokens_in")
            pe.wait_ge(sem("pos_turned"), N // 512)
            for t in range(T):
                o = bank[t // 8][:, t % 8 * D:(t % 8 + 1) * D]
                mm(o, onehot_tok[:, t * P:(t + 1) * P], w_tok[:, :], True, False)
                ins = mm(o, xT[0:S, t * P:(t + 1) * P], w_pe[:, :], False, True)
                if t % 8 == 7:
                    ins.then_inc(sem("embedded"), 1)
            pe.wait_ge(sem("xn_ready"), 1)
            turn(xn)
            pe.wait_ge(sem("g_ready"), 1)
            with pe.Fori(0, S) as b:
                for q in range(TB):
                    a = q % 2
                    it = TB * b + q
                    mm(bank[6 + a][:, 0:P], w_g[:, :], xT[:, bass.ds(b * B + q * P, P)]).then_inc(sem("y_psum"), 1)
                    pe.wait_ge(sem("y_ready"), it + 1)
                    mm(bank[a][:, 0:1], yst[:, a, :], zeros[0:D, 0:1])
                    mm(bank[a][:, :], yst[:, a, :], xT[:, bass.ds(b * B, B)]).then_inc(sem("scores_ready"), 1)
                    pe.wait_ge(sem("prob_ready"), it + 1)
                    for j in range(TB):
                        ins = pe.transpose(bank[2 + a][:, j * P:(j + 1) * P], prob[:, a, j * P:(j + 1) * P], ident[:, :])
                    ins.then_inc(sem("probT_psum"), 1)
                    pe.wait_ge(sem("probT_ready"), it + 1)
                    for j in range(TB):
                        row = xn[:, bass.ds(b * TB + j, 1), :].rearrange("p t c -> p (t c)")
                        ins = mm(bank[4 + a][:, 0:D], probT[:, a, j * P:(j + 1) * P], row, j == 0, j == TB - 1)
                    ins.then_inc(sem("att_out"), 1)
            pe.wait_ge(sem("xn_ready"), 2)
            turn(xn)
            loaded(pe, "gat_w_in")
            for t in range(T):
                ins = mm(bank[2][:, t * GC:(t + 1) * GC], xT[:, t * P:(t + 1) * P], w_gat_s[:, :])
            ins.then_inc(sem("gat_h"), 1)
            half = T // 2 * SC
            pe.wait_ge(sem("att_added"), T)
            for i in range(2):
                ins = pe.matmul(bank[4 + i][:, 0:half], ones[:, :], zeros[:, 0:half], start=True, stop=False,
                                skip_group_check=True)
            ins.then_inc(sem("edge_bufs_free"), 2)
            pe.wait_ge(sem("cols_known"), 1)
            n = pe.value_load(n_cols[0:1, 0:1], min_val=0, max_val=EC)
            with pe.Fori(0, EC // (2 * G)) as i:
                with pe.If(i * (2 * G) < n):
                    for a in range(2):
                        pe.wait_ge(sem("edges_spread"), 2 * i + a + 1)
                        for j in range(G):
                            for k in range(2):
                                rhs = spread[:, a, j, k * T // 2:(k + 1) * T // 2, :].rearrange("p t c -> p (t c)")
                                ins = pe.matmul(bank[4 + k][:, 0:half], hot_lo[:, a, j, :], rhs, start=False,
                                                stop=False, skip_group_check=True)
                        ins.then_inc(sem("edge_bufs_free"), 1)
                with pe.Else():
                    pe.nop()
            for i in range(2):
                ins = pe.matmul(bank[4 + i][:, 0:half], ones[:, :], zeros[:, 0:half], start=False, stop=True,
                                skip_group_check=True)
            ins.then_inc(sem("edges_summed"), 1)

            def mlp(w1, w2, b2, n_steps, HB, name, first=0):
                mm(bank[7][0:1, 0:1], zeros[:, 0:1], zeros[:, 0:1]).then_inc(sem(f"{name}_hid_free"), 2)
                mm(bank[7][0:1, 0:1], zeros[:, 0:1], zeros[:, 0:1]).then_inc(sem(f"{name}_taken"), min(2, n_steps))
                nb = n_steps * HB

                with pe.Fori(0, N // CH) as c:
                    def up(e):
                        mm(bank[e % 2][:, :], w1[:, e * P:(e + 1) * P], xT[:, bass.ds(c * CH, CH)])\
                            .then_inc(sem(f"{name}_hid_psum"), 1)

                    up(0)
                    for e in range(n_steps):
                        for k in range(HB):
                            s = e * HB + k
                            if s + 1 < nb:
                                up(s + 1)
                            pe.wait_ge(sem(f"{name}_hid"), c * nb + s + 1)
                            if k == 0:
                                pe.wait_ge(sem(f"{name}_taken"), c * n_steps + e + 1)
                            for t in range(TB):
                                ins = pe.matmul(bank[2 + e % 2][:, t * D:(t + 1) * D],
                                                hid[:, s % 2, t * P:(t + 1) * P], w2[:, s, :],
                                                start=(k == 0 and t == 0), stop=False, skip_group_check=True)
                            if k == HB - 1:
                                ins.then_inc(sem(f"{name}_hid_free"), 1)
                                for t in range(TB):
                                    ins = pe.matmul(bank[2 + e % 2][:, t * D:(t + 1) * D], ones[0:1, :],
                                                    b2[0:1, e * D:(e + 1) * D], start=False, stop=(t == TB - 1),
                                                    skip_group_check=True)
                                ins.then_inc(sem(f"{name}_out"), 1)
                            else:
                                ins.then_inc(sem(f"{name}_hid_free"), 1)

            loaded(pe, "moe0_w_in")
            mlp(w1_0[:, :, :].rearrange("p e h -> p (e h)"), w2_0, b2_0[:, :, :].rearrange("p e d -> p (e d)"),
                E0, H0 // P, "moe0")

            pe.wait_ge(sem("x_ready"), 1)
            turn(x5)
            loaded(pe, "lsh_w_in")
            pe.wait_ge(sem("moe0_added"), E0 * (N // CH))
            for t in range(T):
                ins = mm(bank[2][:, t * GC:(t + 1) * GC], xT[:, t * P:(t + 1) * P], w_rot[:, :])
            ins.then_inc(sem("rotated"), 1)
            pe.wait_ge(sem("buckets_made"), 1)
            for s in range(S):
                for q in range(TB):
                    t = s * TB + q
                    hb = hot_b[:, t].rearrange("p h i -> p (h i)")
                    mm(bank[2][0:D, s * M:(s + 1) * M], x5[:, t, :], hb, q == 0, q == TB - 1)
                    ins = mm(bank[3][:, s * M:(s + 1) * M], ones[:, :], hb, q == 0, q == TB - 1)
            ins.then_inc(sem("pooled_psum"), 1)
            pe.wait_ge(sem("pooled_made"), 1)
            mm(bank[3][0:D, 0:S * M], w_kv[:, 0:D], pooled[:, :, 0, :])
            for s in range(S):
                ins = mm(bank[2][:, s * D:(s + 1) * D],
                         pooled[:, s].rearrange("p r m -> p (r m)"), w_kv[:, D:2 * D])
            ins.then_inc(sem("kv_psum"), 1)
            pe.wait_ge(sem("kv_ready"), 1)
            with pe.Fori(0, S) as b:
                for q in range(TB):
                    a = q % 2
                    it = TB * b + q
                    mm(bank[6 + a][:, 0:P], w_qq[:, :], xT[:, bass.ds(b * B + q * P, P)]).then_inc(sem("lq_psum"), 1)
                    pe.wait_ge(sem("lq_ready"), it + 1)
                    mm(bank[a][:, 0:1], yst[:, a, :], zeros[0:D, 0:1])
                    mm(bank[a][:, 0:AH * M], yst[:, a, :],
                       k_bd[:, bass.ds(b, 1)].rearrange("p s h m -> p (s h m)")).then_inc(sem("lsh_scores"), 1)
                    pe.wait_ge(sem("lsh_exp"), it + 1)
                    for j in range(2):
                        ins = pe.transpose(bank[2 + a][:, j * P:(j + 1) * P], score[:, a, j * P:(j + 1) * P], ident[:, :])
                    ins.then_inc(sem("lshT_psum"), 1)
                    pe.wait_ge(sem("lshT"), it + 1)
                    for j in range(2):
                        vv = v_bd[:, bass.ds(b, 1), j, :].rearrange("p s c -> p (s c)")
                        ins = mm(bank[4 + a][:, 0:D], scoreT[:, a, j * P:(j + 1) * P], vv, j == 0, j == 1)
                    ins.then_inc(sem("lsh_att"), 1)
            pe.wait_ge(sem("x_ready"), 2)
            turn(x5)
            loaded(pe, "fc_w_in")
            mlp(w1_f, w2_f, b2_f, 1, HF // P, "fc")
            pe.wait_ge(sem("xn_ready"), 3)
            turn(xn)
            loaded(pe, "moe1_w_in")
            pe.wait_ge(sem("fc_added"), N // CH)
            for t in range(T):
                o = bank[2][:, t * E1:(t + 1) * E1]
                mm(o, xT[:, t * P:(t + 1) * P], w_gate[:, :], True, False)
                ins = mm(o, ones[0:1, :], b_gate[:, :], False, True)
            ins.then_inc(sem("gate_logits"), 1)
            mlp(w1_1[:, :, :].rearrange("p e h -> p (e h)"), w2_1, b2_1[:, :, :].rearrange("p e d -> p (e d)"),
                E1, H1 // P, "moe1")


_INS = ['x', 'L0_tok_token_W', 'L0_tok_pe', 'L0_attn_Wq', 'L0_attn_Wk', 'L0_ffn_W_gat', 'L0_ffn_att_src',
        'L0_ffn_att_dst', 'L0_ffn_b_gat', 'L0_ffn_ln_gamma', 'L0_ffn_ln_beta', 'L0_ffn_W1', 'L0_ffn_b1',
        'L0_ffn_W2', 'L0_ffn_b2', 'L0_ffn_edge_index', 'L1_attn_rotations', 'L1_attn_norm1_g',
        'L1_attn_norm1_b', 'L1_attn_q_w', 'L1_attn_kv_w', 'L1_attn_norm2_g', 'L1_attn_norm2_b',
        'L1_attn_fc1_w', 'L1_attn_fc1_b', 'L1_attn_fc2_w', 'L1_attn_fc2_b', 'L1_ffn_Wg', 'L1_ffn_bg',
        'L1_ffn_W1', 'L1_ffn_b1', 'L1_ffn_W2', 'L1_ffn_b2']


def kernel(**inputs):
    import concourse.bacc as _bacc
    from concourse.bass_utils import run_bass_kernel_spmd as _run

    nc = _bacc.Bacc("TRN2", target_bir_lowering=False, num_devices=1)
    arrays, args = {}, []
    for name in _INS:
        a = np.ascontiguousarray(inputs[name])
        arrays[f"in_{name}"] = a
        args.append(nc.dram_tensor(f"in_{name}", a.shape, mybir.dt.from_np(a.dtype), kind="ExternalInput").ap())
    s, b = inputs['x'].shape
    d = inputs['L0_tok_token_W'].shape[1]
    args.append(nc.dram_tensor("out_h", (s, b, d), F32, kind="ExternalOutput").ap())
    tower_program(nc, *args)
    r = _run(nc, [arrays], core_ids=[0])
    return r.results[0]["out_h"]
```

```python
from contextlib import ExitStack

import numpy as np

import concourse.bass as bass
from concourse import mybir

F32 = mybir.dt.float32
I32 = mybir.dt.int32
BF16 = mybir.dt.bfloat16
ALU = mybir.AluOpType
ACT = mybir.ActivationFunctionType
AX = mybir.AxisListType.X
RMAX = bass.bass_isa.ReduceOp.max

P = 128
LN_EPS = 1e-05
SEP_ID, PAD_ID = 13, 1
NEG = -1.0e30
MARGIN = 60.0


def tower_program(nc, seq, tok_w, pe_w, wq, wk, w_gat, att_src, att_dst, b_gat, ln_g, ln_b,
                  m0_w1, m0_b1, m0_w2, m0_b2, edges, rot, n1_g, n1_b, q_w, kv_w, n2_g, n2_b,
                  fc1_w, fc1_b, fc2_w, fc2_b, wg, bg, m1_w1, m1_b1, m1_w2, m1_b2, out):
    S, B = seq.shape
    V, D = tok_w.shape
    N = S * B
    T = N // P
    TB = B // P
    E0, H0 = m0_w1.shape[0], m0_w1.shape[2]
    E1, H1 = m1_w1.shape[0], m1_w1.shape[2]
    HF = fc1_w.shape[1]
    GH, GE = att_src.shape
    GC = GH * GE
    SC = GH + GC
    NEDGE = edges.shape[1]
    EC = NEDGE // P
    NH, NBK = rot.shape[2], 2 * rot.shape[3]
    M = NH * NBK
    AH = 8
    DH = D // AH
    G = 8
    GB = 16
    CH = B
    assert V == P and N % P == 0 and NEDGE % (2 * G * P) == 0 and D == 64 and N == 4096

    with ExitStack() as ctx:
        def sb(name, shape, dt=F32):
            return ctx.enter_context(nc.sbuf_tensor(name, shape, dt))

        sems = {}

        def sem(name):
            if name not in sems:
                sems[name] = ctx.enter_context(nc.semaphore(name))
            return sems[name]

        ident = sb("ident", [P, P])
        iota_free = sb("iota_free", [P, P])
        iota_part = sb("iota_part", [P, 1])
        ones = sb("ones", [P, P])
        zeros = sb("zeros", [P, 320])
        later = sb("later", [P, E1, E1])
        bucket_rank = sb("bucket_rank", [P, NBK])
        head_mask = sb("head_mask", [D, AH])
        row_mask = sb("row_mask", [P, 2, AH, DH])
        w_tok = sb("w_tok", [V, D])
        w_pe = sb("w_pe", [S, D])
        w_q, w_k = sb("w_q", [D, D]), sb("w_k", [D, D])
        w_g = sb("w_g", [D, 2 * D])
        w_gat_s = sb("w_gat_s", [D, GC])
        att_s, att_d = sb("att_s", [P, GC]), sb("att_d", [P, GC])
        bgat_s, lng_s, lnb_s = sb("bgat_s", [P, GC]), sb("lng_s", [P, GC]), sb("lnb_s", [P, GC])
        w_rot = sb("w_rot", [D, NH * NBK // 2])
        norm_s = sb("norm_s", [P, 4, D])
        w_qq, w_kv = sb("w_qq", [D, 2 * D]), sb("w_kv", [D, 2 * D])
        w_gate, b_gate = sb("w_gate", [D, E1]), sb("b_gate", [1, E1])
        w1_0, b1_0 = sb("w1_0", [P, E0, H0]), sb("b1_0", [P, E0])
        w2_0, b2_0 = sb("w2_0", [P, E0, D]), sb("b2_0", [1, E0, D])
        w1_f, b1_f = sb("w1_f", [P, HF]), sb("b1_f", [P, HF // P])
        w2_f, b2_f = sb("w2_f", [P, HF // P, D]), sb("b2_f", [1, D])
        w1_1, b1_1 = sb("w1_1", [P, E1, H1]), sb("b1_1", [P, E1 * H1 // P])
        w2_1, b2_1 = sb("w2_1", [P, E1 * H1 // P, D]), sb("b2_1", [1, E1, D])
        h = sb("h", [P, T, D])
        xn = sb("xn", [P, T, D])
        x5 = sb("x5", [P, T, D])
        xT_2 = sb("xT_2", [P, N])
        xT = xT_2[0:D, :]
        tmp = sb("tmp", [P, T, D])
        stat = sb("stat", [P, 8, T])
        flags = sb("flags", [P, 32])
        gate = sb("gate", [P, T, E1])
        pairs = sb("pairs", [P, T, E1, E1])
        pairs2 = sb("pairs2", [P, T, E1, E1])
        small = sb("small", [P, 8, T * GH])
        hg = sb("hg", [P, T, GC])
        src_rows = sb("src_rows", [P, T, SC])
        dst_rows = sb("dst_rows", [P, T, 2 * GH])
        pad_row = sb("pad_row", [1, 2 * GH])
        arena = sb("arena", [P, 3 * EC])
        key_a, key_b, key_c = (arena[:, i * EC:(i + 1) * EC] for i in range(3))
        e_idx = sb("e_idx", [P, 2, EC], I32)
        x_12, x_13 = (e_idx[:, i, :].bitcast(BF16) for i in range(2))
        dst_b = key_a.bitcast(BF16).rearrange("p (a c) -> p a c", a=2)
        hotb_lo = pairs[:, :, :, :].rearrange("p t e j -> p (t e j)").bitcast(BF16)\
            .rearrange("p (a l g) -> p a l g", a=2, l=P)
        hotb_hi = sb("hotb_hi", [P, 2, GB, T], BF16)
        iota_lo = sb("iota_lo", [P, P, GB], BF16)
        iota_hi = sb("iota_hi", [P, T], BF16)
        last_row = sb("last_row", [P, P])
        last = sb("last", [P, SC])
        cnt_b = sb("cnt_b", [P, T])
        tokc = sb("tokc", [P, T], I32)
        n_valid = sb("n_valid", [P, 2, 2])
        pool_pad = sb("pool_pad", [P, 2])
        n_cols = sb("n_cols", [P, 2], I32)
        idx_st = sb("idx_st", [P, 2, 2, G], I32)
        src_g = sb("src_g", [P, 2, G, SC])
        dst_g = sb("dst_g", [P, 2, G, 2 * GH])
        z_e = sb("z_e", [P, 2, 2, G, GH])
        msg = sb("msg", [P, 2, G, SC])
        dst_part = sb("dst_part", [P, 2, 2, G], I32)
        dst_partf = sb("dst_partf", [P, 2, 2, G])
        hot_hi = sb("hot_hi", [P, 2, G, T])
        hot_lo = sb("hot_lo", [P, 2, G, P])
        spread = sb("spread", [P, 2, G, T, SC])
        big = spread[:, :, :, :, :].rearrange("p a g t c -> p (a g t c)")
        onehot_tok = big[:, 0:N]
        seq_bc = big[:, N:2 * N].bitcast(I32)
        yst = sb("yst", [D, 2, P])
        prob = big[:, 0:1024].rearrange("p (a n) -> p a n", a=2)
        probT = big[:, 1024:2048].rearrange("p (a n) -> p a n", a=2)
        hid = big[:, 2048:4096].rearrange("p (a n) -> p a n", a=4)
        mx = sb("mx", [P, 2, 4])
        mout = sb("mout", [P, 2, TB * D])
        hot_b = big[:, 4096:4096 + T * M].rearrange("p (t h i) -> p t h i", t=T, h=NH)
        rotv = big[:, 5120:5120 + T * M].rearrange("p (t h i) -> p t h i", t=T, h=NH)
        hmax = big[:, 6144:6144 + T * NH].rearrange("p (t h) -> p t h", t=T)
        pooled = big[0:D, 6272:6272 + S * P].rearrange("p (s r m) -> p s r m", s=S, m=M)
        counts = big[:, 7296:7296 + S * M]
        kT = big[0:D, 7552:7552 + S * M]
        k_bd = big[0:D, 7808:7808 + S * AH * M].rearrange("p (s h m) -> p s h m", s=S, h=AH)
        v_bd = arena[:, 0:S * 2 * D].rearrange("p (s g c) -> p s g c", s=S, g=2)
        score = arena[:, 1024:1536].rearrange("p (a n) -> p a n", a=2)
        scoreT = arena[:, 1536:2048].rearrange("p (a n) -> p a n", a=2)
        head_st = sb("head_st", [P, 2, 3, AH])
        assert 3 * (E1 * H1 + HF) // 2 <= 2 * EC and E0 * H0 <= E1 * H1
        parts_1, parts_f, parts_0 = (
            arena[:, EC + 3 * off // 2:EC + 3 * (off + n) // 2].bitcast(BF16).rearrange("p (a n) -> p a n", a=3)
            for off, n in ((0, E1 * H1), (E1 * H1, HF), (0, E0 * H0)))

        tab_src = nc.dram_tensor("tab_src", [N, SC], F32, kind="Internal").ap()
        tab_dst = nc.dram_tensor("tab_dst", [N + 1, 2 * GH], F32, kind="Internal").ap()

        bank = [ctx.enter_context(nc.psum_tensor(f"bank{i}", [P, 512], F32)) for i in range(8)]

        UP = (0, 1, 4, 5)
        assert CH == B

        block = ctx.enter_context(nc.Block())

        def tiles(ap):
            return ap.rearrange("p (t c) -> p t c", c=D)

        @block.sync
        def _(sp):
            def load(dst, src, name, columns=False):
                sp.dma_start(dst, src, allow_slow_non_contiguous=columns).then_inc(sem(name), 16)

            load(e_idx[:, :, :], edges.rearrange("a (p c) -> p a c", p=P), "edges_in")
            load(seq_bc, seq.rearrange("s b -> (s b)").rearrange("(a n) -> a n", a=1).broadcast_to([P, N]), "tokens_in")
            load(tokc[:, :], seq.rearrange("s (q p) -> p (s q)", p=P), "tokens_in", True)
            load(w_tok[:, :], tok_w, "tokens_in")
            load(w_pe[:, :], pe_w[0:S, :], "tokens_in")
            load(w_q[:, :], wq, "attn_w_in")
            load(w_k[:, :], wk, "attn_w_in")
            load(w_gat_s[:, :], w_gat, "gat_w_in")
            for dst, src in ((att_s, att_src.rearrange("h e -> (h e)")), (att_d, att_dst.rearrange("h e -> (h e)")),
                             (bgat_s, b_gat), (lng_s, ln_g), (lnb_s, ln_b)):
                load(dst[:, :], src.rearrange("(a n) -> a n", a=1).broadcast_to([P, GC]), "gat_w_in")
            for half in (slice(0, D), slice(D, P)):
                load(w1_0[half, :, :], m0_w1.rearrange("e d h -> d e h"), "moe0_w_in")
            load(b1_0[:, :], m0_b1.rearrange("e h -> h e"), "moe0_w_in", True)
            load(w2_0[:, :, :], m0_w2.rearrange("e h d -> h e d"), "moe0_w_in")
            load(b2_0[:, :, :], m0_b2.rearrange("(a e) d -> a e d", a=1), "moe0_w_in")
            load(w_rot[:, :], rot.rearrange("a d h i -> (a d) (h i)"), "lsh_w_in")
            for i, src in enumerate((n1_g, n1_b, n2_g, n2_b)):
                load(norm_s[:, i, :], src.rearrange("(a n) -> a n", a=1).broadcast_to([P, D]), "lsh_w_in")
            load(w_qq[:, 0:D], q_w, "lsh_w_in")
            load(w_qq[:, D:2 * D], q_w, "lsh_w_in")
            load(w_kv[:, :], kv_w, "lsh_w_in")
            for half in (slice(0, D), slice(D, P)):
                load(w1_f[half, :], fc1_w, "fc_w_in")
            load(b1_f[:, :], fc1_b.rearrange("(k p) -> p k", p=P), "fc_w_in", True)
            load(w2_f[:, :, :], fc2_w.rearrange("(k p) d -> p k d", p=P), "fc_w_in")
            load(b2_f[:, :], fc2_b.rearrange("(a n) -> a n", a=1), "fc_w_in")
            load(w_gate[:, :], wg, "moe1_w_in")
            load(b_gate[:, :], bg.rearrange("(a n) -> a n", a=1), "moe1_w_in")
            for half in (slice(0, D), slice(D, P)):
                load(w1_1[half, :, :], m1_w1.rearrange("e d h -> d e h"), "moe1_w_in")
            load(b1_1[:, :], m1_b1.rearrange("e (k p) -> p (e k)", p=P), "moe1_w_in", True)
            load(w2_1[:, :, :], m1_w2.rearrange("e (k p) d -> p (e k) d", p=P), "moe1_w_in")
            load(b2_1[:, :, :], m1_b2.rearrange("(a e) d -> a e d", a=1), "moe1_w_in")
            sp.wait_ge(sem("node_rows_made"), 1)
            sp.dma_start(tab_src.rearrange("(t p) c -> p t c", p=P), src_rows[:, :, :]).then_inc(sem("tables_out"), 16)
            sp.dma_start(tab_dst[0:N, :].rearrange("(t p) c -> p t c", p=P), dst_rows[:, :, :])\
              .then_inc(sem("tables_out"), 16)
            sp.dma_start(tab_dst[N:N + 1, :], pad_row[:, :]).then_inc(sem("tables_out"), 16)
            sp.wait_ge(sem("h_final"), 1)
            sp.dma_start(out.rearrange("s (q p) d -> p (s q) d", p=P), h[:, :, :]).then_inc(sem("out_written"), 16)
            sp.wait_ge(sem("out_written"), 16)

        LOADS = {"tokens_in": 4, "attn_w_in": 2, "gat_w_in": 6, "moe0_w_in": 5, "lsh_w_in": 8,
                 "fc_w_in": 5, "moe1_w_in": 7, "edges_in": 1}

        def loaded(eng, name):
            eng.wait_ge(sem(name), 16 * LOADS[name])

        @block.gpsimd
        def _(pool):
            made = sem("pool_consts")
            pool.memset(ident[:, :], 0.0).then_inc(made, 1)
            pool.memset(ones[:, :], 1.0).then_inc(made, 1)
            pool.memset(zeros[:, :], 0.0).then_inc(made, 1)
            pool.memset(later[:, :, :], 1.0).then_inc(made, 1)
            pool.memset(head_mask[:, :], 1.0).then_inc(made, 1)
            pool.memset(row_mask[:, :, :, :], 1.0).then_inc(made, 1)
            pool.memset(pad_row[:, :], 0.0).then_inc(made, 1)
            pool.iota(iota_free[:, :], [[1, P]], base=0, channel_multiplier=0,
                      allow_small_or_imprecise_dtypes=True).then_inc(made, 1)
            pool.iota(iota_part[:, :], [[0, 1]], base=0, channel_multiplier=1,
                      allow_small_or_imprecise_dtypes=True).then_inc(made, 1)
            pool.iota(bucket_rank[:, :], [[-1, NBK]], base=NBK, channel_multiplier=0,
                      allow_small_or_imprecise_dtypes=True).then_inc(made, 1)
            pool.iota(iota_lo[:, :, :], [[1, P], [0, GB]], base=0, channel_multiplier=0,
                      allow_small_or_imprecise_dtypes=True).then_inc(made, 1)
            pool.iota(iota_hi[:, :], [[1, T]], base=0, channel_multiplier=0,
                      allow_small_or_imprecise_dtypes=True).then_inc(made, 1)
            pool.memset(last_row[:, :], 1.0).then_inc(made, 1)
            pool.wait_ge(made, 13)
            pool.affine_select(out=ident[:, :], in_=ident[:, :], compare_op=ALU.not_equal, fill=1.0,
                               base=0, pattern=[[-1, P]], channel_multiplier=1).then_inc(made, 1)
            pool.affine_select(out=last_row[:, :], in_=last_row[:, :], compare_op=ALU.is_ge, fill=0.0,
                               base=1 - P, pattern=[[0, P]], channel_multiplier=1).then_inc(made, 1)
            pool.affine_select(out=later[:, :, :], in_=later[:, :, :], compare_op=ALU.is_gt, fill=0.0,
                               base=0, pattern=[[1, E1], [-1, E1]], channel_multiplier=0).then_inc(made, 1)
            pool.affine_select(out=head_mask[:, :], in_=head_mask[:, :], compare_op=ALU.is_ge, fill=0.0,
                               base=0, pattern=[[-DH, AH]], channel_multiplier=1).then_inc(made, 1)
            pool.affine_select(out=row_mask[:, :, :, :], in_=row_mask[:, :, :, :], compare_op=ALU.is_ge,
                               fill=0.0, base=0, pattern=[[P, 2], [-M, AH], [0, DH]],
                               channel_multiplier=1).then_inc(made, 1)
            pool.wait_ge(made, 18)
            pool.affine_select(out=head_mask[:, :], in_=head_mask[:, :], compare_op=ALU.is_gt, fill=0.0,
                               base=DH, pattern=[[DH, AH]], channel_multiplier=-1).then_inc(made, 1)
            pool.affine_select(out=row_mask[:, :, :, :], in_=row_mask[:, :, :, :], compare_op=ALU.is_gt,
                               fill=0.0, base=M, pattern=[[-P, 2], [M, AH], [0, DH]],
                               channel_multiplier=-1).then_inc(made, 1)
            pool.wait_ge(made, 20)
            pool.memset(pool_pad[:, :], 0.0).then_inc(made, 1)
            pool.wait_ge(made, 21)
            pool.memset(n_valid[:, :, :], 0.0).then_inc(sem("consts_made"), 1)

            pool.wait_ge(sem("rows_counted"), 1)
            pool.partition_all_reduce(n_valid[:, 1, :], n_valid[:, 0, :], P, RMAX).then_inc(sem("count_reduced"), 1)
            pool.wait_ge(sem("a_src_max_part"), 1)
            pool.partition_all_reduce(small[:, 4, 0:GH], small[:, 3, 0:GH], P, RMAX)\
                .then_inc(sem("a_src_max_all"), 1)

            pool.wait_ge(sem("tables_out"), 48)
            pool.wait_ge(sem("cols_known"), 1)
            n = pool.value_load(n_cols[0:1, 0:1], min_val=0, max_val=EC)
            with pool.Fori(0, EC // (2 * G)) as i:
                with pool.If(i * (2 * G) < n):
                    for a in range(2):
                        pool.wait_ge(sem("gathered_used"), 2 * i + a + 1)
                        pool.tensor_copy(idx_st[:, a, :, :], e_idx[:, :, bass.ds(i * (2 * G) + a * G, G)])\
                            .then_inc(sem("indices_staged"), 1)
                        pool.wait_ge(sem("indices_staged"), 2 * i + a + 1)
                        pool.tensor_tensor(pool_pad[:, 0:1], pool_pad[:, 1:2], pool_pad[:, 1:2], ALU.add)
                        for j in range(G):
                            pool.indirect_dma_start(
                                out=src_g[:, a, j, :], out_offset=None, in_=tab_src,
                                in_offset=bass.IndirectOffsetOnAxis(ap=idx_st[:, a, 0, j:j + 1], axis=0))\
                                .then_inc(sem(f"gathered{a}"), 16)
                            pool.indirect_dma_start(
                                out=dst_g[:, a, j, :], out_offset=None, in_=tab_dst,
                                in_offset=bass.IndirectOffsetOnAxis(ap=idx_st[:, a, 1, j:j + 1], axis=0))\
                                .then_inc(sem(f"gathered{a}"), 16)
                with pool.Else():
                    pool.nop()

            split_step = sem("split_steps")
            split_count = [0]

            def seq_(ins):
                split_count[0] += 1
                ins.then_inc(split_step, 1)
                pool.wait_ge(split_step, split_count[0])

            low, high = slice(0, D), slice(D, P)

            def split_weights(w, parts, name):
                loaded(pool, f"{name}_w_in")
                w11, w22, w31 = (parts[:, i, :] for i in range(3))
                seq_(pool.tensor_copy(w11, w))
                seq_(pool.tensor_tensor(w, w, w11, ALU.subtract))
                seq_(pool.tensor_copy(w22, w))
                pool.tensor_tensor(w31[low], w[low], w22[low], ALU.subtract)
                seq_(pool.tensor_copy(w31[high], w11[high]))

            def split_input(nth_turn, name):
                for k in range(N // CH):
                    pool.wait_ge(sem("turned"), nth_turn * (N // 512) + k + 1)
                    x, x12, x13 = (v[:, k * CH:(k + 1) * CH] for v in (xT_2, x_12, x_13))
                    pool.tensor_copy(x13[low], x[low])
                    seq_(pool.tensor_copy(x12, x))
                    seq_(pool.tensor_tensor(x[high], x[high], x12[high], ALU.subtract))
                    seq_(pool.tensor_copy(x12[high], x[high]))
                    seq_(pool.tensor_tensor(x13[high], x[high], x12[high], ALU.subtract))
                    pool.memset(pool_pad[:, 0:1], 0.0).then_inc(sem(f"{name}_split"), 1)

            pool.wait_ge(sem("edges_summed"), 1)
            split_weights(w1_0[:, :, :].rearrange("p e h -> p (e h)"), parts_0, "moe0")
            split_input(1, "moe0")
            split_weights(w1_f[:, :], parts_f, "fc")
            pool.wait_ge(sem("turned"), 2 * (N // 512) + 1)
            split_weights(w1_1[:, :, :].rearrange("p e h -> p (e h)"), parts_1, "moe1")
            split_input(3, "fc")
            split_input(4, "moe1")

        @block.vector
        def _(dve):
            step = sem("dve_steps")
            count = [0]

            def seq_(ins):
                count[0] += 1
                ins.then_inc(step, 1)
                dve.wait_ge(step, count[0])

            def bc(ap, n):
                return ap.unsqueeze(2).broadcast_to([ap.shape[0], ap.shape[1], n])

            def rep(ap, n):
                return ap.unsqueeze(1).broadcast_to([ap.shape[0], n, ap.shape[1]])

            lns = [0]

            def layer_norm(dst, src, gb=None, width=D):
                lns[0] += 1
                t = src.shape[1]
                cen = tmp[:, 0:t, 0:width]
                seq_(dve.tensor_reduce(stat[:, 0, :], src, AX, ALU.add))
                seq_(dve.tensor_scalar(stat[:, 1, :], stat[:, 0, :], -1.0 / width, None, ALU.mult))
                dve.tensor_tensor(cen, src, bc(stat[:, 1, :], width), ALU.add).then_inc(sem("ln_centred"), 1)
                dve.wait_ge(sem("ln_squared"), lns[0])
                seq_(dve.tensor_reduce(stat[:, 2, :], dst, AX, ALU.add))
                dve.tensor_scalar(stat[:, 3, :], stat[:, 2, :], 1.0 / width, LN_EPS, ALU.mult, ALU.add)\
                   .then_inc(sem("ln_var"), 1)
                dve.wait_ge(sem("ln_std"), lns[0])
                seq_(dve.reciprocal(stat[:, 5, :], stat[:, 4, :]))
                seq_(dve.tensor_tensor(dst, cen, bc(stat[:, 5, :], width), ALU.mult))
                if gb:
                    seq_(dve.tensor_tensor(dst, dst, rep(gb[0], t), ALU.mult))
                    seq_(dve.tensor_tensor(dst, dst, rep(gb[1], t), ALU.add))

            def top2(sc, E):
                a = sc.unsqueeze(3).broadcast_to([P, T, E, E])
                b = sc.unsqueeze(2).broadcast_to([P, T, E, E])
                gt, eq = pairs[:, :, 0:E, 0:E], pairs2[:, :, 0:E, 0:E]
                dve.tensor_tensor(gt, b, a, ALU.is_gt)
                seq_(dve.tensor_tensor(eq, b, a, ALU.is_equal))
                seq_(dve.tensor_tensor(eq, eq, later[:, 0:E, 0:E].unsqueeze(1).broadcast_to([P, T, E, E]), ALU.mult))
                seq_(dve.tensor_tensor(gt, gt, eq, ALU.add))
                rank, top = pairs2[:, :, 0, 0:E], stat[:, 0, :]
                seq_(dve.tensor_reduce(rank, gt, AX, ALU.add))
                seq_(dve.tensor_reduce(top, sc, AX, ALU.max))
                shifted = pairs2[:, :, 1, 0:E]
                dve.tensor_tensor(shifted, sc, bc(top, E), ALU.subtract).then_inc(sem("gate_shifted"), 1)
                gates[0] += 1
                dve.wait_ge(sem("gate_exp"), gates[0])
                ex = pairs[:, :, 0, 0:E]
                seq_(dve.tensor_scalar(rank, rank, 1.5, None, ALU.is_lt))
                seq_(dve.tensor_tensor(ex, ex, rank, ALU.mult))
                seq_(dve.tensor_reduce(stat[:, 1, :], ex, AX, ALU.add))
                seq_(dve.reciprocal(stat[:, 2, :], stat[:, 1, :]))
                seq_(dve.tensor_tensor(gate[:, :, 0:E], ex, bc(stat[:, 2, :], E), ALU.mult))

            gates = [0]

            SORT = [(size, m) for k in range(1, EC.bit_length()) for size in (1 << k,)
                    for m in (1 << j for j in reversed(range(k)))]

            def sort_stage(n):
                size, m = SORT[n]
                cur, nxt = (key_a, key_b) if n % 2 == 0 else (key_b, key_a)
                both = size < EC
                x, y = (v.rearrange("p (n r k u m) -> p n r k u m", r=2 if both else 1, u=2, m=m,
                                    k=size // (2 * m)) for v in (cur, nxt))
                for r in range(2 if both else 1):
                    lo, hi = x[:, :, r, :, 0, :], x[:, :, r, :, 1, :]
                    ops = (ALU.min, ALU.max) if r == 0 else (ALU.max, ALU.min)
                    dve.tensor_tensor(y[:, :, r, :, 0, :], lo, hi, ops[0])
                    ins = dve.tensor_tensor(y[:, :, r, :, 1, :], lo, hi, ops[1])
                seq_(ins)

            loaded(dve, "edges_in")
            dve.tensor_scalar(key_b, e_idx[:, 0, :], float(N - 1), None, ALU.min)
            seq_(dve.tensor_scalar(key_c, e_idx[:, 1, :], float(N), None, ALU.min))
            seq_(dve.tensor_scalar(key_a, key_c, float(N), -float(N * N), ALU.mult, ALU.add))
            seq_(dve.tensor_tensor(key_a, key_a, key_b, ALU.add))
            dve.tensor_scalar(key_b, key_b, float(N - 1), None, ALU.is_equal)
            seq_(dve.tensor_tensor(e_idx[:, 0, :].bitcast(F32), key_c, key_a, ALU.subtract))
            seq_(dve.tensor_tensor(key_b, key_b, e_idx[:, 0, :].bitcast(F32), ALU.mult))
            dve.tensor_scalar(key_c, key_c, float(N), 2.0 * N, ALU.is_equal, ALU.mult)
            seq_(dve.tensor_tensor(key_a, key_a, key_b, ALU.add))
            seq_(dve.tensor_tensor(key_a, key_a, key_c, ALU.add))
            dve.wait_ge(sem("consts_made"), 1)
            loaded(dve, "tokens_in")
            seq_(dve.tensor_copy(onehot_tok, seq_bc))
            dve.tensor_scalar(onehot_tok, onehot_tok, iota_part[:, 0:1], None, ALU.is_equal)\
               .then_inc(sem("onehot_tok_made"), 1)
            dve.tensor_scalar(w_tok[0:1, :], w_tok[0:1, :], 0.0, None, ALU.mult).then_inc(sem("w_tok_masked"), 1)
            tok, sep = small[:, 0, 0:T], small[:, 1, 0:T]
            pad, code = small[:, 2, 0:T], small[:, 3, 0:T]
            prev, npad = small[:, 4, 0:TB], small[:, 5, 0:TB]
            skip = small[:, 6, 0:TB]
            seq_(dve.tensor_copy(tok, tokc[:, :]))
            dve.tensor_scalar(sep, tok, float(SEP_ID), None, ALU.is_equal)
            dve.tensor_scalar(pad, tok, float(PAD_ID), None, ALU.is_equal)
            dve.memset(prev, 0.0)
            seq_(dve.memset(npad, 0.0))
            for s in range(S):
                q = slice(s * TB, (s + 1) * TB)
                seq_(dve.tensor_tensor(skip, prev, pad[:, q], ALU.mult))
                dve.scalar_tensor_tensor(out=code[:, q], in0=skip, scalar=100.0, in1=npad,
                                         op0=ALU.mult, op1=ALU.subtract)
                seq_(dve.tensor_tensor(prev, sep[:, q], skip, ALU.max))
                seq_(dve.tensor_tensor(npad, npad, skip, ALU.add))
                seq_(dve.tensor_scalar(code[:, q], code[:, q], float(s), None, ALU.add))
            onehot_pos = hg[:, :, 0:S]
            dve.tensor_tensor(onehot_pos, bc(code, S), rep(iota_free[:, 0:S], T), ALU.is_equal)\
               .then_inc(sem("onehot_pos_made"), 1)

            for b in range(4):
                dve.wait_ge(sem("embedded"), b + 1)
                ins = dve.tensor_copy(h[:, 8 * b:8 * b + 8, :], tiles(bank[b][:, :]))
                seq_(ins)
            layer_norm(xn[:, :, :], h[:, :, :])
            dve.memset(flags[:, 1:2], 0.0).then_inc(sem("xn_ready"), 1)
            def att_add(it):
                a = it % 2
                dve.wait_ge(sem("prob_ready"), it + 1)
                seq_(dve.reciprocal(mx[:, a, 3:4], mx[:, a, 2:3]))
                dve.wait_ge(sem("att_out"), it + 1)
                dve.scalar_tensor_tensor(out=h[:, it, :], in0=bank[4 + a][:, 0:D], scalar=mx[:, a, 3:4],
                                         in1=h[:, it, :], op0=ALU.mult, op1=ALU.add).then_inc(sem("att_added"), 1)

            for it in range(T):
                a = it % 2
                dve.wait_ge(sem("scores_ready"), it + 1)
                seq_(dve.tensor_reduce(mx[:, a, 0:1], bank[a][:, :], AX, ALU.max))
                dve.tensor_scalar(mx[:, a, 1:2], mx[:, a, 0:1], -float(D) ** -0.5, None, ALU.mult)\
                   .then_inc(sem("max_ready"), 1)
                sort_stage(2 * it)
                if it >= 1:
                    att_add(it - 1)
                sort_stage(2 * it + 1)
            att_add(T - 1)
            dve.wait_ge(sem("att_added"), T)

            layer_norm(xn[:, :, :], h[:, :, :])
            dve.memset(flags[:, 2:3], 0.0).then_inc(sem("xn_ready"), 1)
            for n in range(2 * T, len(SORT)):
                sort_stage(n)
            assert len(SORT) % 2 == 0
            dve.tensor_scalar(key_b, key_a, 0.0, None, ALU.is_lt)
            seq_(dve.tensor_scalar(key_c, key_a, float(N), None, ALU.is_lt))
            dve.tensor_reduce(n_valid[:, 0, 0:1], key_b, AX, ALU.add)
            dve.tensor_reduce(n_valid[:, 0, 1:2], key_c, AX, ALU.add).then_inc(sem("rows_counted"), 1)
            dve.wait_ge(sem("rows_counted"), 1)
            seq_(dve.tensor_scalar(e_idx[:, 0, :], key_a, float(N * N), float(N * N), ALU.add, ALU.min))
            dve.tensor_scalar(e_idx[:, 1, :], e_idx[:, 0, :], 12, None, ALU.logical_shift_right)
            seq_(dve.tensor_scalar(e_idx[:, 0, :], e_idx[:, 0, :], N - 1, None, ALU.bitwise_and))
            dve.wait_ge(sem("count_reduced"), 1)
            dve.tensor_copy(n_cols[:, :], n_valid[:, 1, :]).then_inc(sem("cols_known"), 1)

            loaded(dve, "gat_w_in")
            dve.wait_ge(sem("gat_h"), 1)
            seq_(dve.tensor_copy(hg[:, :, :].rearrange("p t c -> p (t c)"), bank[2][:, :]))
            a_src, a_dst, upper, self_e = (small[:, i, :] for i in range(4))
            shift, ee_self = small[:, 5, :], small[:, 6, :]
            prod = pairs[:, :, 0:GH, 0:GE]
            hg4 = hg[:, :, :].rearrange("p t (h e) -> p t h e", h=GH)
            for att, dst in ((att_s, a_src), (att_d, a_dst)):
                w = att[:, :].rearrange("p (h e) -> p h e", h=GH).unsqueeze(1).broadcast_to([P, T, GH, GE])
                seq_(dve.tensor_tensor(prod, hg4, w, ALU.mult))
                seq_(dve.tensor_reduce(dst.rearrange("p (t h) -> p t h", t=T), prod, AX, ALU.add))
            dve.tensor_reduce(small[:, 3, 0:GH], a_src.rearrange("p (t h) -> p h t", t=T), AX, ALU.max)\
               .then_inc(sem("a_src_max_part"), 1)
            dve.wait_ge(sem("a_src_max_all"), 1)
            seq_(dve.tensor_tensor(upper.rearrange("p (t h) -> p t h", t=T), a_dst.rearrange("p (t h) -> p t h", t=T),
                                   rep(small[:, 4, 0:GH], T), ALU.add))
            seq_(dve.tensor_tensor(self_e, a_src, a_dst, ALU.add))
            for x in (upper, self_e):
                seq_(dve.scalar_tensor_tensor(out=x, in0=x, scalar=0.2, in1=x, op0=ALU.mult, op1=ALU.max))
            seq_(dve.scalar_tensor_tensor(out=shift, in0=self_e, scalar=MARGIN, in1=upper,
                                          op0=ALU.add, op1=ALU.min))
            dve.tensor_tensor(upper, self_e, shift, ALU.subtract).then_inc(sem("self_shifted"), 1)
            dve.tensor_copy(src_rows[:, :, 0:GH], a_src.rearrange("p (t h) -> p t h", t=T))
            dve.tensor_copy(src_rows[:, :, GH:SC], hg[:, :, :])
            dve.tensor_copy(dst_rows[:, :, 0:GH], a_dst.rearrange("p (t h) -> p t h", t=T))
            dve.tensor_copy(dst_rows[:, :, GH:2 * GH], shift.rearrange("p (t h) -> p t h", t=T))\
               .then_inc(sem("dst_rows_made"), 1)
            dve.wait_ge(sem("dst_rows_made"), 1)
            dve.memset(flags[:, 3:4], 0.0).then_inc(sem("node_rows_made"), 1)
            dve.memset(flags[:, 4:5], 0.0).then_inc(sem("gathered_used"), 2)
            kb, kc = key_b.bitcast(I32), key_c.bitcast(I32)
            seq_(dve.tensor_scalar(key_b, key_a, 0.0, 2.0 * N * N, ALU.is_lt, ALU.mult))
            seq_(dve.tensor_tensor(key_a, key_a, key_b, ALU.add))
            seq_(dve.tensor_scalar(kb, key_a, float(N), None, ALU.min))
            dve.tensor_scalar(kc, kb, P - 1, None, ALU.bitwise_and)
            seq_(dve.tensor_scalar(kb, kb, 7, None, ALU.logical_shift_right))
            dve.tensor_copy(dst_b[:, 0, :], kc)
            seq_(dve.tensor_copy(dst_b[:, 1, :], kb))

            dve.wait_ge(sem("cols_known"), 1)
            n = dve.value_load(n_cols[0:1, 0:1], min_val=0, max_val=EC)
            nab = dve.value_load(n_cols[0:1, 1:2], min_val=0, max_val=EC)
            def edges_b(i):
                with dve.If(i * (4 * GB) < nab):
                    for k in range(4):
                        a, g = k % 2, 4 * i + k
                        dve.wait_ge(sem("hotb_free"), g + 1)
                        cols = bass.ds(i * (4 * GB) + k * GB, GB)
                        dve.tensor_tensor(hotb_lo[:, a, :, :],
                                          dst_b[:, 0, cols].unsqueeze(1).broadcast_to([P, P, GB]),
                                          iota_lo[:, :, :], ALU.is_equal).then_inc(sem("hotb_made"), 1)
                        dve.tensor_tensor(hotb_hi[:, a, :, :],
                                          dst_b[:, 1, cols].unsqueeze(2).broadcast_to([P, GB, T]),
                                          rep(iota_hi[:, :], GB), ALU.is_equal).then_inc(sem("hotb_made"), 1)
                with dve.Else():
                    dve.nop()

            def edges_a(i):
                with dve.If(i * (2 * G) < n):
                    for a in range(2):
                        g = 2 * i + a
                        cols = e_idx[:, 1, bass.ds(i * (2 * G) + a * G, G)]
                        dve.tensor_scalar(dst_part[:, a, 0, :], cols, P - 1, None, ALU.bitwise_and)\
                           .then_inc(sem("edge_step"), 1)
                        dve.tensor_scalar(dst_part[:, a, 1, :], cols, 7, None, ALU.logical_shift_right)\
                           .then_inc(sem("edge_step"), 1)
                        dve.wait_ge(sem("edge_step"), 7 * g + 2)
                        dve.tensor_copy(dst_partf[:, a, :, :], dst_part[:, a, :, :]).then_inc(sem("edge_step"), 1)
                        dve.wait_ge(sem("edge_step"), 7 * g + 3)
                        dve.wait_ge(sem("edge_bufs_free"), g + 1)
                        dve.tensor_tensor(hot_lo[:, a, :, :], bc(dst_partf[:, a, 0, :], P),
                                          rep(iota_free[:, :], G), ALU.is_equal)
                        dve.tensor_tensor(hot_hi[:, a, :, :], bc(dst_partf[:, a, 1, :], T),
                                          rep(iota_free[:, 0:T], G), ALU.is_equal).then_inc(sem("edge_step"), 1)
                        dve.wait_ge(sem(f"gathered{a}"), 32 * G * (i + 1))
                        dve.tensor_tensor(z_e[:, a, 0, :, :], src_g[:, a, :, 0:GH], dst_g[:, a, :, 0:GH],
                                          ALU.add).then_inc(sem("edge_step"), 1)
                        dve.wait_ge(sem("edge_step"), 7 * g + 5)
                        dve.scalar_tensor_tensor(out=z_e[:, a, 1, :, :], in0=z_e[:, a, 0, :, :], scalar=0.2,
                                                 in1=z_e[:, a, 0, :, :], op0=ALU.mult, op1=ALU.max)\
                           .then_inc(sem("edge_step"), 1)
                        dve.wait_ge(sem("edge_step"), 7 * g + 6)
                        dve.tensor_tensor(z_e[:, a, 0, :, :], z_e[:, a, 1, :, :], dst_g[:, a, :, GH:2 * GH],
                                          ALU.subtract).then_inc(sem("edge_scores"), 1)
                        dve.wait_ge(sem("edge_exp"), g + 1)
                        dve.tensor_tensor(
                            msg[:, a, :, GH:SC].rearrange("p g (h e) -> p g h e", h=GH),
                            src_g[:, a, :, GH:SC].rearrange("p g (h e) -> p g h e", h=GH),
                            msg[:, a, :, 0:GH].unsqueeze(3).broadcast_to([P, G, GH, GE]), ALU.mult)\
                           .then_inc(sem("edge_step"), 1)
                        dve.wait_ge(sem("edge_step"), 7 * g + 7)
                        dve.tensor_tensor(
                            spread[:, a, :, :, :],
                            hot_hi[:, a, :, :].unsqueeze(3).broadcast_to([P, G, T, SC]),
                            msg[:, a, :, :].unsqueeze(2).broadcast_to([P, G, T, SC]), ALU.mult)\
                           .then_inc(sem("edges_spread"), 1)
                        dve.wait_ge(sem("edges_spread"), g + 1)
                        dve.memset(flags[:, 5:6], 0.0).then_inc(sem("gathered_used"), 1)
                with dve.Else():
                    dve.nop()

            with dve.Fori(0, EC // (4 * GB)) as i:
                edges_b(i)
                edges_a(i)
            with dve.Fori(EC // (4 * GB), EC // (2 * G)) as i:
                edges_a(i)

            den, agg = small[:, 0, :], hg
            dve.wait_ge(sem("edges_summed"), 1)
            dve.wait_ge(sem("self_exp"), 1)
            z_b = small[:, 4, :].rearrange("p (t h) -> p t h", t=T)
            dve.tensor_copy(cnt_b[:, :], bank[6][:, 0:T])
            seq_(dve.tensor_copy(last[:, :], bank[7][:, 0:SC]))
            seq_(dve.tensor_tensor(z_b, dst_rows[:, :, 0:GH], rep(last[:, 0:GH], T), ALU.add))
            seq_(dve.scalar_tensor_tensor(out=z_b, in0=z_b, scalar=0.2, in1=z_b, op0=ALU.mult, op1=ALU.max))
            dve.tensor_tensor(z_b, z_b, dst_rows[:, :, GH:2 * GH], ALU.subtract).then_inc(sem("b_shifted"), 1)
            dve.wait_ge(sem("b_exp"), 1)
            seq_(dve.tensor_tensor(z_b, z_b, bc(cnt_b[:, :], GH), ALU.mult))
            dve.wait_ge(sem("tables_out"), 48)
            msg_b = src_rows[:, :, GH:SC].rearrange("p t (h e) -> p t h e", h=GH)
            lh = last[:, GH:SC].rearrange("p (h e) -> p h e", h=GH).unsqueeze(1).broadcast_to([P, T, GH, GE])
            seq_(dve.tensor_tensor(msg_b, lh, z_b.unsqueeze(3).broadcast_to([P, T, GH, GE]), ALU.mult))
            sums = [bank[4 + i][:, 0:T // 2 * SC].rearrange("p (t c) -> p t c", c=SC) for i in range(2)]
            ee3 = ee_self.rearrange("p (t h) -> p t h", t=T)
            seq_(dve.tensor_tensor(hg4, hg4, ee3.unsqueeze(3).broadcast_to([P, T, GH, GE]), ALU.mult))
            seq_(dve.tensor_tensor(agg[:, :, :], agg[:, :, :], src_rows[:, :, GH:SC], ALU.add))
            for i in range(2):
                q = slice(i * T // 2, (i + 1) * T // 2)
                dve.tensor_tensor(agg[:, q, :], agg[:, q, :], sums[i][:, :, GH:SC], ALU.add)
                seq_(dve.tensor_tensor(den.rearrange("p (t h) -> p t h", t=T)[:, q, :], ee3[:, q, :],
                                       sums[i][:, :, 0:GH], ALU.add))
            dve.tensor_tensor(den, den, small[:, 4, :], ALU.add).then_inc(sem("sums_taken"), 1)
            dve.wait_ge(sem("sums_taken"), 1)
            seq_(dve.scalar_tensor_tensor(out=den, in0=ee_self, scalar=1e-16, in1=den, op0=ALU.mult, op1=ALU.add))
            seq_(dve.reciprocal(small[:, 1, :], den))
            seq_(dve.tensor_tensor(hg4, hg4, small[:, 1, :].rearrange("p (t h) -> p t h", t=T).unsqueeze(3)
                                   .broadcast_to([P, T, GH, GE]), ALU.mult))
            seq_(dve.tensor_tensor(src_rows[:, :, 0:GC], agg[:, :, :], rep(bgat_s[:, :], T), ALU.add))
            layer_norm(hg[:, :, :], src_rows[:, :, 0:GC], (lng_s[:, :], lnb_s[:, :]), GC)
            score4 = small[:, 2, :].rearrange("p (t e) -> p t e", t=T)
            seq_(dve.tensor_reduce(score4, hg[:, :, :].rearrange("p t (h e) -> p t e h", h=GH), AX, ALU.add))
            seq_(dve.tensor_scalar(small[:, 2, :], small[:, 2, :], 1.0 / GH, None, ALU.mult))
            top2(score4, GE)

            mlps = [24]

            def mlp_sum(acc, n_steps, gated, name):
                mlps[0] += 1
                free = min(2, n_steps)
                dve.memset(flags[:, mlps[0]:mlps[0] + 1], 0.0).then_inc(sem(f"{name}_taken"), free)
                with dve.Fori(0, N // CH) as c:
                    for e in range(n_steps):
                        k = c * n_steps + e
                        dve.wait_ge(sem(f"{name}_out"), k + 1)
                        dst = acc[:, bass.ds(c * TB, TB), :]
                        a = e % 2
                        part = bank[2 + a][:, 0:TB * D].rearrange("p (t c) -> p t c", c=D)
                        if not gated:
                            dve.tensor_tensor(dst, dst, part, ALU.add).then_inc(sem(f"{name}_taken"), 1)
                            continue
                        mo = mout[:, a, :].rearrange("p (t c) -> p t c", c=D)
                        g_ = gate[:, bass.ds(c * TB, TB), e:e + 1].broadcast_to([P, TB, D])
                        dve.tensor_tensor(mo, part, g_, ALU.mult).then_inc(sem(f"{name}_taken"), 1)
                        dve.wait_ge(sem(f"{name}_taken"), k + 1 + free)
                        if e:
                            dve.wait_ge(sem(f"{name}_added"), k)
                        dve.tensor_tensor(dst, dst, mo, ALU.add).then_inc(sem(f"{name}_added"), 1)
                if gated:
                    dve.wait_ge(sem(f"{name}_added"), n_steps * (N // CH))
                else:
                    dve.wait_ge(sem(f"{name}_taken"), n_steps * (N // CH) + free)

            mlp_sum(h, E0, True, "moe0")

            layer_norm(xn[:, :, :], h[:, :, :])
            loaded(dve, "lsh_w_in")
            layer_norm(x5[:, :, :], xn[:, :, :], (norm_s[:, 0, :], norm_s[:, 1, :]))
            dve.memset(flags[:, 7:8], 0.0).then_inc(sem("x_ready"), 1)
            dve.wait_ge(sem("rotated"), 1)
            rp = bank[2][:, :].rearrange("p (t h i) -> p t h i", t=T, h=NH)
            for t in range(0, T, T // 2):
                q = slice(t, t + T // 2)
                dve.tensor_copy(rotv[:, q, :, 0:NBK // 2], rp[:, q])
                dve.tensor_scalar(rotv[:, q, :, NBK // 2:NBK], rp[:, q], -1.0, None, ALU.mult)\
                   .then_inc(sem("rot_copied"), 1)
            dve.wait_ge(sem("rot_copied"), 2)
            hm = hmax.rearrange("p t h -> p (t h)")
            rot2, hot2 = (x.rearrange("p t h i -> p (t h) i") for x in (rotv, hot_b))
            seq_(dve.tensor_reduce(hm, rot2, AX, ALU.max))
            seq_(dve.tensor_tensor(hot2, rot2, bc(hm, NBK), ALU.is_equal))
            seq_(dve.tensor_tensor(hot2, hot2, rep(bucket_rank[:, :], T * NH), ALU.mult))
            seq_(dve.tensor_reduce(hm, hot2, AX, ALU.max))
            seq_(dve.tensor_tensor(hot2, rep(bucket_rank[:, :], T * NH), bc(hm, NBK), ALU.is_equal))
            dve.memset(flags[:, 8:9], 0.0).then_inc(sem("buckets_made"), 1)
            dve.wait_ge(sem("pooled_psum"), 1)
            seq_(dve.tensor_scalar(counts, bank[3][:, 0:S * M], 1e-20, None, ALU.add))
            seq_(dve.reciprocal(kT, counts[0:D, :]))
            dve.tensor_tensor(pooled, *(x.rearrange("p (s m) -> p s m", s=S).unsqueeze(2)
                                        .broadcast_to([D, S, P // M, M]) for x in (bank[2][0:D, 0:S * M], kT)),
                              ALU.mult).then_inc(sem("pooled_made"), 1)
            seq_(dve.tensor_scalar(counts, counts, 0.5, NEG, ALU.is_lt, ALU.mult))
            dve.wait_ge(sem("kv_psum"), 1)
            seq_(dve.tensor_copy(kT, bank[3][0:D, 0:S * M]))
            for s in range(S):
                dve.tensor_tensor(k_bd[:, s], kT[:, s * M:(s + 1) * M].unsqueeze(1).broadcast_to([D, AH, M]),
                                  bc(head_mask[:, :], M), ALU.mult)
                dve.tensor_tensor(v_bd[:, s], bank[2][:, s * D:(s + 1) * D].unsqueeze(1).broadcast_to([P, 2, D]),
                                  row_mask[:, :, :, :].rearrange("p g h d -> p g (h d)"), ALU.mult)\
                   .then_inc(sem("kv_made"), 1)
            dve.wait_ge(sem("kv_made"), S)
            dve.memset(flags[:, 9:10], 0.0).then_inc(sem("kv_ready"), 1)
            def lsh_shift(it, a, b):
                s3 = score[:, a, :].rearrange("p (h m) -> p h m", h=AH)
                dve.wait_ge(sem("lsh_scores"), it + 1)
                dve.tensor_tensor(s3, bank[a][:, 0:AH * M].rearrange("p (h m) -> p h m", h=AH),
                                  counts[:, bass.ds(b * M, M)].unsqueeze(1).broadcast_to([P, AH, M]), ALU.add)\
                   .then_inc(sem("lsh_shift_step"), 1)
                dve.wait_ge(sem("lsh_shift_step"), 2 * it + 1)
                dve.tensor_reduce(head_st[:, a, 0, :], s3, AX, ALU.max).then_inc(sem("lsh_shift_step"), 1)
                dve.wait_ge(sem("lsh_shift_step"), 2 * it + 2)
                dve.tensor_tensor(s3, s3, bc(head_st[:, a, 0, :], M), ALU.subtract).then_inc(sem("lsh_shifted"), 1)

            def lsh_add(it, a):
                s3 = score[:, a, :].rearrange("p (h m) -> p h m", h=AH)
                step3 = sem("lsh_add_step")
                dve.wait_ge(sem("lsh_exp"), it + 1)
                dve.tensor_reduce(head_st[:, a, 1, :], s3, AX, ALU.add).then_inc(step3, 1)
                dve.wait_ge(step3, 3 * it + 1)
                dve.reciprocal(head_st[:, a, 2, :], head_st[:, a, 1, :]).then_inc(step3, 1)
                dve.wait_ge(step3, 3 * it + 2)
                dve.wait_ge(sem("lsh_att"), it + 1)
                o3 = mout[:, a, 0:D].rearrange("p (h d) -> p h d", h=AH)
                dve.tensor_tensor(o3, bank[4 + a][:, 0:D].rearrange("p (h d) -> p h d", h=AH),
                                  bc(head_st[:, a, 2, :], DH), ALU.mult).then_inc(step3, 1)
                dve.wait_ge(step3, 3 * it + 3)
                row = xn[:, bass.ds(it, 1), :].rearrange("p t c -> p (t c)")
                dve.tensor_tensor(row, row, mout[:, a, 0:D], ALU.add).then_inc(sem("lsh_added"), 1)

            def lsh_batch(b, start=False):
                for q in range(TB):
                    it = TB * b + q
                    lsh_shift(it, q % 2, b)
                    if not (start and q == 0):
                        lsh_add(it - 1, 1 - q % 2)

            lsh_batch(0, start=True)
            with dve.Fori(1, S) as b:
                lsh_batch(b)
            lsh_add(T - 1, 1)
            dve.wait_ge(sem("lsh_added"), T)
            layer_norm(x5[:, :, :], xn[:, :, :], (norm_s[:, 2, :], norm_s[:, 3, :]))
            dve.memset(flags[:, 10:11], 0.0).then_inc(sem("x_ready"), 1)
            mlp_sum(xn, 1, False, "fc")
            seq_(dve.tensor_tensor(h[:, :, :], h[:, :, :], xn[:, :, :], ALU.add))
            layer_norm(xn[:, :, :], h[:, :, :])
            dve.memset(flags[:, 11:12], 0.0).then_inc(sem("xn_ready"), 1)
            dve.wait_ge(sem("gate_logits"), 1)
            lg = tmp[:, :, 0:E1]
            seq_(dve.tensor_copy(lg, bank[2][:, 0:T * E1].rearrange("p (t e) -> p t e", t=T)))
            top2(lg, E1)
            mlp_sum(h, E1, True, "moe1")
            dve.memset(flags[:, 12:13], 0.0).then_inc(sem("h_final"), 1)

        @block.scalar
        def _(act):
            lns = [0]

            def layer_norm(dst, width=D):
                lns[0] += 1
                act.wait_ge(sem("ln_centred"), lns[0])
                act.activation(dst, tmp[:, 0:T, 0:width], ACT.Square).then_inc(sem("ln_squared"), 1)
                act.wait_ge(sem("ln_var"), lns[0])
                act.activation(stat[:, 4, :], stat[:, 3, :], ACT.Sqrt).then_inc(sem("ln_std"), 1)

            turned = [0]

            def turn(twice=True):
                for k in range(N // 512):
                    turned[0] += 1
                    act.wait_ge(sem("turned_psum"), turned[0])
                    cols = slice(k * 512, (k + 1) * 512)
                    if twice:
                        act.activation(xT_2[D:P, cols], bank[k % 2][0:D, :], ACT.Copy)
                    act.activation(xT[:, cols], bank[k % 2][0:D, :], ACT.Copy)\
                       .then_inc(sem("turned"), 1)

            gates = [0]

            def top2(E):
                gates[0] += 1
                act.wait_ge(sem("gate_shifted"), gates[0])
                act.activation(pairs[:, :, 0, 0:E], pairs2[:, :, 1, 0:E], ACT.Exp).then_inc(sem("gate_exp"), 1)

            for k in range(N // 512):
                act.wait_ge(sem("pos_psum"), k + 1)
                act.activation(xT[0:S, k * 512:(k + 1) * 512], bank[4 + k % 2][0:S, :], ACT.Copy)\
                   .then_inc(sem("pos_turned"), 1)
            act.wait_ge(sem("g_psum"), 1)
            act.activation(w_g[:, :], bank[6][0:D, 0:2 * D], ACT.Copy).then_inc(sem("g_ready"), 1)
            layer_norm(xn[:, :, :])
            turn(False)
            def y_copy(it, a):
                act.wait_ge(sem("y_psum"), it + 1)
                act.activation(yst[:, a, :], bank[6 + a][0:D, 0:P], ACT.Copy).then_inc(sem("y_ready"), 1)

            y_copy(0, 0)
            with act.Fori(0, S) as b:
                for q in range(TB):
                    a = q % 2
                    it = TB * b + q
                    y_copy(it + 1, 1 - a)
                    act.wait_ge(sem("max_ready"), it + 1)
                    act.activation(prob[:, a, :], bank[a][:, :], ACT.Exp, bias=mx[:, a, 1:2],
                                   scale=float(D) ** -0.5, accum_out=mx[:, a, 2:3]).then_inc(sem("prob_ready"), 1)
                    act.wait_ge(sem("probT_psum"), it + 1)
                    act.activation(probT[:, a, :], bank[2 + a][:, :], ACT.Copy).then_inc(sem("probT_ready"), 1)
            layer_norm(xn[:, :, :])
            turn()
            act.wait_ge(sem("self_shifted"), 1)
            act.activation(small[:, 6, :], small[:, 2, :], ACT.Exp).then_inc(sem("self_exp"), 1)
            act.wait_ge(sem("cols_known"), 1)
            n = act.value_load(n_cols[0:1, 0:1], min_val=0, max_val=EC)
            with act.Fori(0, EC // (2 * G)) as i:
                with act.If(i * (2 * G) < n):
                    for a in range(2):
                        g = 2 * i + a
                        act.wait_ge(sem("edge_scores"), g + 1)
                        act.activation(msg[:, a, :, 0:GH], z_e[:, a, 0, :, :], ACT.Exp).then_inc(sem("edge_exp"), 1)
                with act.Else():
                    act.nop()
            act.wait_ge(sem("b_shifted"), 1)
            act.activation(small[:, 4, :], small[:, 4, :], ACT.Exp).then_inc(sem("b_exp"), 1)
            layer_norm(hg[:, :, :], GC)
            top2(GE)

            def mlp(b1, n_steps, HB, name):
                with act.Fori(0, N // CH) as c:
                    for e in range(n_steps * HB):
                        k = c * (n_steps * HB) + e
                        act.wait_ge(sem(f"{name}_hid_psum"), k + 1)
                        act.activation(hid[:, e % 4, :], bank[UP[e % 4]][:, :], ACT.Gelu, bias=b1[:, e:e + 1])\
                           .then_inc(sem(f"{name}_hid"), 1)

            loaded(act, "moe0_w_in")
            mlp(b1_0, E0, H0 // P, "moe0")
            layer_norm(xn[:, :, :])
            layer_norm(x5[:, :, :])
            turn(False)
            act.wait_ge(sem("kv_ready"), 1)
            def lq_copy(it, a):
                act.wait_ge(sem("lq_psum"), it + 1)
                act.activation(yst[:, a, :], bank[6 + a][0:D, 0:P], ACT.Copy).then_inc(sem("lq_ready"), 1)

            lq_copy(0, 0)
            with act.Fori(0, S) as b:
                for q in range(TB):
                    a = q % 2
                    it = TB * b + q
                    lq_copy(it + 1, 1 - a)
                    act.wait_ge(sem("lsh_shifted"), it + 1)
                    act.activation(score[:, a, :], score[:, a, :], ACT.Exp, scale=float(DH) ** -0.5)\
                       .then_inc(sem("lsh_exp"), 1)
                    act.wait_ge(sem("lshT_psum"), it + 1)
                    act.activation(scoreT[:, a, :], bank[2 + a][:, 0:2 * P], ACT.Copy).then_inc(sem("lshT"), 1)
            layer_norm(x5[:, :, :])
            turn()
            loaded(act, "fc_w_in")
            mlp(b1_f, 1, HF // P, "fc")
            layer_norm(xn[:, :, :])
            turn()
            top2(E1)
            loaded(act, "moe1_w_in")
            mlp(b1_1, E1, H1 // P, "moe1")

        @block.tensor
        def _(pe):
            def mm(o, l, r, start=True, stop=True):
                return pe.matmul(o, l, r, start=start, stop=stop)

            turned = [0]

            def turn(src):
                for k in range(N // 512):
                    if k >= 2:
                        pe.wait_ge(sem("turned"), turned[0] - 1)
                    for j in range(4):
                        ins = pe.transpose(bank[k % 2][0:D, j * P:(j + 1) * P], src[:, 4 * k + j, :], ident[:, :])
                    ins.then_inc(sem("turned_psum"), 1)
                    turned[0] += 1
                pe.wait_ge(sem("turned"), turned[0])

            pe.wait_ge(sem("consts_made"), 1)
            pe.wait_ge(sem("onehot_pos_made"), 1)
            for k in range(N // 512):
                if k >= 2:
                    pe.wait_ge(sem("pos_turned"), k - 1)
                for j in range(4):
                    ins = pe.transpose(bank[4 + k % 2][0:S, j * P:(j + 1) * P], hg[:, 4 * k + j, 0:S], ident[:, :])
                ins.then_inc(sem("pos_psum"), 1)
            loaded(pe, "attn_w_in")
            mm(bank[6][0:D, 0:D], w_q[:, :], w_k[:, :])
            mm(bank[6][0:D, D:2 * D], w_q[:, :], w_k[:, :]).then_inc(sem("g_psum"), 1)
            pe.wait_ge(sem("onehot_tok_made"), 1)
            pe.wait_ge(sem("w_tok_masked"), 1)
            loaded(pe, "tokens_in")
            pe.wait_ge(sem("pos_turned"), N // 512)
            for t in range(T):
                o = bank[t // 8][:, t % 8 * D:(t % 8 + 1) * D]
                mm(o, onehot_tok[:, t * P:(t + 1) * P], w_tok[:, :], True, False)
                ins = mm(o, xT[0:S, t * P:(t + 1) * P], w_pe[:, :], False, True)
                if t % 8 == 7:
                    ins.then_inc(sem("embedded"), 1)
            pe.wait_ge(sem("xn_ready"), 1)
            turn(xn)
            pe.wait_ge(sem("g_ready"), 1)
            def att_y(it, a, col):
                mm(bank[6 + a][:, 0:P], w_g[:, :], xT[:, col]).then_inc(sem("y_psum"), 1)

            def att_scores(it, a, cols):
                pe.wait_ge(sem("y_ready"), it + 1)
                mm(bank[a][:, 0:1], yst[:, a, :], zeros[0:D, 0:1])
                mm(bank[a][:, :], yst[:, a, :], xT[:, cols]).then_inc(sem("scores_ready"), 1)

            def att_turn(it, a):
                pe.wait_ge(sem("prob_ready"), it + 1)
                for j in range(TB):
                    ins = pe.transpose(bank[2 + a][:, j * P:(j + 1) * P], prob[:, a, j * P:(j + 1) * P], ident[:, :])
                ins.then_inc(sem("probT_psum"), 1)

            def att_out(it, a, tile0, first=False):
                pe.wait_ge(sem("probT_ready"), it + 1)
                if not first:
                    pe.wait_ge(sem("att_added"), it - 1)
                for j in range(TB):
                    row = xn[:, bass.ds(tile0 + j, 1), :].rearrange("p t c -> p (t c)")
                    ins = mm(bank[4 + a][:, 0:D], probT[:, a, j * P:(j + 1) * P], row, j == 0, j == TB - 1)
                ins.then_inc(sem("att_out"), 1)

            def att_batch(b, start=False, end=False):
                for q in range(TB):
                    a, it = q % 2, TB * b + q
                    more = not (end and q == TB - 1)
                    nb = b + (1 if q == TB - 1 else 0)
                    att_y(it + 1, 1 - a, bass.ds((b * B + (q + 1) * P) if more else b * B, P))
                    if not (start and q == 0):
                        att_out(it - 1, 1 - a, (b if q else b - 1) * TB, start and q <= 2)
                    if more:
                        att_scores(it + 1, 1 - a, bass.ds(nb * B, B))
                    att_turn(it, a)

            att_y(0, 0, bass.ds(0, P))
            att_scores(0, 0, bass.ds(0, B))
            att_batch(0, start=True)
            with pe.Fori(1, S - 1) as b:
                att_batch(b)
            att_batch(S - 1, end=True)
            att_out(T - 1, 1, (S - 1) * TB)
            pe.wait_ge(sem("xn_ready"), 2)
            turn(xn)
            loaded(pe, "gat_w_in")
            for t in range(T):
                ins = mm(bank[2][:, t * GC:(t + 1) * GC], xT[:, t * P:(t + 1) * P], w_gat_s[:, :])
            ins.then_inc(sem("gat_h"), 1)
            half = T // 2 * SC
            pe.wait_ge(sem("att_added"), T)
            for i in range(2):
                ins = pe.matmul(bank[4 + i][:, 0:half], ones[:, :], zeros[:, 0:half], start=True, stop=False,
                                skip_group_check=True)
            ins.then_inc(sem("edge_bufs_free"), 2)
            pe.matmul(bank[6][:, 0:T], ones[:, :], zeros[:, 0:T], start=True, stop=False,
                      skip_group_check=True).then_inc(sem("hotb_free"), 2)
            pe.wait_ge(sem("node_rows_made"), 1)
            mm(bank[7][:, 0:SC], last_row[:, :], src_rows[:, T - 1, :])
            pe.wait_ge(sem("cols_known"), 1)
            n = pe.value_load(n_cols[0:1, 0:1], min_val=0, max_val=EC)
            nab = pe.value_load(n_cols[0:1, 1:2], min_val=0, max_val=EC)
            def edges_b(i):
                with pe.If(i * (4 * GB) < nab):
                    for k in range(4):
                        pe.wait_ge(sem("hotb_made"), 2 * (4 * i + k + 1))
                        for j in range(GB):
                            ins = pe.matmul(bank[6][:, 0:T], hotb_lo[:, k % 2, :, j], hotb_hi[:, k % 2, j, :],
                                            start=False, stop=False, skip_group_check=True)
                        ins.then_inc(sem("hotb_free"), 1)
                with pe.Else():
                    pe.nop()

            def edges_a(i):
                with pe.If(i * (2 * G) < n):
                    for a in range(2):
                        pe.wait_ge(sem("edges_spread"), 2 * i + a + 1)
                        for j in range(G):
                            for k in range(2):
                                rhs = spread[:, a, j, k * T // 2:(k + 1) * T // 2, :].rearrange("p t c -> p (t c)")
                                ins = pe.matmul(bank[4 + k][:, 0:half], hot_lo[:, a, j, :], rhs, start=False,
                                                stop=False, skip_group_check=True)
                        ins.then_inc(sem("edge_bufs_free"), 1)
                with pe.Else():
                    pe.nop()

            with pe.Fori(0, EC // (4 * GB)) as i:
                edges_b(i)
                edges_a(i)
            with pe.Fori(EC // (4 * GB), EC // (2 * G)) as i:
                edges_a(i)
            for i in range(2):
                ins = pe.matmul(bank[4 + i][:, 0:half], ones[:, :], zeros[:, 0:half], start=False, stop=True,
                                skip_group_check=True)
            pe.matmul(bank[6][:, 0:T], ones[:, :], zeros[:, 0:T], start=False, stop=True,
                      skip_group_check=True).then_inc(sem("edges_summed"), 1)

            def mlp(w1, w2, b2, n_steps, HB, name):
                nb = n_steps * HB
                R = min(len(UP), nb)
                lead = R // 2

                def up(e, cols):
                    for i, x in enumerate((x_12, x_12, x_13)):
                        ins = mm(bank[UP[e % 4]][:, :], w1[:, i, e * P:(e + 1) * P], x[:, cols], i == 0, i == 2)
                    ins.then_inc(sem(f"{name}_hid_psum"), 1)

                def chunk(c, final=False):
                    for s in range(nb):
                        e, k = divmod(s, HB)
                        if s + lead < nb:
                            up(s + lead, bass.ds(c * CH, CH))
                        elif not final:
                            if s + lead == nb:
                                pe.wait_ge(sem(f"{name}_split"), c + 2)
                                mm(bank[UP[0]][:, 0:1], zeros[:, 0:P], zeros[:, 0:1])
                            up(s + lead - nb, bass.ds(c * CH + CH, CH))
                        o = bank[2 + e % 2]
                        if k == 0:
                            pe.wait_ge(sem(f"{name}_taken"), c * n_steps + e + 1)
                            pe.matmul(o[:, 0:TB * D].rearrange("p (t d) -> p t d", d=D), ones[0:1, :],
                                      b2[0:1, e * D:(e + 1) * D].unsqueeze(1).broadcast_to([1, TB, D]),
                                      start=True, stop=False, skip_group_check=True)
                        pe.wait_ge(sem(f"{name}_hid"), c * nb + s + 1)
                        for t in range(TB):
                            ins = pe.matmul(o[:, t * D:(t + 1) * D], hid[:, s % 4, t * P:(t + 1) * P], w2[:, s, :],
                                            start=False, stop=(k == HB - 1), skip_group_check=True)
                        if k == HB - 1:
                            ins.then_inc(sem(f"{name}_out"), 1)

                pe.wait_ge(sem(f"{name}_split"), 1)
                for e in range(lead):
                    up(e, bass.ds(0, CH))
                with pe.Fori(0, N // CH - 1) as c:
                    chunk(c)
                chunk(N // CH - 1, final=True)

            loaded(pe, "moe0_w_in")
            pe.wait_ge(sem("sums_taken"), 1)
            mlp(parts_0, w2_0, b2_0[:, :, :].rearrange("p e d -> p (e d)"),
                E0, H0 // P, "moe0")

            pe.wait_ge(sem("x_ready"), 1)
            turn(x5)
            loaded(pe, "lsh_w_in")
            pe.wait_ge(sem("moe0_added"), E0 * (N // CH))
            for t in range(T):
                ins = mm(bank[2][:, t * GC:(t + 1) * GC], xT[:, t * P:(t + 1) * P], w_rot[:, :])
            ins.then_inc(sem("rotated"), 1)
            pe.wait_ge(sem("buckets_made"), 1)
            for s in range(S):
                for q in range(TB):
                    t = s * TB + q
                    hb = hot_b[:, t].rearrange("p h i -> p (h i)")
                    mm(bank[2][0:D, s * M:(s + 1) * M], x5[:, t, :], hb, q == 0, q == TB - 1)
                    ins = mm(bank[3][:, s * M:(s + 1) * M], ones[:, :], hb, q == 0, q == TB - 1)
            ins.then_inc(sem("pooled_psum"), 1)
            pe.wait_ge(sem("pooled_made"), 1)
            mm(bank[3][0:D, 0:S * M], w_kv[:, 0:D], pooled[:, :, 0, :])
            for s in range(S):
                ins = mm(bank[2][:, s * D:(s + 1) * D],
                         pooled[:, s].rearrange("p r m -> p (r m)"), w_kv[:, D:2 * D])
            ins.then_inc(sem("kv_psum"), 1)
            pe.wait_ge(sem("kv_ready"), 1)
            def lsh_q(it, a, cols):
                mm(bank[6 + a][:, 0:P], w_qq[:, :], xT[:, cols]).then_inc(sem("lq_psum"), 1)

            def lsh_scores(it, a, b):
                pe.wait_ge(sem("lq_ready"), it + 1)
                mm(bank[a][:, 0:1], yst[:, a, :], zeros[0:D, 0:1])
                mm(bank[a][:, 0:AH * M], yst[:, a, :],
                   k_bd[:, bass.ds(b, 1)].rearrange("p s h m -> p (s h m)")).then_inc(sem("lsh_scores"), 1)

            def lsh_turn(it, a):
                pe.wait_ge(sem("lsh_exp"), it + 1)
                for j in range(2):
                    ins = pe.transpose(bank[2 + a][:, j * P:(j + 1) * P], score[:, a, j * P:(j + 1) * P], ident[:, :])
                ins.then_inc(sem("lshT_psum"), 1)

            def lsh_out(it, a, b, first=False):
                pe.wait_ge(sem("lshT"), it + 1)
                if not first:
                    pe.wait_ge(sem("lsh_added"), it - 1)
                for j in range(2):
                    vv = v_bd[:, bass.ds(b, 1), j, :].rearrange("p s c -> p (s c)")
                    ins = mm(bank[4 + a][:, 0:D], scoreT[:, a, j * P:(j + 1) * P], vv, j == 0, j == 1)
                ins.then_inc(sem("lsh_att"), 1)

            def lsh_batch(b, start=False, end=False):
                for q in range(TB):
                    a, it = q % 2, TB * b + q
                    more = not (end and q == TB - 1)
                    lsh_q(it + 1, 1 - a, bass.ds((b * B + (q + 1) * P) if more else b * B, P))
                    if not (start and q == 0):
                        lsh_out(it - 1, 1 - a, b if q else b - 1, start and q <= 2)
                    if more:
                        lsh_scores(it + 1, 1 - a, b + (1 if q == TB - 1 else 0))
                    lsh_turn(it, a)

            lsh_q(0, 0, bass.ds(0, P))
            lsh_scores(0, 0, 0)
            lsh_batch(0, start=True)
            with pe.Fori(1, S - 1) as b:
                lsh_batch(b)
            lsh_batch(S - 1, end=True)
            lsh_out(T - 1, 1, S - 1)
            pe.wait_ge(sem("x_ready"), 2)
            turn(x5)
            loaded(pe, "fc_w_in")
            mlp(parts_f, w2_f, b2_f, 1, HF // P, "fc")
            pe.wait_ge(sem("xn_ready"), 3)
            turn(xn)
            loaded(pe, "moe1_w_in")
            pe.wait_ge(sem("fc_taken"), N // CH + 1)
            for t in range(T):
                o = bank[2][:, t * E1:(t + 1) * E1]
                mm(o, xT[:, t * P:(t + 1) * P], w_gate[:, :], True, False)
                ins = mm(o, ones[0:1, :], b_gate[:, :], False, True)
            ins.then_inc(sem("gate_logits"), 1)
            mlp(parts_1, w2_1, b2_1[:, :, :].rearrange("p e d -> p (e d)"),
                E1, H1 // P, "moe1")


_INS = ['x', 'L0_tok_token_W', 'L0_tok_pe', 'L0_attn_Wq', 'L0_attn_Wk', 'L0_ffn_W_gat', 'L0_ffn_att_src',
        'L0_ffn_att_dst', 'L0_ffn_b_gat', 'L0_ffn_ln_gamma', 'L0_ffn_ln_beta', 'L0_ffn_W1', 'L0_ffn_b1',
        'L0_ffn_W2', 'L0_ffn_b2', 'L0_ffn_edge_index', 'L1_attn_rotations', 'L1_attn_norm1_g',
        'L1_attn_norm1_b', 'L1_attn_q_w', 'L1_attn_kv_w', 'L1_attn_norm2_g', 'L1_attn_norm2_b',
        'L1_attn_fc1_w', 'L1_attn_fc1_b', 'L1_attn_fc2_w', 'L1_attn_fc2_b', 'L1_ffn_Wg', 'L1_ffn_bg',
        'L1_ffn_W1', 'L1_ffn_b1', 'L1_ffn_W2', 'L1_ffn_b2']


def kernel(**inputs):
    import concourse.bacc as _bacc
    from concourse.bass_utils import run_bass_kernel_spmd as _run

    nc = _bacc.Bacc("TRN2", target_bir_lowering=False, num_devices=1)
    arrays, args = {}, []
    for name in _INS:
        a = np.ascontiguousarray(inputs[name])
        arrays[f"in_{name}"] = a
        args.append(nc.dram_tensor(f"in_{name}", a.shape, mybir.dt.from_np(a.dtype), kind="ExternalInput").ap())
    s, b = inputs['x'].shape
    d = inputs['L0_tok_token_W'].shape[1]
    args.append(nc.dram_tensor("out_h", (s, b, d), F32, kind="ExternalOutput").ap())
    tower_program(nc, *args)
    r = _run(nc, [arrays], core_ids=[0])
    return r.results[0]["out_h"]
```

```python
from contextlib import ExitStack

import numpy as np

import concourse.bass as bass
from concourse import mybir

F32 = mybir.dt.float32
I32 = mybir.dt.int32
BF16 = mybir.dt.bfloat16
ALU = mybir.AluOpType
ACT = mybir.ActivationFunctionType
AX = mybir.AxisListType.X
RMAX = bass.bass_isa.ReduceOp.max

P = 128
LN_EPS = 1e-05
SEP_ID, PAD_ID = 13, 1
NEG = -1.0e30
MARGIN = 60.0


def tower_program(nc, seq, tok_w, pe_w, wq, wk, w_gat, att_src, att_dst, b_gat, ln_g, ln_b,
                  m0_w1, m0_b1, m0_w2, m0_b2, edges, rot, n1_g, n1_b, q_w, kv_w, n2_g, n2_b,
                  fc1_w, fc1_b, fc2_w, fc2_b, wg, bg, m1_w1, m1_b1, m1_w2, m1_b2, out):
    S, B = seq.shape
    V, D = tok_w.shape
    N = S * B
    T = N // P
    TB = B // P
    E0, H0 = m0_w1.shape[0], m0_w1.shape[2]
    E1, H1 = m1_w1.shape[0], m1_w1.shape[2]
    HF = fc1_w.shape[1]
    GH, GE = att_src.shape
    GC = GH * GE
    SC = GH + GC
    NEDGE = edges.shape[1]
    EC = NEDGE // P
    NH, NBK = rot.shape[2], 2 * rot.shape[3]
    M = NH * NBK
    AH = 8
    DH = D // AH
    G = 8
    GB = 16
    CH = B
    assert V == P and N % P == 0 and NEDGE % (2 * G * P) == 0 and D == 64 and N == 4096

    with ExitStack() as ctx:
        def sb(name, shape, dt=F32):
            return ctx.enter_context(nc.sbuf_tensor(name, shape, dt))

        sems = {}

        def sem(name):
            if name not in sems:
                sems[name] = ctx.enter_context(nc.semaphore(name))
            return sems[name]

        ident = sb("ident", [P, P])
        iota_free = sb("iota_free", [P, P])
        iota_part = sb("iota_part", [P, 1])
        ones = sb("ones", [P, P])
        zeros = sb("zeros", [P, 320])
        later = sb("later", [P, E1, E1])
        bucket_rank = sb("bucket_rank", [P, NBK])
        head_mask = sb("head_mask", [D, AH])
        row_mask = sb("row_mask", [P, 2, AH, DH])
        w_tok = sb("w_tok", [V, D])
        w_pe = sb("w_pe", [S, D])
        w_q, w_k = sb("w_q", [D, D]), sb("w_k", [D, D])
        w_g = sb("w_g", [D, 2 * D])
        w_gat_s = sb("w_gat_s", [D, GC])
        att_s, att_d = sb("att_s", [P, GC]), sb("att_d", [P, GC])
        bgat_s, lng_s, lnb_s = sb("bgat_s", [P, GC]), sb("lng_s", [P, GC]), sb("lnb_s", [P, GC])
        w_rot = sb("w_rot", [D, NH * NBK // 2])
        norm_s = sb("norm_s", [P, 4, D])
        w_qq, w_kv = sb("w_qq", [D, 2 * D]), sb("w_kv", [D, 2 * D])
        w_gate, b_gate = sb("w_gate", [D, E1]), sb("b_gate", [P, E1])
        w1_0, b1_0 = sb("w1_0", [P, E0, H0]), sb("b1_0", [P, E0])
        w2_0 = sb("w2_0", [P, E0, D])
        w1_f, b1_f = sb("w1_f", [P, HF]), sb("b1_f", [P, HF // P])
        w2_f = sb("w2_f", [P, HF // P, D])
        w1_1, b1_1 = sb("w1_1", [P, E1, H1]), sb("b1_1", [P, E1 * H1 // P])
        w2_1 = sb("w2_1", [P, E1 * H1 // P, D])
        NB2 = (E0 + 1 + E1) * D
        b2_all = sb("b2_all", [P, NB2])
        h = sb("h", [P, T, D])
        xn = sb("xn", [P, T, D])
        x5 = sb("x5", [P, T, D])
        xT_2 = sb("xT_2", [P, N])
        xT = xT_2[0:D, :]
        tmp = sb("tmp", [P, T, D])
        stat = sb("stat", [P, 8, T])
        flags = sb("flags", [P, 32])
        gate = sb("gate", [P, T, E1])
        pairs = sb("pairs", [P, T, E1, E1])
        pairs2 = sb("pairs2", [P, T, E1, E1])
        small = sb("small", [P, 8, T * GH])
        hg = sb("hg", [P, T, GC])
        src_rows = sb("src_rows", [P, T, SC])
        dst_rows = sb("dst_rows", [P, T, 2 * GH])
        pad_row = sb("pad_row", [1, 2 * GH])
        arena = sb("arena", [P, 3 * EC])
        key_a, key_b, key_c = (arena[:, i * EC:(i + 1) * EC] for i in range(3))
        e_idx = sb("e_idx", [P, 2, EC], I32)
        x_12, x_13 = (e_idx[:, i, :].bitcast(BF16) for i in range(2))
        dst_b = key_a.bitcast(BF16).rearrange("p (a c) -> p a c", a=2)
        hotb_lo = pairs[:, :, :, :].rearrange("p t e j -> p (t e j)").bitcast(BF16)\
            .rearrange("p (a l g) -> p a l g", a=2, l=P)
        hotb_hi = sb("hotb_hi", [P, 2, GB, T], BF16)
        iota_lo = sb("iota_lo", [P, P, GB], BF16)
        iota_hi = sb("iota_hi", [P, T], BF16)
        last_row = sb("last_row", [P, P])
        last = sb("last", [P, SC])
        cnt_b = sb("cnt_b", [P, T])
        tokc = sb("tokc", [P, T], I32)
        n_valid = sb("n_valid", [P, 2, 2])
        pool_pad = sb("pool_pad", [P, 3])
        n_cols = sb("n_cols", [P, 3], I32)
        idx_st = sb("idx_st", [P, 2, 2, G], I32)
        src_g = sb("src_g", [P, 2, G, SC])
        dst_g = sb("dst_g", [P, 2, G, 2 * GH])
        z_e = sb("z_e", [P, 2, 2, G, GH])
        msg = sb("msg", [P, 2, G, SC])
        dst_part = sb("dst_part", [P, 2, 2, G], I32)
        dst_partf = sb("dst_partf", [P, 2, 2, G])
        hot_hi = sb("hot_hi", [P, 2, G, T])
        hot_lo = sb("hot_lo", [P, 2, G, P])
        spread = sb("spread", [P, 2, G, T, SC])
        big = spread[:, :, :, :, :].rearrange("p a g t c -> p (a g t c)")
        onehot_tok = big[:, 0:N]
        seq_bc = big[:, N:2 * N].bitcast(I32)
        yst = sb("yst", [D, 2, P])
        prob = big[:, 0:1024].rearrange("p (a n) -> p a n", a=2)
        probT = big[:, 1024:2048].rearrange("p (a n) -> p a n", a=2)
        hid = big[:, 2048:4096].rearrange("p (a n) -> p a n", a=4)
        mx = sb("mx", [P, 2, 4])
        mout = sb("mout", [P, 2, TB * D])
        hot_b = big[:, 4096:4096 + T * M].rearrange("p (t h i) -> p t h i", t=T, h=NH)
        rotv = big[:, 5120:5120 + T * M].rearrange("p (t h i) -> p t h i", t=T, h=NH)
        hmax = big[:, 6144:6144 + T * NH].rearrange("p (t h) -> p t h", t=T)
        pooled = big[0:D, 6272:6272 + S * P].rearrange("p (s r m) -> p s r m", s=S, m=M)
        counts = big[:, 7296:7296 + S * M]
        kT = big[0:D, 7552:7552 + S * M]
        k_bd = big[0:D, 7808:7808 + S * AH * M].rearrange("p (s h m) -> p s h m", s=S, h=AH)
        v_bd = arena[:, 0:S * 2 * D].rearrange("p (s g c) -> p s g c", s=S, g=2)
        score = arena[:, 1024:1536].rearrange("p (a n) -> p a n", a=2)
        scoreT = arena[:, 1536:2048].rearrange("p (a n) -> p a n", a=2)
        head_st = sb("head_st", [P, 2, 3, AH])
        x5_flat, half_ar = x5[:, :, :].rearrange("p t c -> p (t c)"), arena[:, EC:3 * EC]

        def parts(flat, off, n):
            return flat[:, 3 * off // 2:3 * (off + n) // 2].bitcast(BF16).rearrange("p (a n) -> p a n", a=3)

        parts_0, parts_1 = parts(x5_flat, 0, E0 * H0), parts(half_ar, 0, E1 * H1)
        parts_f = parts(half_ar, E1 * H1, HF)
        b_parts, ones_b, b_early, b_rest = (
            flat[:, off:off + n // 2].bitcast(BF16) for flat, off, n in (
                (half_ar, 3 * (E1 * H1 + HF) // 2, NB2), (half_ar, 3 * (E1 * H1 + HF) // 2 + NB2 // 2, P),
                (x5_flat, 3 * E0 * H0 // 2, NB2), (x5_flat, (3 * E0 * H0 + NB2) // 2, NB2)))
        hot_any = iota_lo[:, :, :].rearrange("p l g -> p (l g)")

        tab_src = nc.dram_tensor("tab_src", [N, SC], F32, kind="Internal").ap()
        tab_dst = nc.dram_tensor("tab_dst", [N + 1, 2 * GH], F32, kind="Internal").ap()

        bank = [ctx.enter_context(nc.psum_tensor(f"bank{i}", [P, 512], F32)) for i in range(8)]

        UP = (0, 1, 4, 5)
        assert CH == B

        block = ctx.enter_context(nc.Block())

        def tiles(ap):
            return ap.rearrange("p (t c) -> p t c", c=D)

        @block.sync
        def _(sp):
            def load(dst, src, name, columns=False):
                sp.dma_start(dst, src, allow_slow_non_contiguous=columns).then_inc(sem(name), 16)

            load(tokc[:, :], seq.rearrange("s (q p) -> p (s q)", p=P), "tokens_in", True)
            load(seq_bc, seq.rearrange("s b -> (s b)").rearrange("(a n) -> a n", a=1).broadcast_to([P, N]), "tokens_in")
            load(w_tok[:, :], tok_w, "tokens_in")
            load(w_pe[:, :], pe_w[0:S, :], "tokens_in")
            load(e_idx[:, :, :], edges.rearrange("a (p c) -> p a c", p=P), "edges_in")
            load(w_q[:, :], wq, "attn_w_in")
            load(w_k[:, :], wk, "attn_w_in")
            load(w_gat_s[:, :], w_gat, "gat_w_in")
            for dst, src in ((att_s, att_src.rearrange("h e -> (h e)")), (att_d, att_dst.rearrange("h e -> (h e)")),
                             (bgat_s, b_gat), (lng_s, ln_g), (lnb_s, ln_b)):
                load(dst[:, :], src.rearrange("(a n) -> a n", a=1).broadcast_to([P, GC]), "gat_w_in")
            for half in (slice(0, D), slice(D, P)):
                load(w1_0[half, :, :], m0_w1.rearrange("e d h -> d e h"), "moe0_w_in")
            load(b1_0[:, :], m0_b1.rearrange("e h -> h e"), "moe0_w_in", True)
            load(w2_0[:, :, :], m0_w2.rearrange("e h d -> h e d"), "moe0_w_in")
            for p in (0, 32, 64):
                for off, src in ((0, m0_b2.rearrange("e d -> (e d)")), (E0 * D, fc2_b),
                                 ((E0 + 1) * D, m1_b2.rearrange("e d -> (e d)"))):
                    n = src.shape[0]
                    load(b2_all[p:p + 1, off:off + n], src.rearrange("(a n) -> a n", a=1), "b2_in")
            load(w_rot[:, :], rot.rearrange("a d h i -> (a d) (h i)"), "lsh_w_in")
            for i, src in enumerate((n1_g, n1_b, n2_g, n2_b)):
                load(norm_s[:, i, :], src.rearrange("(a n) -> a n", a=1).broadcast_to([P, D]), "lsh_w_in")
            load(w_qq[:, 0:D], q_w, "lsh_w_in")
            load(w_qq[:, D:2 * D], q_w, "lsh_w_in")
            load(w_kv[:, :], kv_w, "lsh_w_in")
            for half in (slice(0, D), slice(D, P)):
                load(w1_f[half, :], fc1_w, "fc_w_in")
            load(b1_f[:, :], fc1_b.rearrange("(k p) -> p k", p=P), "fc_w_in", True)
            load(w2_f[:, :, :], fc2_w.rearrange("(k p) d -> p k d", p=P), "fc_w_in")
            load(w_gate[:, :], wg, "moe1_w_in")
            load(b_gate[:, :], bg.rearrange("(a n) -> a n", a=1).broadcast_to([P, E1]), "moe1_w_in")
            for half in (slice(0, D), slice(D, P)):
                load(w1_1[half, :, :], m1_w1.rearrange("e d h -> d e h"), "moe1_w_in")
            load(b1_1[:, :], m1_b1.rearrange("e (k p) -> p (e k)", p=P), "moe1_w_in", True)
            load(w2_1[:, :, :], m1_w2.rearrange("e (k p) d -> p (e k) d", p=P), "moe1_w_in")
            sp.wait_ge(sem("node_rows_made"), 1)
            sp.dma_start(tab_src.rearrange("(t p) c -> p t c", p=P), src_rows[:, :, :]).then_inc(sem("tables_out"), 16)
            sp.dma_start(tab_dst[0:N, :].rearrange("(t p) c -> p t c", p=P), dst_rows[:, :, :])\
              .then_inc(sem("tables_out"), 16)
            sp.dma_start(tab_dst[N:N + 1, :], pad_row[:, :]).then_inc(sem("tables_out"), 16)
            sp.wait_ge(sem("h_final"), 1)
            sp.dma_start(out.rearrange("s (q p) d -> p (s q) d", p=P), h[:, :, :]).then_inc(sem("out_written"), 16)
            sp.wait_ge(sem("out_written"), 16)

        LOADS = {"tokens_in": 4, "attn_w_in": 2, "gat_w_in": 6, "b2_in": 9, "moe0_w_in": 4, "lsh_w_in": 8,
                 "fc_w_in": 4, "moe1_w_in": 6, "edges_in": 1}

        def loaded(eng, name):
            eng.wait_ge(sem(name), 16 * LOADS[name])

        ROUNDS = EC // (2 * G)
        FRONT = ROUNDS // 4
        assert 4 * GB == 8 * G and FRONT % 8 == 0

        def edge_rounds(eng, first, end, block, n, body):
            with eng.Fori(first // block, end // block) as o:
                with eng.If(o * (block * 2 * G) < n):
                    with eng.Fori(0, block) as k:
                        body(o * block + k)
                with eng.Else():
                    eng.nop()

        low, high = slice(0, D), slice(D, P)

        def split_input(eng, chained, name, x1_too=False):
            for k in range(N // CH):
                eng.wait_ge(sem(f"{name}_x1"), k + 1)
                x, x12, x13 = (v[high, k * CH:(k + 1) * CH] for v in (xT_2, x_12, x_13))
                if x1_too:
                    eng.tensor_copy(x_13[low, k * CH:(k + 1) * CH], xT[:, k * CH:(k + 1) * CH])
                chained(eng.tensor_tensor(x, x, x12, ALU.subtract))
                chained(eng.tensor_copy(x12, x))
                eng.tensor_tensor(x13, x, x12, ALU.subtract).then_inc(sem(f"{name}_split"), 1)

        @block.gpsimd
        def _(pool):
            made = sem("pool_consts")
            pool.memset(ident[:, :], 0.0).then_inc(made, 1)
            pool.memset(ones[:, :], 1.0).then_inc(made, 1)
            pool.memset(zeros[:, :], 0.0).then_inc(made, 1)
            pool.memset(later[:, :, :], 1.0).then_inc(made, 1)
            pool.memset(head_mask[:, :], 1.0).then_inc(made, 1)
            pool.memset(row_mask[:, :, :, :], 1.0).then_inc(made, 1)
            pool.memset(pad_row[:, :], 0.0).then_inc(made, 1)
            pool.iota(iota_free[:, :], [[1, P]], base=0, channel_multiplier=0,
                      allow_small_or_imprecise_dtypes=True).then_inc(made, 1)
            pool.iota(iota_part[:, :], [[0, 1]], base=0, channel_multiplier=1,
                      allow_small_or_imprecise_dtypes=True).then_inc(made, 1)
            pool.iota(bucket_rank[:, :], [[-1, NBK]], base=NBK, channel_multiplier=0,
                      allow_small_or_imprecise_dtypes=True).then_inc(made, 1)
            pool.iota(iota_lo[:, :, :], [[1, P], [0, GB]], base=0, channel_multiplier=0,
                      allow_small_or_imprecise_dtypes=True).then_inc(made, 1)
            pool.iota(iota_hi[:, :], [[1, T]], base=0, channel_multiplier=0,
                      allow_small_or_imprecise_dtypes=True).then_inc(made, 1)
            pool.memset(last_row[:, :], 1.0).then_inc(made, 1)
            pool.wait_ge(made, 13)
            pool.affine_select(out=ident[:, :], in_=ident[:, :], compare_op=ALU.not_equal, fill=1.0,
                               base=0, pattern=[[-1, P]], channel_multiplier=1).then_inc(made, 1)
            pool.affine_select(out=last_row[:, :], in_=last_row[:, :], compare_op=ALU.is_ge, fill=0.0,
                               base=1 - P, pattern=[[0, P]], channel_multiplier=1).then_inc(made, 1)
            pool.affine_select(out=later[:, :, :], in_=later[:, :, :], compare_op=ALU.is_gt, fill=0.0,
                               base=0, pattern=[[1, E1], [-1, E1]], channel_multiplier=0).then_inc(made, 1)
            pool.affine_select(out=head_mask[:, :], in_=head_mask[:, :], compare_op=ALU.is_ge, fill=0.0,
                               base=0, pattern=[[-DH, AH]], channel_multiplier=1).then_inc(made, 1)
            pool.affine_select(out=row_mask[:, :, :, :], in_=row_mask[:, :, :, :], compare_op=ALU.is_ge,
                               fill=0.0, base=0, pattern=[[P, 2], [-M, AH], [0, DH]],
                               channel_multiplier=1).then_inc(made, 1)
            pool.wait_ge(made, 18)
            pool.affine_select(out=head_mask[:, :], in_=head_mask[:, :], compare_op=ALU.is_gt, fill=0.0,
                               base=DH, pattern=[[DH, AH]], channel_multiplier=-1).then_inc(made, 1)
            pool.affine_select(out=row_mask[:, :, :, :], in_=row_mask[:, :, :, :], compare_op=ALU.is_gt,
                               fill=0.0, base=M, pattern=[[-P, 2], [M, AH], [0, DH]],
                               channel_multiplier=-1).then_inc(made, 1)
            pool.wait_ge(made, 20)
            pool.memset(pool_pad[:, :], 0.0).then_inc(made, 1)
            pool.wait_ge(made, 21)
            pool.memset(n_valid[:, :, :], 0.0).then_inc(sem("consts_made"), 1)

            step = sem("pool_steps")
            count = [0]

            def seq_(ins):
                count[0] += 1
                ins.then_inc(step, 1)
                pool.wait_ge(step, count[0])

            seq_(pool.memset(b_early, 0.0))
            loaded(pool, "b2_in")
            one = [slice(p, p + 1) for p in (0, 32, 64)]
            seq_(pool.tensor_copy(b_early[one[0]], b2_all[one[0], :]))
            for q in one[1:]:
                seq_(pool.tensor_copy(b_rest[q], b2_all[q, :]))
                seq_(pool.tensor_tensor(b2_all[q, :], b2_all[q, :], b_rest[q], ALU.subtract))
            seq_(pool.tensor_copy(b_early[one[1]], b2_all[one[1], :]))
            seq_(pool.tensor_copy(b_rest[one[2]], b2_all[one[2], :]))
            pool.tensor_tensor(b_early[one[2]], b2_all[one[2], :], b_rest[one[2]], ALU.subtract)\
                .then_inc(sem("b_parts_made"), 1)
            pool.wait_ge(sem("b_parts_made"), 1)

            pool.wait_ge(sem("rows_counted"), 1)
            pool.partition_all_reduce(n_valid[:, 1, :], n_valid[:, 0, :], P, RMAX).then_inc(sem("count_reduced"), 1)
            pool.wait_ge(sem("a_src_max_part"), 1)
            pool.partition_all_reduce(small[:, 4, 0:GH], small[:, 3, 0:GH], P, RMAX)\
                .then_inc(sem("a_src_max_all"), 1)

            pool.wait_ge(sem("tables_out"), 48)
            pool.wait_ge(sem("cols_known"), 1)
            n = pool.value_load(n_cols[0:1, 0:1], min_val=0, max_val=EC)
            def gather(i):
                with pool.If(i * (2 * G) < n):
                    for a in range(2):
                        pool.wait_ge(sem("gathered_used"), 2 * i + a + 1)
                        pool.tensor_copy(idx_st[:, a, :, :], e_idx[:, :, bass.ds(i * (2 * G) + a * G, G)])\
                            .then_inc(sem("indices_staged"), 1)
                        pool.wait_ge(sem("indices_staged"), 2 * i + a + 1)
                        pool.tensor_tensor(pool_pad[:, 0:1], pool_pad[:, 1:2], pool_pad[:, 1:2], ALU.add)
                        for j in range(G):
                            pool.indirect_dma_start(
                                out=src_g[:, a, j, :], out_offset=None, in_=tab_src,
                                in_offset=bass.IndirectOffsetOnAxis(ap=idx_st[:, a, 0, j:j + 1], axis=0))\
                                .then_inc(sem(f"gathered{a}"), 16)
                            pool.indirect_dma_start(
                                out=dst_g[:, a, j, :], out_offset=None, in_=tab_dst,
                                in_offset=bass.IndirectOffsetOnAxis(ap=idx_st[:, a, 1, j:j + 1], axis=0))\
                                .then_inc(sem(f"gathered{a}"), 16)
                with pool.Else():
                    pool.nop()

            edge_rounds(pool, 0, FRONT, 8, n, gather)
            edge_rounds(pool, FRONT, ROUNDS, FRONT, n, gather)
            seq_(pool.memset(pool_pad[:, 2:3], 0.0))
            split_input(pool, seq_, "moe0")
            split_input(pool, seq_, "moe1")

        @block.vector
        def _(dve):
            step = sem("dve_steps")
            count = [0]

            def seq_(ins):
                count[0] += 1
                ins.then_inc(step, 1)
                dve.wait_ge(step, count[0])

            def bc(ap, n):
                return ap.unsqueeze(2).broadcast_to([ap.shape[0], ap.shape[1], n])

            def rep(ap, n):
                return ap.unsqueeze(1).broadcast_to([ap.shape[0], n, ap.shape[1]])

            lns = [0]

            def layer_norm(dst, src, gb=None, width=D):
                lns[0] += 1
                t = src.shape[1]
                cen = tmp[:, 0:t, 0:width]
                seq_(dve.tensor_reduce(stat[:, 0, :], src, AX, ALU.add))
                seq_(dve.tensor_scalar(stat[:, 1, :], stat[:, 0, :], -1.0 / width, None, ALU.mult))
                halves = slice(0, t // 2), slice(t // 2, t)
                for q in halves:
                    dve.tensor_tensor(cen[:, q], src[:, q], bc(stat[:, 1, q], width), ALU.add)\
                       .then_inc(sem("ln_centred"), 1)
                for i, q in enumerate(halves):
                    dve.wait_ge(sem("ln_squared"), 2 * lns[0] - 1 + i)
                    ins = dve.tensor_reduce(stat[:, 2, q], dst[:, q], AX, ALU.add)
                seq_(ins)
                dve.tensor_scalar(stat[:, 3, :], stat[:, 2, :], 1.0 / width, LN_EPS, ALU.mult, ALU.add)\
                   .then_inc(sem("ln_var"), 1)
                dve.wait_ge(sem("ln_std"), lns[0])
                seq_(dve.reciprocal(stat[:, 5, :], stat[:, 4, :]))
                seq_(dve.tensor_tensor(dst, cen, bc(stat[:, 5, :], width), ALU.mult))
                if gb:
                    seq_(dve.tensor_tensor(dst, dst, rep(gb[0], t), ALU.mult))
                    seq_(dve.tensor_tensor(dst, dst, rep(gb[1], t), ALU.add))

            def top2(sc, E):
                a = sc.unsqueeze(3).broadcast_to([P, T, E, E])
                b = sc.unsqueeze(2).broadcast_to([P, T, E, E])
                gt, eq = pairs[:, :, 0:E, 0:E], pairs2[:, :, 0:E, 0:E]
                dve.tensor_tensor(gt, b, a, ALU.is_gt)
                seq_(dve.tensor_tensor(eq, b, a, ALU.is_equal))
                seq_(dve.tensor_tensor(eq, eq, later[:, 0:E, 0:E].unsqueeze(1).broadcast_to([P, T, E, E]), ALU.mult))
                seq_(dve.tensor_tensor(gt, gt, eq, ALU.add))
                rank, top = pairs2[:, :, 0, 0:E], stat[:, 0, :]
                seq_(dve.tensor_reduce(rank, gt, AX, ALU.add))
                seq_(dve.tensor_reduce(top, sc, AX, ALU.max))
                shifted = pairs2[:, :, 1, 0:E]
                dve.tensor_tensor(shifted, sc, bc(top, E), ALU.subtract).then_inc(sem("gate_shifted"), 1)
                gates[0] += 1
                dve.wait_ge(sem("gate_exp"), gates[0])
                ex = pairs[:, :, 0, 0:E]
                seq_(dve.tensor_scalar(rank, rank, 1.5, None, ALU.is_lt))
                seq_(dve.tensor_tensor(ex, ex, rank, ALU.mult))
                seq_(dve.tensor_reduce(stat[:, 1, :], ex, AX, ALU.add))
                seq_(dve.reciprocal(stat[:, 2, :], stat[:, 1, :]))
                seq_(dve.tensor_tensor(gate[:, :, 0:E], ex, bc(stat[:, 2, :], E), ALU.mult))

            gates = [0]

            SORT = [(size, m) for k in range(1, EC.bit_length()) for size in (1 << k,)
                    for m in (1 << j for j in reversed(range(k)))]

            def sort_stage(n):
                size, m = SORT[n]
                cur, nxt = (key_a, key_b) if n % 2 == 0 else (key_b, key_a)
                both = size < EC
                x, y = (v.rearrange("p (n r k u m) -> p n r k u m", r=2 if both else 1, u=2, m=m,
                                    k=size // (2 * m)) for v in (cur, nxt))
                for r in range(2 if both else 1):
                    lo, hi = x[:, :, r, :, 0, :], x[:, :, r, :, 1, :]
                    ops = (ALU.min, ALU.max) if r == 0 else (ALU.max, ALU.min)
                    dve.tensor_tensor(y[:, :, r, :, 0, :], lo, hi, ops[0])
                    ins = dve.tensor_tensor(y[:, :, r, :, 1, :], lo, hi, ops[1])
                seq_(ins)

            dve.wait_ge(sem("consts_made"), 1)
            loaded(dve, "tokens_in")
            EARLY, TURNING, LATE = 4, 4, 3
            LEFT = len(SORT) - EARLY - TURNING - LATE - T
            sorted_ = [0]

            def sort_stages(n):
                for _ in range(n):
                    sort_stage(sorted_[0])
                    sorted_[0] += 1

            tok, sep = small[:, 0, 0:T], small[:, 1, 0:T]
            pad, code = small[:, 2, 0:T], small[:, 3, 0:T]
            prev, npad = small[:, 4, 0:TB], small[:, 5, 0:TB]
            skip = small[:, 6, 0:TB]
            seq_(dve.tensor_copy(tok, tokc[:, :]))
            dve.tensor_scalar(sep, tok, float(SEP_ID), None, ALU.is_equal)
            dve.tensor_scalar(pad, tok, float(PAD_ID), None, ALU.is_equal)
            dve.memset(prev, 0.0)
            seq_(dve.memset(npad, 0.0))
            for s in range(S):
                q = slice(s * TB, (s + 1) * TB)
                seq_(dve.tensor_tensor(skip, prev, pad[:, q], ALU.mult))
                dve.scalar_tensor_tensor(out=code[:, q], in0=skip, scalar=100.0, in1=npad,
                                         op0=ALU.mult, op1=ALU.subtract)
                seq_(dve.tensor_tensor(prev, sep[:, q], skip, ALU.max))
                seq_(dve.tensor_tensor(npad, npad, skip, ALU.add))
                seq_(dve.tensor_scalar(code[:, q], code[:, q], float(s), None, ALU.add))
            onehot_pos = hg[:, :, 0:S]
            dve.tensor_tensor(onehot_pos, bc(code, S), rep(iota_free[:, 0:S], T), ALU.is_equal)\
               .then_inc(sem("onehot_pos_made"), 1)

            seq_(dve.tensor_copy(onehot_tok, seq_bc))
            dve.tensor_scalar(onehot_tok, onehot_tok, iota_part[:, 0:1], None, ALU.is_equal)\
               .then_inc(sem("onehot_tok_made"), 1)
            dve.tensor_scalar(w_tok[0:1, :], w_tok[0:1, :], 0.0, None, ALU.mult).then_inc(sem("w_tok_masked"), 1)
            loaded(dve, "edges_in")
            dve.tensor_scalar(key_b, e_idx[:, 0, :], float(N - 1), None, ALU.min)
            seq_(dve.tensor_scalar(key_c, e_idx[:, 1, :], float(N), None, ALU.min))
            seq_(dve.tensor_scalar(key_a, key_c, float(N), -float(N * N), ALU.mult, ALU.add))
            seq_(dve.tensor_tensor(key_a, key_a, key_b, ALU.add))
            dve.tensor_scalar(key_b, key_b, float(N - 1), None, ALU.is_equal)
            seq_(dve.tensor_tensor(e_idx[:, 0, :].bitcast(F32), key_c, key_a, ALU.subtract))
            seq_(dve.tensor_tensor(key_b, key_b, e_idx[:, 0, :].bitcast(F32), ALU.mult))
            dve.tensor_scalar(key_c, key_c, float(N), 2.0 * N, ALU.is_equal, ALU.mult)
            seq_(dve.tensor_tensor(key_a, key_a, key_b, ALU.add))
            seq_(dve.tensor_tensor(key_a, key_a, key_c, ALU.add))
            sort_stages(EARLY)
            for b in range(4):
                dve.wait_ge(sem("embedded"), b + 1)
                ins = dve.tensor_copy(h[:, 8 * b:8 * b + 8, :], tiles(bank[b][:, :]))
                seq_(ins)
            layer_norm(xn[:, :, :], h[:, :, :])
            dve.memset(flags[:, 1:2], 0.0).then_inc(sem("xn_ready"), 1)
            sort_stages(TURNING)
            def att_add(it):
                a = it % 2
                dve.wait_ge(sem("prob_ready"), it + 1)
                seq_(dve.reciprocal(mx[:, a, 3:4], mx[:, a, 2:3]))
                dve.wait_ge(sem("att_out"), it + 1)
                dve.scalar_tensor_tensor(out=h[:, it, :], in0=bank[4 + a][:, 0:D], scalar=mx[:, a, 3:4],
                                         in1=h[:, it, :], op0=ALU.mult, op1=ALU.add).then_inc(sem("att_added"), 1)

            for it in range(T):
                a = it % 2
                dve.wait_ge(sem("scores_ready"), it + 1)
                seq_(dve.tensor_reduce(mx[:, a, 0:1], bank[a][:, :], AX, ALU.max))
                dve.tensor_scalar(mx[:, a, 1:2], mx[:, a, 0:1], -float(D) ** -0.5, None, ALU.mult)\
                   .then_inc(sem("max_ready"), 1)
                sort_stages(1)
                if it >= 1:
                    att_add(it - 1)
                sort_stages((it + 1) * LEFT // T - it * LEFT // T)
            att_add(T - 1)
            dve.wait_ge(sem("att_added"), T)

            layer_norm(xn[:, :, :], h[:, :, :])
            dve.memset(flags[:, 2:3], 0.0).then_inc(sem("xn_ready"), 1)
            sort_stages(LATE)
            assert len(SORT) % 2 == 0 and sorted_[0] == len(SORT)
            dve.tensor_scalar(key_b, key_a, 0.0, None, ALU.is_lt)
            seq_(dve.tensor_scalar(key_c, key_a, float(N), None, ALU.is_lt))
            dve.tensor_reduce(n_valid[:, 0, 0:1], key_b, AX, ALU.add)
            dve.tensor_reduce(n_valid[:, 0, 1:2], key_c, AX, ALU.add).then_inc(sem("rows_counted"), 1)
            dve.wait_ge(sem("rows_counted"), 1)
            seq_(dve.tensor_scalar(e_idx[:, 0, :], key_a, float(N * N), float(N * N), ALU.add, ALU.min))
            dve.tensor_scalar(e_idx[:, 1, :], e_idx[:, 0, :], 12, None, ALU.logical_shift_right)
            seq_(dve.tensor_scalar(e_idx[:, 0, :], e_idx[:, 0, :], N - 1, None, ALU.bitwise_and))
            dve.wait_ge(sem("count_reduced"), 1)
            seq_(dve.tensor_scalar(n_valid[:, 0, 0:1], n_valid[:, 1, 1:2], 0.25, 0.75, ALU.mult, ALU.add))
            dve.tensor_tensor(n_cols[:, 2:3], n_valid[:, 0, 0:1], n_valid[:, 1, 0:1], ALU.max)
            dve.tensor_copy(n_cols[:, 0:2], n_valid[:, 1, :]).then_inc(sem("cols_known"), 1)

            loaded(dve, "gat_w_in")
            dve.wait_ge(sem("gat_h"), 1)
            seq_(dve.tensor_copy(hg[:, :, :].rearrange("p t c -> p (t c)"), bank[2][:, :]))
            a_src, a_dst, upper, self_e = (small[:, i, :] for i in range(4))
            shift, ee_self = small[:, 5, :], small[:, 6, :]
            prod = pairs[:, :, 0:GH, 0:GE]
            hg4 = hg[:, :, :].rearrange("p t (h e) -> p t h e", h=GH)
            for att, dst in ((att_s, a_src), (att_d, a_dst)):
                w = att[:, :].rearrange("p (h e) -> p h e", h=GH).unsqueeze(1).broadcast_to([P, T, GH, GE])
                seq_(dve.tensor_tensor(prod, hg4, w, ALU.mult))
                seq_(dve.tensor_reduce(dst.rearrange("p (t h) -> p t h", t=T), prod, AX, ALU.add))
            dve.tensor_reduce(small[:, 3, 0:GH], a_src.rearrange("p (t h) -> p h t", t=T), AX, ALU.max)\
               .then_inc(sem("a_src_max_part"), 1)
            dve.wait_ge(sem("a_src_max_all"), 1)
            seq_(dve.tensor_tensor(upper.rearrange("p (t h) -> p t h", t=T), a_dst.rearrange("p (t h) -> p t h", t=T),
                                   rep(small[:, 4, 0:GH], T), ALU.add))
            seq_(dve.tensor_tensor(self_e, a_src, a_dst, ALU.add))
            for x in (upper, self_e):
                seq_(dve.scalar_tensor_tensor(out=x, in0=x, scalar=0.2, in1=x, op0=ALU.mult, op1=ALU.max))
            seq_(dve.scalar_tensor_tensor(out=shift, in0=self_e, scalar=MARGIN, in1=upper,
                                          op0=ALU.add, op1=ALU.min))
            dve.tensor_tensor(upper, self_e, shift, ALU.subtract).then_inc(sem("self_shifted"), 1)
            dve.tensor_copy(src_rows[:, :, 0:GH], a_src.rearrange("p (t h) -> p t h", t=T))
            dve.tensor_copy(src_rows[:, :, GH:SC], hg[:, :, :])
            dve.tensor_copy(dst_rows[:, :, 0:GH], a_dst.rearrange("p (t h) -> p t h", t=T))
            dve.tensor_copy(dst_rows[:, :, GH:2 * GH], shift.rearrange("p (t h) -> p t h", t=T))\
               .then_inc(sem("dst_rows_made"), 1)
            dve.wait_ge(sem("dst_rows_made"), 1)
            dve.memset(flags[:, 3:4], 0.0).then_inc(sem("node_rows_made"), 1)
            dve.memset(flags[:, 4:5], 0.0).then_inc(sem("gathered_used"), 2)
            kb, kc = key_b.bitcast(I32), key_c.bitcast(I32)
            seq_(dve.tensor_scalar(key_b, key_a, 0.0, 2.0 * N * N, ALU.is_lt, ALU.mult))
            seq_(dve.tensor_tensor(key_a, key_a, key_b, ALU.add))
            seq_(dve.tensor_scalar(kb, key_a, float(N), None, ALU.min))
            dve.tensor_scalar(kc, kb, P - 1, None, ALU.bitwise_and)
            seq_(dve.tensor_scalar(kb, kb, 7, None, ALU.logical_shift_right))
            dve.tensor_copy(dst_b[:, 0, :], kc)
            seq_(dve.tensor_copy(dst_b[:, 1, :], kb))

            for w, p3, name in ((w1_0[:, :, :].rearrange("p e h -> p (e h)"), parts_0, "moe0"),
                                (w1_f[:, :], parts_f, "fc"),
                                (w1_1[:, :, :].rearrange("p e h -> p (e h)"), parts_1, "moe1")):
                loaded(dve, f"{name}_w_in")
                w11, w22, w31 = (p3[:, i, :] for i in range(3))
                seq_(dve.tensor_copy(w11, w))
                seq_(dve.tensor_tensor(w, w, w11, ALU.subtract))
                seq_(dve.tensor_copy(w22, w))
                dve.tensor_tensor(w31[low], w[low], w22[low], ALU.subtract)
                seq_(dve.tensor_copy(w31[high], w11[high]))
            dve.wait_ge(sem("b_parts_made"), 1)
            dve.tensor_copy(b_parts, b_early)
            dve.memset(ones_b, 1.0).then_inc(sem("parts_made"), 1)

            dve.wait_ge(sem("cols_known"), 1)
            n = dve.value_load(n_cols[0:1, 0:1], min_val=0, max_val=EC)
            nab = dve.value_load(n_cols[0:1, 1:2], min_val=0, max_val=EC)
            n_both = dve.value_load(n_cols[0:1, 2:3], min_val=0, max_val=EC)
            def edges_b(i):
                with dve.If(i * (4 * GB) < nab):
                    for k in range(4):
                        a, g = k % 2, 4 * i + k
                        dve.wait_ge(sem("hotb_free"), g + 1)
                        cols = bass.ds(i * (4 * GB) + k * GB, GB)
                        dve.tensor_tensor(hotb_lo[:, a, :, :],
                                          dst_b[:, 0, cols].unsqueeze(1).broadcast_to([P, P, GB]),
                                          iota_lo[:, :, :], ALU.is_equal).then_inc(sem("hotb_made"), 1)
                        dve.tensor_tensor(hotb_hi[:, a, :, :],
                                          dst_b[:, 1, cols].unsqueeze(2).broadcast_to([P, GB, T]),
                                          rep(iota_hi[:, :], GB), ALU.is_equal).then_inc(sem("hotb_made"), 1)
                with dve.Else():
                    dve.nop()

            def edges_a(i):
                with dve.If(i * (2 * G) < n):
                    for a in range(2):
                        g = 2 * i + a
                        cols = e_idx[:, 1, bass.ds(i * (2 * G) + a * G, G)]
                        dve.tensor_scalar(dst_part[:, a, 0, :], cols, P - 1, None, ALU.bitwise_and)\
                           .then_inc(sem("edge_step"), 1)
                        dve.tensor_scalar(dst_part[:, a, 1, :], cols, 7, None, ALU.logical_shift_right)\
                           .then_inc(sem("edge_step"), 1)
                        dve.wait_ge(sem("edge_step"), 7 * g + 2)
                        dve.tensor_copy(dst_partf[:, a, :, :], dst_part[:, a, :, :]).then_inc(sem("edge_step"), 1)
                        dve.wait_ge(sem("edge_step"), 7 * g + 3)
                        dve.wait_ge(sem("edge_bufs_free"), g + 1)
                        dve.tensor_tensor(hot_lo[:, a, :, :], bc(dst_partf[:, a, 0, :], P),
                                          rep(iota_free[:, :], G), ALU.is_equal)
                        dve.tensor_tensor(hot_hi[:, a, :, :], bc(dst_partf[:, a, 1, :], T),
                                          rep(iota_free[:, 0:T], G), ALU.is_equal).then_inc(sem("edge_step"), 1)
                        dve.wait_ge(sem(f"gathered{a}"), 32 * G * (i + 1))
                        dve.tensor_tensor(z_e[:, a, 0, :, :], src_g[:, a, :, 0:GH], dst_g[:, a, :, 0:GH],
                                          ALU.add).then_inc(sem("edge_step"), 1)
                        dve.wait_ge(sem("edge_step"), 7 * g + 5)
                        dve.scalar_tensor_tensor(out=z_e[:, a, 1, :, :], in0=z_e[:, a, 0, :, :], scalar=0.2,
                                                 in1=z_e[:, a, 0, :, :], op0=ALU.mult, op1=ALU.max)\
                           .then_inc(sem("edge_step"), 1)
                        dve.wait_ge(sem("edge_step"), 7 * g + 6)
                        dve.tensor_tensor(z_e[:, a, 0, :, :], z_e[:, a, 1, :, :], dst_g[:, a, :, GH:2 * GH],
                                          ALU.subtract).then_inc(sem("edge_scores"), 1)
                        dve.wait_ge(sem("edge_exp"), g + 1)
                        dve.tensor_tensor(
                            msg[:, a, :, GH:SC].rearrange("p g (h e) -> p g h e", h=GH),
                            src_g[:, a, :, GH:SC].rearrange("p g (h e) -> p g h e", h=GH),
                            msg[:, a, :, 0:GH].unsqueeze(3).broadcast_to([P, G, GH, GE]), ALU.mult)\
                           .then_inc(sem("edge_step"), 1)
                        dve.wait_ge(sem("edge_step"), 7 * g + 7)
                        dve.tensor_tensor(
                            spread[:, a, :, :, :],
                            hot_hi[:, a, :, :].unsqueeze(3).broadcast_to([P, G, T, SC]),
                            msg[:, a, :, :].unsqueeze(2).broadcast_to([P, G, T, SC]), ALU.mult)\
                           .then_inc(sem("edges_spread"), 1)
                        dve.wait_ge(sem("edges_spread"), g + 1)
                        dve.memset(flags[:, 5:6], 0.0).then_inc(sem("gathered_used"), 1)
                with dve.Else():
                    dve.nop()

            def edges_both(i):
                edges_b(i)
                edges_a(i)

            edge_rounds(dve, 0, FRONT, 8, n_both, edges_both)
            edge_rounds(dve, FRONT, ROUNDS, FRONT, n, edges_a)

            den, agg = small[:, 0, :], hg
            dve.wait_ge(sem("edges_summed"), 1)
            dve.wait_ge(sem("self_exp"), 1)
            z_b = small[:, 4, :].rearrange("p (t h) -> p t h", t=T)
            dve.tensor_copy(cnt_b[:, :], bank[6][:, 0:T])
            seq_(dve.tensor_copy(last[:, :], bank[7][:, 0:SC]))
            seq_(dve.tensor_tensor(z_b, dst_rows[:, :, 0:GH], rep(last[:, 0:GH], T), ALU.add))
            seq_(dve.scalar_tensor_tensor(out=z_b, in0=z_b, scalar=0.2, in1=z_b, op0=ALU.mult, op1=ALU.max))
            dve.tensor_tensor(z_b, z_b, dst_rows[:, :, GH:2 * GH], ALU.subtract).then_inc(sem("b_shifted"), 1)
            dve.wait_ge(sem("b_exp"), 1)
            seq_(dve.tensor_tensor(z_b, z_b, bc(cnt_b[:, :], GH), ALU.mult))
            dve.wait_ge(sem("tables_out"), 48)
            msg_b = src_rows[:, :, GH:SC].rearrange("p t (h e) -> p t h e", h=GH)
            lh = last[:, GH:SC].rearrange("p (h e) -> p h e", h=GH).unsqueeze(1).broadcast_to([P, T, GH, GE])
            seq_(dve.tensor_tensor(msg_b, lh, z_b.unsqueeze(3).broadcast_to([P, T, GH, GE]), ALU.mult))
            sums = [bank[4 + i][:, 0:T // 2 * SC].rearrange("p (t c) -> p t c", c=SC) for i in range(2)]
            ee3 = ee_self.rearrange("p (t h) -> p t h", t=T)
            seq_(dve.tensor_tensor(hg4, hg4, ee3.unsqueeze(3).broadcast_to([P, T, GH, GE]), ALU.mult))
            seq_(dve.tensor_tensor(agg[:, :, :], agg[:, :, :], src_rows[:, :, GH:SC], ALU.add))
            for i in range(2):
                q = slice(i * T // 2, (i + 1) * T // 2)
                dve.tensor_tensor(agg[:, q, :], agg[:, q, :], sums[i][:, :, GH:SC], ALU.add)
                seq_(dve.tensor_tensor(den.rearrange("p (t h) -> p t h", t=T)[:, q, :], ee3[:, q, :],
                                       sums[i][:, :, 0:GH], ALU.add))
            dve.tensor_tensor(den, den, small[:, 4, :], ALU.add).then_inc(sem("sums_taken"), 1)
            dve.wait_ge(sem("sums_taken"), 1)
            seq_(dve.scalar_tensor_tensor(out=den, in0=ee_self, scalar=1e-16, in1=den, op0=ALU.mult, op1=ALU.add))
            seq_(dve.reciprocal(small[:, 1, :], den))
            seq_(dve.tensor_tensor(hg4, hg4, small[:, 1, :].rearrange("p (t h) -> p t h", t=T).unsqueeze(3)
                                   .broadcast_to([P, T, GH, GE]), ALU.mult))
            seq_(dve.tensor_tensor(src_rows[:, :, 0:GC], agg[:, :, :], rep(bgat_s[:, :], T), ALU.add))
            layer_norm(hg[:, :, :], src_rows[:, :, 0:GC], (lng_s[:, :], lnb_s[:, :]), GC)
            score4 = small[:, 2, :].rearrange("p (t e) -> p t e", t=T)
            seq_(dve.tensor_reduce(score4, hg[:, :, :].rearrange("p t (h e) -> p t e h", h=GH), AX, ALU.add))
            seq_(dve.tensor_scalar(small[:, 2, :], small[:, 2, :], 1.0 / GH, None, ALU.mult))
            top2(score4, GE)

            mlps = [24]

            def mlp_sum(acc, n_steps, gated, name):
                mlps[0] += 1
                free = min(2, n_steps)
                dve.memset(flags[:, mlps[0]:mlps[0] + 1], 0.0).then_inc(sem(f"{name}_taken"), free)
                with dve.Fori(0, N // CH) as c:
                    for e in range(n_steps):
                        k = c * n_steps + e
                        dve.wait_ge(sem(f"{name}_out"), k + 1)
                        dst = acc[:, bass.ds(c * TB, TB), :]
                        a = e % 2
                        part = bank[2 + a][:, 0:TB * D].rearrange("p (t c) -> p t c", c=D)
                        if not gated:
                            dve.tensor_tensor(dst, dst, part, ALU.add).then_inc(sem(f"{name}_taken"), 1)
                            continue
                        mo = mout[:, a, :].rearrange("p (t c) -> p t c", c=D)
                        g_ = gate[:, bass.ds(c * TB, TB), e:e + 1].broadcast_to([P, TB, D])
                        dve.tensor_tensor(mo, part, g_, ALU.mult).then_inc(sem(f"{name}_taken"), 1)
                        dve.wait_ge(sem(f"{name}_taken"), k + 1 + free)
                        if e:
                            dve.wait_ge(sem(f"{name}_added"), k)
                        dve.tensor_tensor(dst, dst, mo, ALU.add).then_inc(sem(f"{name}_added"), 1)
                if gated:
                    dve.wait_ge(sem(f"{name}_added"), n_steps * (N // CH))
                else:
                    dve.wait_ge(sem(f"{name}_taken"), n_steps * (N // CH) + free)

            mlp_sum(h, E0, True, "moe0")

            layer_norm(xn[:, :, :], h[:, :, :])
            loaded(dve, "lsh_w_in")
            layer_norm(x5[:, :, :], xn[:, :, :], (norm_s[:, 0, :], norm_s[:, 1, :]))
            dve.memset(flags[:, 7:8], 0.0).then_inc(sem("x_ready"), 1)
            dve.wait_ge(sem("rotated"), 1)
            rp = bank[2][:, :].rearrange("p (t h i) -> p t h i", t=T, h=NH)
            for t in range(0, T, T // 2):
                q = slice(t, t + T // 2)
                dve.tensor_copy(rotv[:, q, :, 0:NBK // 2], rp[:, q])
                dve.tensor_scalar(rotv[:, q, :, NBK // 2:NBK], rp[:, q], -1.0, None, ALU.mult)\
                   .then_inc(sem("rot_copied"), 1)
            dve.wait_ge(sem("rot_copied"), 2)
            hm = hmax.rearrange("p t h -> p (t h)")
            rot2, hot2 = (x.rearrange("p t h i -> p (t h) i") for x in (rotv, hot_b))
            seq_(dve.tensor_reduce(hm, rot2, AX, ALU.max))
            seq_(dve.tensor_tensor(hot2, rot2, bc(hm, NBK), ALU.is_equal))
            seq_(dve.tensor_tensor(hot2, hot2, rep(bucket_rank[:, :], T * NH), ALU.mult))
            seq_(dve.tensor_reduce(hm, hot2, AX, ALU.max))
            seq_(dve.tensor_tensor(hot2, rep(bucket_rank[:, :], T * NH), bc(hm, NBK), ALU.is_equal))
            dve.memset(flags[:, 8:9], 0.0).then_inc(sem("buckets_made"), 1)
            dve.wait_ge(sem("pooled_psum"), 1)
            seq_(dve.tensor_scalar(counts, bank[3][:, 0:S * M], 1e-20, None, ALU.add))
            seq_(dve.reciprocal(kT, counts[0:D, :]))
            dve.tensor_tensor(pooled, *(x.rearrange("p (s m) -> p s m", s=S).unsqueeze(2)
                                        .broadcast_to([D, S, P // M, M]) for x in (bank[2][0:D, 0:S * M], kT)),
                              ALU.mult).then_inc(sem("pooled_made"), 1)
            seq_(dve.tensor_scalar(counts, counts, 0.5, NEG, ALU.is_lt, ALU.mult))
            dve.wait_ge(sem("kv_psum"), 1)
            seq_(dve.tensor_copy(kT, bank[3][0:D, 0:S * M]))
            for s in range(S):
                dve.tensor_tensor(k_bd[:, s], kT[:, s * M:(s + 1) * M].unsqueeze(1).broadcast_to([D, AH, M]),
                                  bc(head_mask[:, :], M), ALU.mult)
                dve.tensor_tensor(v_bd[:, s], bank[2][:, s * D:(s + 1) * D].unsqueeze(1).broadcast_to([P, 2, D]),
                                  row_mask[:, :, :, :].rearrange("p g h d -> p g (h d)"), ALU.mult)\
                   .then_inc(sem("kv_made"), 1)
            dve.wait_ge(sem("kv_made"), S)
            dve.memset(flags[:, 9:10], 0.0).then_inc(sem("kv_ready"), 1)
            def lsh_shift(it, a, b):
                s3 = score[:, a, :].rearrange("p (h m) -> p h m", h=AH)
                dve.wait_ge(sem("lsh_scores"), it + 1)
                dve.tensor_tensor(s3, bank[a][:, 0:AH * M].rearrange("p (h m) -> p h m", h=AH),
                                  counts[:, bass.ds(b * M, M)].unsqueeze(1).broadcast_to([P, AH, M]), ALU.add)\
                   .then_inc(sem("lsh_shift_step"), 1)
                dve.wait_ge(sem("lsh_shift_step"), 2 * it + 1)
                dve.tensor_reduce(head_st[:, a, 0, :], s3, AX, ALU.max).then_inc(sem("lsh_shift_step"), 1)
                dve.wait_ge(sem("lsh_shift_step"), 2 * it + 2)
                dve.tensor_tensor(s3, s3, bc(head_st[:, a, 0, :], M), ALU.subtract).then_inc(sem("lsh_shifted"), 1)

            def lsh_add(it, a):
                s3 = score[:, a, :].rearrange("p (h m) -> p h m", h=AH)
                step3 = sem("lsh_add_step")
                dve.wait_ge(sem("lsh_exp"), it + 1)
                dve.tensor_reduce(head_st[:, a, 1, :], s3, AX, ALU.add).then_inc(step3, 1)
                dve.wait_ge(step3, 3 * it + 1)
                dve.reciprocal(head_st[:, a, 2, :], head_st[:, a, 1, :]).then_inc(step3, 1)
                dve.wait_ge(step3, 3 * it + 2)
                dve.wait_ge(sem("lsh_att"), it + 1)
                o3 = mout[:, a, 0:D].rearrange("p (h d) -> p h d", h=AH)
                dve.tensor_tensor(o3, bank[4 + a][:, 0:D].rearrange("p (h d) -> p h d", h=AH),
                                  bc(head_st[:, a, 2, :], DH), ALU.mult).then_inc(step3, 1)
                dve.wait_ge(step3, 3 * it + 3)
                row = xn[:, bass.ds(it, 1), :].rearrange("p t c -> p (t c)")
                dve.tensor_tensor(row, row, mout[:, a, 0:D], ALU.add).then_inc(sem("lsh_added"), 1)

            def lsh_batch(b, start=False):
                for q in range(TB):
                    it = TB * b + q
                    lsh_shift(it, q % 2, b)
                    if not (start and q == 0):
                        lsh_add(it - 1, 1 - q % 2)

            lsh_batch(0, start=True)
            with dve.Fori(1, S) as b:
                lsh_batch(b)
            lsh_add(T - 1, 1)
            dve.wait_ge(sem("lsh_added"), T)
            layer_norm(x5[:, :, :], xn[:, :, :], (norm_s[:, 2, :], norm_s[:, 3, :]))
            dve.memset(flags[:, 10:11], 0.0).then_inc(sem("x_ready"), 1)
            split_input(dve, seq_, "fc", x1_too=True)
            mlp_sum(xn, 1, False, "fc")
            seq_(dve.tensor_tensor(h[:, :, :], h[:, :, :], xn[:, :, :], ALU.add))
            layer_norm(xn[:, :, :], h[:, :, :])
            dve.memset(flags[:, 11:12], 0.0).then_inc(sem("xn_ready"), 1)
            dve.wait_ge(sem("gate_logits"), 1)
            lg = tmp[:, :, 0:E1]
            seq_(dve.tensor_tensor(lg, bank[2][:, 0:T * E1].rearrange("p (t e) -> p t e", t=T),
                                   rep(b_gate[:, :], T), ALU.add))
            top2(lg, E1)
            mlp_sum(h, E1, True, "moe1")
            dve.memset(flags[:, 12:13], 0.0).then_inc(sem("h_final"), 1)

        @block.scalar
        def _(act):
            lns = [0]

            def layer_norm(dst, width=D):
                lns[0] += 1
                for i, q in enumerate((slice(0, T // 2), slice(T // 2, T))):
                    act.wait_ge(sem("ln_centred"), 2 * lns[0] - 1 + i)
                    act.activation(dst[:, q], tmp[:, q, 0:width], ACT.Square).then_inc(sem("ln_squared"), 1)
                act.wait_ge(sem("ln_var"), lns[0])
                act.activation(stat[:, 4, :], stat[:, 3, :], ACT.Sqrt).then_inc(sem("ln_std"), 1)

            turned = [0]

            def turn(twice=True):
                for k in range(N // 512):
                    turned[0] += 1
                    act.wait_ge(sem("turned_psum"), turned[0])
                    cols = slice(k * 512, (k + 1) * 512)
                    if twice:
                        act.activation(xT_2[D:P, cols], bank[k % 2][0:D, :], ACT.Copy)
                    act.activation(xT[:, cols], bank[k % 2][0:D, :], ACT.Copy)\
                       .then_inc(sem("turned"), 1)

            def split_x1(first, name, once_more=True):
                for k in range(N // CH):
                    cols = slice(k * CH, (k + 1) * CH)
                    act.wait_ge(sem("turned"), first + k + 1)
                    if once_more:
                        act.activation(x_13[low, cols], xT[:, cols], ACT.Copy)
                    act.activation(x_12[:, cols], xT_2[:, cols], ACT.Copy).then_inc(sem(f"{name}_x1"), 1)

            gates = [0]

            def top2(E):
                gates[0] += 1
                act.wait_ge(sem("gate_shifted"), gates[0])
                act.activation(pairs[:, :, 0, 0:E], pairs2[:, :, 1, 0:E], ACT.Exp).then_inc(sem("gate_exp"), 1)

            for k in range(N // 512):
                act.wait_ge(sem("pos_psum"), k + 1)
                act.activation(xT[0:S, k * 512:(k + 1) * 512], bank[4 + k % 2][0:S, :], ACT.Copy)\
                   .then_inc(sem("pos_turned"), 1)
            act.wait_ge(sem("g_psum"), 1)
            act.activation(w_g[:, :], bank[6][0:D, 0:2 * D], ACT.Copy).then_inc(sem("g_ready"), 1)
            layer_norm(xn[:, :, :])
            turn(False)
            def y_copy(it, a):
                act.wait_ge(sem("y_psum"), it + 1)
                act.activation(yst[:, a, :], bank[6 + a][0:D, 0:P], ACT.Copy).then_inc(sem("y_ready"), 1)

            y_copy(0, 0)
            with act.Fori(0, S) as b:
                for q in range(TB):
                    a = q % 2
                    it = TB * b + q
                    y_copy(it + 1, 1 - a)
                    act.wait_ge(sem("max_ready"), it + 1)
                    act.activation(prob[:, a, :], bank[a][:, :], ACT.Exp, bias=mx[:, a, 1:2],
                                   scale=float(D) ** -0.5, accum_out=mx[:, a, 2:3]).then_inc(sem("prob_ready"), 1)
                    act.wait_ge(sem("probT_psum"), it + 1)
                    act.activation(probT[:, a, :], bank[2 + a][:, :], ACT.Copy).then_inc(sem("probT_ready"), 1)
            layer_norm(xn[:, :, :])
            turn()
            act.wait_ge(sem("self_shifted"), 1)
            act.activation(small[:, 6, :], small[:, 2, :], ACT.Exp).then_inc(sem("self_exp"), 1)
            act.wait_ge(sem("cols_known"), 1)
            n = act.value_load(n_cols[0:1, 0:1], min_val=0, max_val=EC)
            def edge_exp(i):
                with act.If(i * (2 * G) < n):
                    for a in range(2):
                        g = 2 * i + a
                        act.wait_ge(sem("edge_scores"), g + 1)
                        act.activation(msg[:, a, :, 0:GH], z_e[:, a, 0, :, :], ACT.Exp).then_inc(sem("edge_exp"), 1)
                with act.Else():
                    act.nop()

            edge_rounds(act, 0, FRONT, 8, n, edge_exp)
            edge_rounds(act, FRONT, ROUNDS, FRONT, n, edge_exp)
            act.wait_ge(sem("edges_summed"), 1)
            act.wait_ge(sem("b_shifted"), 1)
            act.activation(small[:, 4, :], small[:, 4, :], ACT.Exp).then_inc(sem("b_exp"), 1)
            split_x1(N // CH, "moe0")
            layer_norm(hg[:, :, :], GC)
            top2(GE)

            def mlp(b1, n_steps, HB, name):
                with act.Fori(0, N // CH) as c:
                    for e in range(n_steps * HB):
                        k = c * (n_steps * HB) + e
                        act.wait_ge(sem(f"{name}_hid_psum"), k + 1)
                        act.activation(hid[:, e % 4, :], bank[UP[e % 4]][:, :], ACT.Gelu, bias=b1[:, e:e + 1])\
                           .then_inc(sem(f"{name}_hid"), 1)

            loaded(act, "moe0_w_in")
            mlp(b1_0, E0, H0 // P, "moe0")
            layer_norm(xn[:, :, :])
            layer_norm(x5[:, :, :])
            turn(False)
            act.wait_ge(sem("kv_ready"), 1)
            def lq_copy(it, a):
                act.wait_ge(sem("lq_psum"), it + 1)
                act.activation(yst[:, a, :], bank[6 + a][0:D, 0:P], ACT.Copy).then_inc(sem("lq_ready"), 1)

            lq_copy(0, 0)
            with act.Fori(0, S) as b:
                for q in range(TB):
                    a = q % 2
                    it = TB * b + q
                    lq_copy(it + 1, 1 - a)
                    act.wait_ge(sem("lsh_shifted"), it + 1)
                    act.activation(score[:, a, :], score[:, a, :], ACT.Exp, scale=float(DH) ** -0.5)\
                       .then_inc(sem("lsh_exp"), 1)
                    act.wait_ge(sem("lshT_psum"), it + 1)
                    act.activation(scoreT[:, a, :], bank[2 + a][:, 0:2 * P], ACT.Copy).then_inc(sem("lshT"), 1)
            layer_norm(x5[:, :, :])
            turn()
            split_x1(3 * (N // CH), "fc", once_more=False)
            loaded(act, "fc_w_in")
            mlp(b1_f, 1, HF // P, "fc")
            layer_norm(xn[:, :, :])
            turn()
            split_x1(4 * (N // CH), "moe1")
            top2(E1)
            loaded(act, "moe1_w_in")
            mlp(b1_1, E1, H1 // P, "moe1")

        @block.tensor
        def _(pe):
            def mm(o, l, r, start=True, stop=True):
                return pe.matmul(o, l, r, start=start, stop=stop)

            turned = [0]

            def turn(src, product=None):
                for k in range(N // 512):
                    if k >= 2:
                        pe.wait_ge(sem("turned"), turned[0] - 1)
                    for j in range(4):
                        ins = pe.transpose(bank[k % 2][0:D, j * P:(j + 1) * P], src[:, 4 * k + j, :], ident[:, :])
                    ins.then_inc(sem("turned_psum"), 1)
                    turned[0] += 1
                    if product and k >= 2:
                        for t in range(4 * k - 8, 4 * k - 4):
                            product(t)
                pe.wait_ge(sem("turned"), turned[0])
                if product:
                    for t in range(T - 8, T):
                        ins = product(t)
                return ins

            pe.wait_ge(sem("consts_made"), 1)
            pe.wait_ge(sem("onehot_pos_made"), 1)
            for k in range(N // 512):
                if k >= 2:
                    pe.wait_ge(sem("pos_turned"), k - 1)
                for j in range(4):
                    ins = pe.transpose(bank[4 + k % 2][0:S, j * P:(j + 1) * P], hg[:, 4 * k + j, 0:S], ident[:, :])
                ins.then_inc(sem("pos_psum"), 1)
            loaded(pe, "attn_w_in")
            mm(bank[6][0:D, 0:D], w_q[:, :], w_k[:, :])
            mm(bank[6][0:D, D:2 * D], w_q[:, :], w_k[:, :]).then_inc(sem("g_psum"), 1)
            pe.wait_ge(sem("onehot_tok_made"), 1)
            pe.wait_ge(sem("w_tok_masked"), 1)
            loaded(pe, "tokens_in")
            pe.wait_ge(sem("pos_turned"), N // 512)
            for t in range(T):
                o = bank[t // 8][:, t % 8 * D:(t % 8 + 1) * D]
                mm(o, onehot_tok[:, t * P:(t + 1) * P], w_tok[:, :], True, False)
                ins = mm(o, xT[0:S, t * P:(t + 1) * P], w_pe[:, :], False, True)
                if t % 8 == 7:
                    ins.then_inc(sem("embedded"), 1)
            pe.wait_ge(sem("xn_ready"), 1)
            turn(xn)
            pe.wait_ge(sem("g_ready"), 1)
            def att_y(it, a, col):
                mm(bank[6 + a][:, 0:P], w_g[:, :], xT[:, col]).then_inc(sem("y_psum"), 1)

            def att_scores(it, a, cols):
                pe.wait_ge(sem("y_ready"), it + 1)
                mm(bank[a][:, 0:1], yst[:, a, :], zeros[0:D, 0:1])
                mm(bank[a][:, :], yst[:, a, :], xT[:, cols]).then_inc(sem("scores_ready"), 1)

            def att_turn(it, a):
                pe.wait_ge(sem("prob_ready"), it + 1)
                for j in range(TB):
                    ins = pe.transpose(bank[2 + a][:, j * P:(j + 1) * P], prob[:, a, j * P:(j + 1) * P], ident[:, :])
                ins.then_inc(sem("probT_psum"), 1)

            def att_out(it, a, tile0, first=False):
                pe.wait_ge(sem("probT_ready"), it + 1)
                if not first:
                    pe.wait_ge(sem("att_added"), it - 1)
                for j in range(TB):
                    row = xn[:, bass.ds(tile0 + j, 1), :].rearrange("p t c -> p (t c)")
                    ins = mm(bank[4 + a][:, 0:D], probT[:, a, j * P:(j + 1) * P], row, j == 0, j == TB - 1)
                ins.then_inc(sem("att_out"), 1)

            def att_batch(b, start=False, end=False):
                for q in range(TB):
                    a, it = q % 2, TB * b + q
                    more = not (end and q == TB - 1)
                    nb = b + (1 if q == TB - 1 else 0)
                    att_y(it + 1, 1 - a, bass.ds((b * B + (q + 1) * P) if more else b * B, P))
                    if not (start and q == 0):
                        att_out(it - 1, 1 - a, (b if q else b - 1) * TB, start and q <= 2)
                    if more:
                        att_scores(it + 1, 1 - a, bass.ds(nb * B, B))
                    att_turn(it, a)

            att_y(0, 0, bass.ds(0, P))
            att_scores(0, 0, bass.ds(0, B))
            att_batch(0, start=True)
            with pe.Fori(1, S - 1) as b:
                att_batch(b)
            att_batch(S - 1, end=True)
            att_out(T - 1, 1, (S - 1) * TB)
            pe.wait_ge(sem("xn_ready"), 2)
            loaded(pe, "gat_w_in")
            pe.wait_ge(sem("att_added"), T)
            turn(xn, lambda t: mm(bank[2][:, t * GC:(t + 1) * GC], xT[:, t * P:(t + 1) * P], w_gat_s[:, :]))\
                .then_inc(sem("gat_h"), 1)
            half = T // 2 * SC
            pe.wait_ge(sem("att_added"), T)
            for i in range(2):
                ins = pe.matmul(bank[4 + i][:, 0:half], ones[:, :], zeros[:, 0:half], start=True, stop=False,
                                skip_group_check=True)
            ins.then_inc(sem("edge_bufs_free"), 2)
            pe.matmul(bank[6][:, 0:T], ones[:, :], zeros[:, 0:T], start=True, stop=False,
                      skip_group_check=True).then_inc(sem("hotb_free"), 2)
            pe.wait_ge(sem("node_rows_made"), 1)
            mm(bank[7][:, 0:SC], last_row[:, :], src_rows[:, T - 1, :])
            pe.wait_ge(sem("cols_known"), 1)
            n = pe.value_load(n_cols[0:1, 0:1], min_val=0, max_val=EC)
            nab = pe.value_load(n_cols[0:1, 1:2], min_val=0, max_val=EC)
            n_both = pe.value_load(n_cols[0:1, 2:3], min_val=0, max_val=EC)
            def edges_b(i):
                with pe.If(i * (4 * GB) < nab):
                    for k in range(4):
                        pe.wait_ge(sem("hotb_made"), 2 * (4 * i + k + 1))
                        for j in range(GB):
                            ins = pe.matmul(bank[6][:, 0:T], hotb_lo[:, k % 2, :, j], hotb_hi[:, k % 2, j, :],
                                            start=False, stop=False, skip_group_check=True)
                        ins.then_inc(sem("hotb_free"), 1)
                with pe.Else():
                    pe.nop()

            def edges_a(i):
                with pe.If(i * (2 * G) < n):
                    for a in range(2):
                        pe.wait_ge(sem("edges_spread"), 2 * i + a + 1)
                        for j in range(G):
                            for k in range(2):
                                rhs = spread[:, a, j, k * T // 2:(k + 1) * T // 2, :].rearrange("p t c -> p (t c)")
                                ins = pe.matmul(bank[4 + k][:, 0:half], hot_lo[:, a, j, :], rhs, start=False,
                                                stop=False, skip_group_check=True)
                        ins.then_inc(sem("edge_bufs_free"), 1)
                with pe.Else():
                    pe.nop()

            def edges_both(i):
                edges_b(i)
                edges_a(i)

            edge_rounds(pe, 0, FRONT, 8, n_both, edges_both)
            edge_rounds(pe, FRONT, ROUNDS, FRONT, n, edges_a)
            for i in range(2):
                ins = pe.matmul(bank[4 + i][:, 0:half], ones[:, :], zeros[:, 0:half], start=False, stop=True,
                                skip_group_check=True)
            pe.matmul(bank[6][:, 0:T], ones[:, :], zeros[:, 0:T], start=False, stop=True,
                      skip_group_check=True).then_inc(sem("edges_summed"), 1)

            def warm_up(n):
                for i in range(n):
                    mm(bank[7][:, :], hot_any[:, 0:P], hot_any[:, 0:512])

            def mlp(w1, w2, b2, n_steps, HB, name):
                nb = n_steps * HB
                R = min(len(UP), nb)
                lead = R // 2

                def up(e, cols):
                    for i, x in enumerate((x_12, x_12, x_13)):
                        ins = mm(bank[UP[e % 4]][:, :], w1[:, i, e * P:(e + 1) * P], x[:, cols], i == 0, i == 2)
                    ins.then_inc(sem(f"{name}_hid_psum"), 1)

                def chunk(c, final=False):
                    for s in range(nb):
                        e, k = divmod(s, HB)
                        if s + lead < nb:
                            up(s + lead, bass.ds(c * CH, CH))
                        elif not final:
                            if s + lead == nb:
                                pe.wait_ge(sem(f"{name}_split"), c + 2)
                                mm(bank[UP[0]][:, 0:1], zeros[:, 0:P], zeros[:, 0:1])
                            up(s + lead - nb, bass.ds(c * CH + CH, CH))
                        o = bank[2 + e % 2]
                        if k == 0:
                            pe.wait_ge(sem(f"{name}_taken"), c * n_steps + e + 1)
                            pe.matmul(o[:, 0:TB * D].rearrange("p (t d) -> p t d", d=D), ones_b,
                                      b2[:, e * D:(e + 1) * D].unsqueeze(1).broadcast_to([P, TB, D]),
                                      start=True, stop=False, skip_group_check=True)
                        pe.wait_ge(sem(f"{name}_hid"), c * nb + s + 1)
                        for t in range(TB):
                            ins = pe.matmul(o[:, t * D:(t + 1) * D], hid[:, s % 4, t * P:(t + 1) * P], w2[:, s, :],
                                            start=False, stop=(k == HB - 1), skip_group_check=True)
                        if k == HB - 1:
                            ins.then_inc(sem(f"{name}_out"), 1)

                pe.wait_ge(sem(f"{name}_split"), 1)
                for e in range(lead):
                    up(e, bass.ds(0, CH))
                with pe.Fori(0, N // CH - 1) as c:
                    chunk(c)
                chunk(N // CH - 1, final=True)

            loaded(pe, "moe0_w_in")
            pe.wait_ge(sem("parts_made"), 1)
            pe.wait_ge(sem("sums_taken"), 1)
            pe.wait_ge(sem("gate_shifted"), 1)
            warm_up(10)
            mlp(parts_0, w2_0, b_parts[:, 0:E0 * D],
                E0, H0 // P, "moe0")

            pe.wait_ge(sem("x_ready"), 1)
            loaded(pe, "lsh_w_in")
            pe.wait_ge(sem("moe0_added"), E0 * (N // CH))
            turn(x5, lambda t: mm(bank[2][:, t * GC:(t + 1) * GC], xT[:, t * P:(t + 1) * P], w_rot[:, :]))\
                .then_inc(sem("rotated"), 1)
            pe.wait_ge(sem("buckets_made"), 1)
            for s in range(S):
                for q in range(TB):
                    t = s * TB + q
                    hb = hot_b[:, t].rearrange("p h i -> p (h i)")
                    mm(bank[2][0:D, s * M:(s + 1) * M], x5[:, t, :], hb, q == 0, q == TB - 1)
            for q in range(TB):
                hb = hot_b[:, :, :, :].rearrange("p (s q) h i -> p q s (h i)", q=TB)[:, q]
                ins = mm(bank[3][:, 0:S * M].rearrange("p (s m) -> p s m", s=S), ones[:, :], hb, q == 0, q == TB - 1)
            ins.then_inc(sem("pooled_psum"), 1)
            pe.wait_ge(sem("pooled_made"), 1)
            mm(bank[3][0:D, 0:S * M], w_kv[:, 0:D], pooled[:, :, 0, :])
            for s in range(S):
                ins = mm(bank[2][:, s * D:(s + 1) * D],
                         pooled[:, s].rearrange("p r m -> p (r m)"), w_kv[:, D:2 * D])
            ins.then_inc(sem("kv_psum"), 1)
            pe.wait_ge(sem("kv_ready"), 1)
            def lsh_q(it, a, cols):
                mm(bank[6 + a][:, 0:P], w_qq[:, :], xT[:, cols]).then_inc(sem("lq_psum"), 1)

            def lsh_scores(it, a, b):
                pe.wait_ge(sem("lq_ready"), it + 1)
                mm(bank[a][:, 0:1], yst[:, a, :], zeros[0:D, 0:1])
                mm(bank[a][:, 0:AH * M], yst[:, a, :],
                   k_bd[:, bass.ds(b, 1)].rearrange("p s h m -> p (s h m)")).then_inc(sem("lsh_scores"), 1)

            def lsh_turn(it, a):
                pe.wait_ge(sem("lsh_exp"), it + 1)
                for j in range(2):
                    ins = pe.transpose(bank[2 + a][:, j * P:(j + 1) * P], score[:, a, j * P:(j + 1) * P], ident[:, :])
                ins.then_inc(sem("lshT_psum"), 1)

            def lsh_out(it, a, b, first=False):
                pe.wait_ge(sem("lshT"), it + 1)
                if not first:
                    pe.wait_ge(sem("lsh_added"), it - 1)
                for j in range(2):
                    vv = v_bd[:, bass.ds(b, 1), j, :].rearrange("p s c -> p (s c)")
                    ins = mm(bank[4 + a][:, 0:D], scoreT[:, a, j * P:(j + 1) * P], vv, j == 0, j == 1)
                ins.then_inc(sem("lsh_att"), 1)

            def lsh_batch(b, start=False, end=False):
                for q in range(TB):
                    a, it = q % 2, TB * b + q
                    more = not (end and q == TB - 1)
                    lsh_q(it + 1, 1 - a, bass.ds((b * B + (q + 1) * P) if more else b * B, P))
                    if not (start and q == 0):
                        lsh_out(it - 1, 1 - a, b if q else b - 1, start and q <= 2)
                    if more:
                        lsh_scores(it + 1, 1 - a, b + (1 if q == TB - 1 else 0))
                    lsh_turn(it, a)

            lsh_q(0, 0, bass.ds(0, P))
            lsh_scores(0, 0, 0)
            lsh_batch(0, start=True)
            with pe.Fori(1, S - 1) as b:
                lsh_batch(b)
            lsh_batch(S - 1, end=True)
            lsh_out(T - 1, 1, S - 1)
            pe.wait_ge(sem("x_ready"), 2)
            turn(x5)
            loaded(pe, "fc_w_in")
            warm_up(10)
            mlp(parts_f, w2_f, b_parts[:, E0 * D:(E0 + 1) * D], 1, HF // P, "fc")
            pe.wait_ge(sem("xn_ready"), 3)
            loaded(pe, "moe1_w_in")
            pe.wait_ge(sem("fc_taken"), N // CH + 1)
            turn(xn, lambda t: mm(bank[2][:, t * E1:(t + 1) * E1], xT[:, t * P:(t + 1) * P], w_gate[:, :]))\
                .then_inc(sem("gate_logits"), 1)
            pe.wait_ge(sem("gate_shifted"), 2)
            warm_up(10)
            mlp(parts_1, w2_1, b_parts[:, (E0 + 1) * D:NB2],
                E1, H1 // P, "moe1")


_INS = ['x', 'L0_tok_token_W', 'L0_tok_pe', 'L0_attn_Wq', 'L0_attn_Wk', 'L0_ffn_W_gat', 'L0_ffn_att_src',
        'L0_ffn_att_dst', 'L0_ffn_b_gat', 'L0_ffn_ln_gamma', 'L0_ffn_ln_beta', 'L0_ffn_W1', 'L0_ffn_b1',
        'L0_ffn_W2', 'L0_ffn_b2', 'L0_ffn_edge_index', 'L1_attn_rotations', 'L1_attn_norm1_g',
        'L1_attn_norm1_b', 'L1_attn_q_w', 'L1_attn_kv_w', 'L1_attn_norm2_g', 'L1_attn_norm2_b',
        'L1_attn_fc1_w', 'L1_attn_fc1_b', 'L1_attn_fc2_w', 'L1_attn_fc2_b', 'L1_ffn_Wg', 'L1_ffn_bg',
        'L1_ffn_W1', 'L1_ffn_b1', 'L1_ffn_W2', 'L1_ffn_b2']


def kernel(**inputs):
    import concourse.bacc as _bacc
    from concourse.bass_utils import run_bass_kernel_spmd as _run

    nc = _bacc.Bacc("TRN2", target_bir_lowering=False, num_devices=1)
    arrays, args = {}, []
    for name in _INS:
        a = np.ascontiguousarray(inputs[name])
        arrays[f"in_{name}"] = a
        args.append(nc.dram_tensor(f"in_{name}", a.shape, mybir.dt.from_np(a.dtype), kind="ExternalInput").ap())
    s, b = inputs['x'].shape
    d = inputs['L0_tok_token_W'].shape[1]
    args.append(nc.dram_tensor("out_h", (s, b, d), F32, kind="ExternalOutput").ap())
    tower_program(nc, *args)
    r = _run(nc, [arrays], core_ids=[0])
    return r.results[0]["out_h"]
```
